# Optimizing a Trainium2 kernel written in Bass

```python
import numpy as np
import jax
import jax.numpy as jnp

def _softmax(x, axis=-1):
    return jax.nn.softmax(x, axis=axis)

def _gelu(x):
    return jax.nn.gelu(x, approximate=True)

def _silu(x):
    return jax.nn.silu(x)

def _sigmoid(x):
    return jax.nn.sigmoid(x)

def _layernorm(x, axis=-1, eps=1e-05):
    m = jnp.mean(x, axis=axis, keepdims=True)
    v = jnp.var(x, axis=axis, keepdims=True)
    return (x - m) / jnp.sqrt(v + eps)

def _scatter_add(tgt, idx, src, axis=0):
    return tgt.at[idx].add(src)

def _segment_sum(src, seg, n):
    return jax.ops.segment_sum(src, seg, n)
kernel_name = 'mk_flamingo_gated_d4_seqx_r8_95551e'

def setup_inputs(seed: int=0):
    np.random.seed(seed)
    _w = jnp.asarray

    def _rec_inputs():
        import jax
        import jax.numpy as jnp
        _rk = jax.random.key(seed)
        x = 7.22e-05 + 1 * jax.random.normal(jax.random.fold_in(_rk, 1), (8, 256, 128), jnp.float32)
        _lenS = 256 - jax.random.randint(jax.random.fold_in(_rk, 7), (8,), 0, max(1, 256 // 4) + 1, jnp.int32)
        _lenS2 = 256 - jax.random.randint(jax.random.fold_in(_rk, 8), (8,), 0, max(1, 256 // 4) + 1, jnp.int32)
        _ctx_1024P = jax.random.normal(jax.random.fold_in(_rk, 11), (8, 16, 128), jnp.float32)
        _ctx_1024c = jax.random.dirichlet(jax.random.fold_in(_rk, 511), 0.3 * jnp.ones((16,), jnp.float32), (8, 256))
        _ctx_1024t = jnp.einsum('bsk,bkd->bsd', _ctx_1024c, _ctx_1024P)
        _ctx_1024t = _ctx_1024t * jax.lax.rsqrt(jnp.mean(jnp.square(_ctx_1024t)) + 1e-12) * 0.953939
        ctx_1024 = 4.13588e-05 + 0.999923 * (_ctx_1024t + 0.3 * jax.random.normal(jax.random.fold_in(_rk, 611), (8, 256, 128), jnp.float32))
        _validS = jnp.arange(256)[None, :] < _lenS[:, None]
        _validS2 = jnp.arange(256)[None, :] < _lenS2[:, None]
        _causal = jnp.tril(jnp.ones((256, 256), dtype=bool))
        mask_Bx1xSxS2_ik1 = jnp.where(jnp.broadcast_to(_validS2[:, None, None, :], (8, 1, 256, 256)), 1, 0).astype(jnp.int32)
        mask_1x1xSxS2_ik0 = jnp.where(jnp.broadcast_to(_validS2[0:1, None, None, :], (1, 1, 256, 256)), 0, 1).astype(jnp.int32)
        _g = jax.random.normal(jax.random.fold_in(_rk, 9001), (2, 4), jnp.float32)
        _g = jnp.sign(_g) * jnp.maximum(jnp.abs(_g), 1.0) + (_g == 0) * 1.0
        g_xattn = _g[0]
        g_ffn = _g[1]
        return (x, ctx_1024, mask_Bx1xSxS2_ik1, mask_1x1xSxS2_ik0, g_xattn, g_ffn)
    x, ctx_1024, mask_Bx1xSxS2_ik1, mask_1x1xSxS2_ik0, g_xattn, g_ffn = _rec_inputs()

    def _L0_xattn_setup():
        import jax, jax.numpy as jnp
        import numpy as np
        BETA = 128
        NUM_HEADS = 16
        NORM = (BETA // NUM_HEADS) ** (-0.5)
        key = jax.random.key(seed)
        ks = jax.random.split(key, 6)
        B, N = (4, 256)
        D_in_q = D_in_k = D_in_v = 128
        D_out_k = D_out_v = 128
        q = jax.random.normal(ks[0], (B, N, D_in_q), dtype=jnp.float32)
        k = jax.random.normal(ks[1], (B, N, D_in_k), dtype=jnp.float32)
        v = jax.random.normal(ks[2], (B, N, D_in_v), dtype=jnp.float32)
        Wq = jax.random.normal(ks[3], (D_out_k, D_in_q), dtype=jnp.float32) * D_in_q ** (-0.5)
        Wk = jax.random.normal(ks[4], (D_out_k, D_in_k), dtype=jnp.float32) * D_in_k ** (-0.5)
        Wv = jax.random.normal(ks[5], (D_out_v, D_in_v), dtype=jnp.float32) * D_in_v ** (-0.5)
        return {'q': q, 'k': k, 'v': v, 'Wq': Wq, 'Wk': Wk, 'Wv': Wv}
    _L0_xattn_all = _L0_xattn_setup()
    _L0_xattn_in = {k: v for k, v in _L0_xattn_all.items() if k in ('Wq', 'Wk', 'Wv')}
    del _L0_xattn_all

    def _L0_ffn_setup():
        import jax, jax.numpy as jnp
        import numpy as np
        B, S, H, F, E, K = (2, 256, 128, 512, 8, 2)

        def _init_w(key, shape, fan_in):
            return jax.random.normal(key, shape, jnp.float32) * fan_in ** (-0.5)

        def _ffn(x, wi, bi, wo, bo):
            return jax.nn.selu(x @ wi + bi) @ wo + bo
        key = jax.random.key(seed)
        ks = jax.random.split(key, 6)
        return {'x': jax.random.normal(ks[0], (B, S, H), jnp.float32), 'gate_wi': _init_w(ks[1], (H, F), H), 'gate_bi': jnp.zeros((F,), jnp.float32), 'gate_wo': _init_w(ks[2], (F, H), F), 'gate_bo': jnp.zeros((H,), jnp.float32), 'exp_wi': _init_w(ks[3], (E, H, F), H), 'exp_bi': jnp.zeros((E, F), jnp.float32), 'exp_wo': _init_w(ks[4], (E, F, H), F), 'exp_bo': jnp.zeros((E, H), jnp.float32)}
    _L0_ffn_all = _L0_ffn_setup()
    _L0_ffn_in = {k: v for k, v in _L0_ffn_all.items() if k in ('gate_wi', 'gate_bi', 'gate_wo', 'gate_bo', 'exp_wi', 'exp_bi', 'exp_wo', 'exp_bo')}
    del _L0_ffn_all

    def _L1_xattn_setup():
        import jax, jax.numpy as jnp
        import numpy as np
        B, S, E, H = (2, 256, 128, 16)
        D = E // H
        key = jax.random.key(seed)
        ks = jax.random.split(key, 14)
        inp = {'query': jax.random.normal(ks[0], (B, S, E), jnp.float32), 'key': jax.random.normal(ks[1], (B, S, E), jnp.float32), 'value': jax.random.normal(ks[2], (B, S, E), jnp.float32), 'adj': jax.random.normal(ks[3], (S, S), jnp.float32), 'mask': jax.random.randint(ks[4], (B, 1, S, S), 0, 2, jnp.int32)}
        sc = 1.0 / np.sqrt(E)
        inp['Wq'] = jax.random.normal(ks[5], (E, E), jnp.float32) * sc
        inp['bq'] = jax.random.normal(ks[6], (E,), jnp.float32) * sc
        inp['Wk'] = jax.random.normal(ks[7], (E, E), jnp.float32) * sc
        inp['bk'] = jax.random.normal(ks[8], (E,), jnp.float32) * sc
        inp['Wv'] = jax.random.normal(ks[9], (E, E), jnp.float32) * sc
        inp['bv'] = jax.random.normal(ks[10], (E,), jnp.float32) * sc
        inp['Wo'] = jax.random.normal(ks[11], (E, E), jnp.float32) * sc
        inp['bo'] = jax.random.normal(ks[12], (E,), jnp.float32) * sc
        return inp
    _L1_xattn_all = _L1_xattn_setup()
    _L1_xattn_in = {k: v for k, v in _L1_xattn_all.items() if k in ('adj', 'Wq', 'bq', 'Wk', 'bk', 'Wv', 'bv', 'Wo', 'bo')}
    del _L1_xattn_all

    def _L1_ffn_setup():
        import jax, jax.numpy as jnp
        import numpy as np
        EPS = 1e-05

        def rmsnorm(x):
            return x * jax.lax.rsqrt(jnp.mean(x * x, axis=-1, keepdims=True) + EPS)

        def act_quant(x):
            scale = 127.0 / jnp.clip(jnp.max(jnp.abs(x), axis=-1, keepdims=True), 1e-05)
            q = jnp.clip(jnp.round(x * scale), -128.0, 127.0) / scale
            return x + jax.lax.stop_gradient(q - x)

        def weight_quant(w):
            scale = 1.0 / jnp.clip(jnp.mean(jnp.abs(w)), 1e-05)
            q = jnp.clip(jnp.round(w * scale), -1.0, 1.0) / scale
            return w + jax.lax.stop_gradient(q - w)

        def bitlinear(x, w, b):
            xq = act_quant(rmsnorm(x))
            wq = weight_quant(w)
            return jnp.einsum('bsd,fd->bsf', xq, wq) + b
        key = jax.random.key(seed)
        k0, k1, k2 = jax.random.split(key, 3)
        B, S, D, F = (2, 1024, 128, 512)
        x = jax.random.normal(k0, (B, S, D), dtype=jnp.float32)
        w1 = jax.random.normal(k1, (F, D), dtype=jnp.float32) * (1.0 / np.sqrt(D))
        b1 = jnp.zeros((F,), dtype=jnp.float32)
        w2 = jax.random.normal(k2, (D, F), dtype=jnp.float32) * (1.0 / np.sqrt(F))
        b2 = jnp.zeros((D,), dtype=jnp.float32)
        return {'x': x, 'w1': w1, 'b1': b1, 'w2': w2, 'b2': b2}
    _L1_ffn_all = _L1_ffn_setup()
    _L1_ffn_in = {k: v for k, v in _L1_ffn_all.items() if k in ('w1', 'b1', 'w2', 'b2')}
    del _L1_ffn_all

    def _L2_xattn_setup():
        import jax, jax.numpy as jnp
        import numpy as np
        B, L, D, H = (2, 256, 128, 16)
        HD = D // H

        def _xavier(key, out_f, in_f):
            std = (2.0 / (in_f + out_f)) ** 0.5
            return jax.random.normal(key, (out_f, in_f), dtype=jnp.float32) * std
        key = jax.random.key(seed)
        k = jax.random.split(key, 8)
        Q = jax.random.normal(k[0], (B, L, D), dtype=jnp.float32)
        K = jax.random.normal(k[1], (B, L, D), dtype=jnp.float32)
        V = jax.random.normal(k[2], (B, L, D), dtype=jnp.float32)
        mask = jnp.tril(jnp.ones((L, L), dtype=jnp.int32))[None, None]
        wq = _xavier(k[3], D, D)
        wk = _xavier(k[4], D, D)
        wv = _xavier(k[5], D, D)
        wo = _xavier(k[6], D, D)
        bo = jnp.zeros((D,), dtype=jnp.float32)
        return {'Q': Q, 'K': K, 'V': V, 'mask': mask, 'wq': wq, 'wk': wk, 'wv': wv, 'wo': wo, 'bo': bo}
    _L2_xattn_all = _L2_xattn_setup()
    _L2_xattn_in = {k: v for k, v in _L2_xattn_all.items() if k in ('wq', 'wk', 'wv', 'wo', 'bo')}
    del _L2_xattn_all

    def _L2_ffn_setup():
        import jax, jax.numpy as jnp
        import numpy as np
        DIM = 128
        HID = 256
        E = 8
        K = 2
        R = 16
        B_, S_ = (2, 128)

        def _lora_in(xf, W, b, A, B):
            base = jnp.einsum('td,ehd->teh', xf, W)
            low = jnp.einsum('ter,ehr->teh', jnp.einsum('td,erd->ter', xf, A), B)
            return base + low + b

        def _lora_out(g, W, b, A, B):
            base = jnp.einsum('teh,edh->ted', g, W)
            low = jnp.einsum('ter,edr->ted', jnp.einsum('teh,erh->ter', g, A), B)
            return base + low + b
        key = jax.random.key(seed)
        ks = jax.random.split(key, 14)
        n = lambda k, shape, scale: jax.random.normal(k, shape, jnp.float32) * scale
        inp = {'x': jax.random.normal(ks[0], (B_, S_, DIM), jnp.float32), 'Wg': n(ks[1], (E, DIM), DIM ** (-0.5)), 'W1': n(ks[2], (E, HID, DIM), DIM ** (-0.5)), 'b1': jnp.zeros((E, HID), jnp.float32), 'A1': n(ks[3], (E, R, DIM), DIM ** (-0.5)), 'B1': n(ks[4], (E, HID, R), 0.01), 'W2': n(ks[5], (E, DIM, HID), HID ** (-0.5)), 'b2': jnp.zeros((E, DIM), jnp.float32), 'A2': n(ks[6], (E, R, HID), HID ** (-0.5)), 'B2': n(ks[7], (E, DIM, R), 0.01), 'W3': n(ks[8], (E, HID, DIM), DIM ** (-0.5)), 'b3': jnp.zeros((E, HID), jnp.float32), 'A3': n(ks[9], (E, R, DIM), DIM ** (-0.5)), 'B3': n(ks[10], (E, HID, R), 0.01)}
        return inp
    _L2_ffn_all = _L2_ffn_setup()
    _L2_ffn_in = {k: v for k, v in _L2_ffn_all.items() if k in ('Wg', 'W1', 'b1', 'A1', 'B1', 'W2', 'b2', 'A2', 'B2', 'W3', 'b3', 'A3', 'B3')}
    del _L2_ffn_all

    def _L3_xattn_setup():
        import jax, jax.numpy as jnp
        import numpy as np
        N_HEADS = 16
        D_MODEL = 128
        D_HEAD = 64
        B, S = (4, 256)
        key = jax.random.key(seed)
        kv, kk, kq, kwi, kwo = jax.random.split(key, 5)
        v = jax.random.normal(kv, (B, S, D_MODEL), dtype=jnp.float32)
        k = jax.random.normal(kk, (B, S, D_MODEL), dtype=jnp.float32)
        q = jax.random.normal(kq, (B, S, D_MODEL), dtype=jnp.float32)
        wi = jax.random.normal(kwi, (D_MODEL, D_HEAD), dtype=jnp.float32) * D_MODEL ** (-0.5)
        Wo = jax.random.normal(kwo, (N_HEADS * D_HEAD, D_MODEL), dtype=jnp.float32) * (N_HEADS * D_HEAD) ** (-0.5)
        bo = jnp.zeros((D_MODEL,), dtype=jnp.float32)
        return {'v': v, 'k': k, 'q': q, 'wi': wi, 'Wo': Wo, 'bo': bo}
    _L3_xattn_all = _L3_xattn_setup()
    _L3_xattn_in = {k: v for k, v in _L3_xattn_all.items() if k in ('wi', 'Wo', 'bo')}
    del _L3_xattn_all

    def _L3_ffn_setup():
        import jax, jax.numpy as jnp
        import numpy as np
        BS, L, D = (4, 256, 128)
        H, E, K = (8, 16, 2)
        HD = D // H
        I = 512 // H
        key = jax.random.key(seed)
        ks = jax.random.split(key, 10)
        s = lambda k, shp, fan: jax.random.normal(k, shp, jnp.float32) / np.sqrt(fan)
        return {'x': jax.random.normal(ks[0], (BS, L, D), jnp.float32), 'Wm': s(ks[1], (D, D), D), 'bm': jnp.zeros((D,), jnp.float32), 'expert_emb': jax.random.normal(ks[2], (HD, E), jnp.float32), 'W1': s(ks[3], (E, HD, I), HD), 'b1': jnp.zeros((E, I), jnp.float32), 'W2': s(ks[4], (E, I, HD), I), 'b2': jnp.zeros((E, HD), jnp.float32), 'Wo': s(ks[5], (D, D), D), 'bo': jnp.zeros((D,), jnp.float32)}
    _L3_ffn_all = _L3_ffn_setup()
    _L3_ffn_in = {k: v for k, v in _L3_ffn_all.items() if k in ('Wm', 'bm', 'expert_emb', 'W1', 'b1', 'W2', 'b2', 'Wo', 'bo')}
    del _L3_ffn_all
    return {'x': x, 'ctx_1024': ctx_1024, 'mask_Bx1xSxS2_ik1': mask_Bx1xSxS2_ik1, 'mask_1x1xSxS2_ik0': mask_1x1xSxS2_ik0, 'g_xattn': g_xattn, 'g_ffn': g_ffn, 'L0_xattn_Wq': _L0_xattn_in['Wq'], 'L0_xattn_Wk': _L0_xattn_in['Wk'], 'L0_xattn_Wv': _L0_xattn_in['Wv'], 'L0_ffn_gate_wi': _L0_ffn_in['gate_wi'], 'L0_ffn_gate_bi': _L0_ffn_in['gate_bi'], 'L0_ffn_gate_wo': _L0_ffn_in['gate_wo'], 'L0_ffn_gate_bo': _L0_ffn_in['gate_bo'], 'L0_ffn_exp_wi': _L0_ffn_in['exp_wi'], 'L0_ffn_exp_bi': _L0_ffn_in['exp_bi'], 'L0_ffn_exp_wo': _L0_ffn_in['exp_wo'], 'L0_ffn_exp_bo': _L0_ffn_in['exp_bo'], 'L1_xattn_adj': _L1_xattn_in['adj'], 'L1_xattn_Wq': _L1_xattn_in['Wq'], 'L1_xattn_bq': _L1_xattn_in['bq'], 'L1_xattn_Wk': _L1_xattn_in['Wk'], 'L1_xattn_bk': _L1_xattn_in['bk'], 'L1_xattn_Wv': _L1_xattn_in['Wv'], 'L1_xattn_bv': _L1_xattn_in['bv'], 'L1_xattn_Wo': _L1_xattn_in['Wo'], 'L1_xattn_bo': _L1_xattn_in['bo'], 'L1_ffn_w1': _L1_ffn_in['w1'], 'L1_ffn_b1': _L1_ffn_in['b1'], 'L1_ffn_w2': _L1_ffn_in['w2'], 'L1_ffn_b2': _L1_ffn_in['b2'], 'L2_xattn_wq': _L2_xattn_in['wq'], 'L2_xattn_wk': _L2_xattn_in['wk'], 'L2_xattn_wv': _L2_xattn_in['wv'], 'L2_xattn_wo': _L2_xattn_in['wo'], 'L2_xattn_bo': _L2_xattn_in['bo'], 'L2_ffn_Wg': _L2_ffn_in['Wg'], 'L2_ffn_W1': _L2_ffn_in['W1'], 'L2_ffn_b1': _L2_ffn_in['b1'], 'L2_ffn_A1': _L2_ffn_in['A1'], 'L2_ffn_B1': _L2_ffn_in['B1'], 'L2_ffn_W2': _L2_ffn_in['W2'], 'L2_ffn_b2': _L2_ffn_in['b2'], 'L2_ffn_A2': _L2_ffn_in['A2'], 'L2_ffn_B2': _L2_ffn_in['B2'], 'L2_ffn_W3': _L2_ffn_in['W3'], 'L2_ffn_b3': _L2_ffn_in['b3'], 'L2_ffn_A3': _L2_ffn_in['A3'], 'L2_ffn_B3': _L2_ffn_in['B3'], 'L3_xattn_wi': _L3_xattn_in['wi'], 'L3_xattn_Wo': _L3_xattn_in['Wo'], 'L3_xattn_bo': _L3_xattn_in['bo'], 'L3_ffn_Wm': _L3_ffn_in['Wm'], 'L3_ffn_bm': _L3_ffn_in['bm'], 'L3_ffn_expert_emb': _L3_ffn_in['expert_emb'], 'L3_ffn_W1': _L3_ffn_in['W1'], 'L3_ffn_b1': _L3_ffn_in['b1'], 'L3_ffn_W2': _L3_ffn_in['W2'], 'L3_ffn_b2': _L3_ffn_in['b2'], 'L3_ffn_Wo': _L3_ffn_in['Wo'], 'L3_ffn_bo': _L3_ffn_in['bo']}

def reference(x, ctx_1024, mask_Bx1xSxS2_ik1, mask_1x1xSxS2_ik0, g_xattn, g_ffn, L0_xattn_Wq, L0_xattn_Wk, L0_xattn_Wv, L0_ffn_gate_wi, L0_ffn_gate_bi, L0_ffn_gate_wo, L0_ffn_gate_bo, L0_ffn_exp_wi, L0_ffn_exp_bi, L0_ffn_exp_wo, L0_ffn_exp_bo, L1_xattn_adj, L1_xattn_Wq, L1_xattn_bq, L1_xattn_Wk, L1_xattn_bk, L1_xattn_Wv, L1_xattn_bv, L1_xattn_Wo, L1_xattn_bo, L1_ffn_w1, L1_ffn_b1, L1_ffn_w2, L1_ffn_b2, L2_xattn_wq, L2_xattn_wk, L2_xattn_wv, L2_xattn_wo, L2_xattn_bo, L2_ffn_Wg, L2_ffn_W1, L2_ffn_b1, L2_ffn_A1, L2_ffn_B1, L2_ffn_W2, L2_ffn_b2, L2_ffn_A2, L2_ffn_B2, L2_ffn_W3, L2_ffn_b3, L2_ffn_A3, L2_ffn_B3, L3_xattn_wi, L3_xattn_Wo, L3_xattn_bo, L3_ffn_Wm, L3_ffn_bm, L3_ffn_expert_emb, L3_ffn_W1, L3_ffn_b1, L3_ffn_W2, L3_ffn_b2, L3_ffn_Wo, L3_ffn_bo):
    import jax
    import jax.numpy as jnp

    def _L0_xattn_ref(q, k, v, Wq, Wk, Wv):
        import jax, jax.numpy as jnp
        import numpy as np
        BETA = 128
        NUM_HEADS = 16
        NORM = (BETA // NUM_HEADS) ** (-0.5)
        qp = jax.nn.relu(jnp.einsum('bnd,od->bno', q, Wq))
        kp = jax.nn.relu(jnp.einsum('bnd,od->bno', k, Wk))
        vp = jax.nn.relu(jnp.einsum('bnd,od->bno', v, Wv))
        B, N, D = qp.shape
        dh = D // NUM_HEADS
        qh = qp.reshape(B, N, NUM_HEADS, dh)
        kh = kp.reshape(B, N, NUM_HEADS, dh)
        vh = vp.reshape(B, N, NUM_HEADS, vp.shape[-1] // NUM_HEADS)
        E = NORM * jnp.einsum('bqhd,bkhd->bhqk', qh, kh)
        A = jax.nn.softmax(E, axis=-1)
        out = jnp.einsum('bhqk,bkhd->bqhd', A, vh)
        return out.reshape(B, N, -1)

    def _L0_ffn_ref(x, gate_wi, gate_bi, gate_wo, gate_bo, exp_wi, exp_bi, exp_wo, exp_bo):
        import jax, jax.numpy as jnp
        import numpy as np
        B, S, H, F, E, K = (2, 256, 128, 512, 8, 2)

        def _init_w(key, shape, fan_in):
            return jax.random.normal(key, shape, jnp.float32) * fan_in ** (-0.5)

        def _ffn(x, wi, bi, wo, bo):
            return jax.nn.selu(x @ wi + bi) @ wo + bo
        Bb, Ss, Hh = x.shape
        xf = x.reshape(-1, Hh)
        gate_logits = _ffn(xf, gate_wi, gate_bi, gate_wo, gate_bo)
        topv, topi = jax.lax.top_k(gate_logits, K)
        topv = topv / jnp.sum(topv, axis=-1, keepdims=True)
        onehot = (topi[..., None] == jnp.arange(E)).astype(x.dtype)
        w = jnp.einsum('nk,nke->ne', topv, onehot)
        h = jax.nn.selu(jnp.einsum('nh,ehf->enf', xf, exp_wi) + exp_bi[:, None, :])
        out_e = jnp.einsum('enf,efh->enh', h, exp_wo) + exp_bo[:, None, :]
        out = jnp.einsum('enh,ne->nh', out_e, w)
        return out.reshape(Bb, Ss, Hh)

    def _L1_xattn_ref(query, key, value, adj, mask, Wq, bq, Wk, bk, Wv, bv, Wo, bo):
        import jax, jax.numpy as jnp
        import numpy as np
        B, S, E, H = (2, 256, 128, 16)
        D = E // H
        b, s, _ = query.shape

        def heads(x, W, bias):
            y = jnp.einsum('bse,ef->bsf', x, W.T) + bias
            return y.reshape(b, s, H, D).transpose(0, 2, 1, 3)
        Q = heads(query, Wq, bq)
        K = heads(key, Wk, bk)
        V = heads(value, Wv, bv)
        scores = jnp.einsum('bhqd,bhkd->bhqk', Q, K) / jnp.sqrt(jnp.float32(D))
        scores = scores + adj[None, None, :, :]
        scores = jnp.where(mask == 0, jnp.float32(-jnp.inf), scores)
        weights = jax.nn.softmax(scores, axis=-1)
        out = jnp.einsum('bhqk,bhkd->bhqd', weights, V)
        out = out.transpose(0, 2, 1, 3).reshape(b, s, E)
        return jnp.einsum('bse,ef->bsf', out, Wo.T) + bo

    def _L1_ffn_ref(x, w1, b1, w2, b2):
        import jax, jax.numpy as jnp
        import numpy as np
        EPS = 1e-05

        def rmsnorm(x):
            return x * jax.lax.rsqrt(jnp.mean(x * x, axis=-1, keepdims=True) + EPS)

        def act_quant(x):
            scale = 127.0 / jnp.clip(jnp.max(jnp.abs(x), axis=-1, keepdims=True), 1e-05)
            q = jnp.clip(jnp.round(x * scale), -128.0, 127.0) / scale
            return x + jax.lax.stop_gradient(q - x)

        def weight_quant(w):
            scale = 1.0 / jnp.clip(jnp.mean(jnp.abs(w)), 1e-05)
            q = jnp.clip(jnp.round(w * scale), -1.0, 1.0) / scale
            return w + jax.lax.stop_gradient(q - w)

        def bitlinear(x, w, b):
            xq = act_quant(rmsnorm(x))
            wq = weight_quant(w)
            return jnp.einsum('bsd,fd->bsf', xq, wq) + b
        h = bitlinear(x, w1, b1)
        h = jax.nn.gelu(h, approximate=False)
        return bitlinear(h, w2, b2)

    def _L2_xattn_ref(Q, K, V, mask, wq, wk, wv, wo, bo):
        import jax, jax.numpy as jnp
        import numpy as np
        B, L, D, H = (2, 256, 128, 16)
        HD = D // H

        def _xavier(key, out_f, in_f):
            std = (2.0 / (in_f + out_f)) ** 0.5
            return jax.random.normal(key, (out_f, in_f), dtype=jnp.float32) * std
        N, Lq, Dm = Q.shape
        q = (Q @ wq.T).reshape(N, Lq, H, HD).transpose(0, 2, 1, 3)
        kk = (K @ wk.T).reshape(N, Lq, H, HD).transpose(0, 2, 1, 3)
        v = (V @ wv.T).reshape(N, Lq, H, HD).transpose(0, 2, 1, 3)
        score = jnp.einsum('bhqd,bhkd->bhqk', q, kk) / jnp.sqrt(jnp.float32(HD))
        score = jnp.where(mask == 0, -jnp.inf, score)
        weights = jax.nn.softmax(score, axis=-1)
        attn = jnp.einsum('bhqk,bhkd->bhqd', weights, v)
        out = attn.transpose(0, 2, 1, 3).reshape(N, Lq, Dm)
        return out @ wo.T + bo

    def _L2_ffn_ref(x, Wg, W1, b1, A1, B1, W2, b2, A2, B2, W3, b3, A3, B3):
        import jax, jax.numpy as jnp
        import numpy as np
        DIM = 128
        HID = 256
        E = 8
        K = 2
        R = 16
        B_, S_ = (2, 128)

        def _lora_in(xf, W, b, A, B):
            base = jnp.einsum('td,ehd->teh', xf, W)
            low = jnp.einsum('ter,ehr->teh', jnp.einsum('td,erd->ter', xf, A), B)
            return base + low + b

        def _lora_out(g, W, b, A, B):
            base = jnp.einsum('teh,edh->ted', g, W)
            low = jnp.einsum('ter,edr->ted', jnp.einsum('teh,erh->ter', g, A), B)
            return base + low + b
        orig_shape = x.shape
        xf = x.reshape(-1, x.shape[-1])
        scores = jax.nn.softmax(xf @ Wg.T, axis=-1)
        expert_weights, expert_indices = jax.lax.top_k(scores, K)
        expert_weights = expert_weights / expert_weights.sum(-1, keepdims=True)
        gates = (jax.nn.one_hot(expert_indices, E, dtype=xf.dtype) * expert_weights[..., None]).sum(axis=1)
        h1 = _lora_in(xf, W1, b1, A1, B1)
        h3 = _lora_in(xf, W3, b3, A3, B3)
        g = jax.nn.silu(h1) * h3
        y_e = _lora_out(g, W2, b2, A2, B2)
        y = jnp.einsum('te,ted->td', gates, y_e)
        return y.reshape(orig_shape)

    def _L3_xattn_ref(v, k, q, wi, Wo, bo):
        import jax, jax.numpy as jnp
        import numpy as np
        N_HEADS = 16
        D_MODEL = 128
        D_HEAD = 64
        B, S = (4, 256)
        qp = q @ wi
        kp = k @ wi
        vp = v @ wi
        scores = jnp.einsum('bsd,btd->bst', qp, kp) / jnp.sqrt(jnp.asarray(D_HEAD, qp.dtype))
        attn = jax.nn.softmax(scores, axis=-1)
        head = qp + jnp.einsum('bst,btd->bsd', attn, vp)
        concat = jnp.tile(head, (1, 1, N_HEADS))
        return concat @ Wo + bo

    def _L3_ffn_ref(x, Wm, bm, expert_emb, W1, b1, W2, b2, Wo, bo):
        import jax, jax.numpy as jnp
        import numpy as np
        BS, L, D = (4, 256, 128)
        H, E, K = (8, 16, 2)
        HD = D // H
        I = 512 // H
        bs, L_, d = x.shape
        h = x @ Wm + bm
        t = h.reshape(bs * L_ * H, HD)
        logits = t @ expert_emb
        w = jax.nn.softmax(logits, axis=-1)
        topw, topi = jax.lax.top_k(w, K)
        hmid = jax.nn.gelu(jnp.einsum('td,edi->tei', t, W1) + b1, approximate=False)
        eo = jnp.einsum('tei,eio->teo', hmid, W2) + b2
        sel = jnp.take_along_axis(eo, topi[:, :, None], axis=1)
        comb = (sel * topw[:, :, None]).sum(axis=1)
        out = comb.reshape(bs, L_, d)
        return out @ Wo + bo
    x = x + jnp.tanh(g_xattn[0]) * _L0_xattn_ref(_layernorm(x, axis=-1), ctx_1024, ctx_1024, L0_xattn_Wq, L0_xattn_Wk, L0_xattn_Wv)
    x = x + jnp.tanh(g_ffn[0]) * _L0_ffn_ref(_layernorm(x, axis=-1), L0_ffn_gate_wi, L0_ffn_gate_bi, L0_ffn_gate_wo, L0_ffn_gate_bo, L0_ffn_exp_wi, L0_ffn_exp_bi, L0_ffn_exp_wo, L0_ffn_exp_bo)
    x = x + jnp.tanh(g_xattn[1]) * _L1_xattn_ref(_layernorm(x, axis=-1), ctx_1024, ctx_1024, L1_xattn_adj, mask_Bx1xSxS2_ik1, L1_xattn_Wq, L1_xattn_bq, L1_xattn_Wk, L1_xattn_bk, L1_xattn_Wv, L1_xattn_bv, L1_xattn_Wo, L1_xattn_bo)
    x = x + jnp.tanh(g_ffn[1]) * _L1_ffn_ref(_layernorm(x, axis=-1), L1_ffn_w1, L1_ffn_b1, L1_ffn_w2, L1_ffn_b2)
    x = x + jnp.tanh(g_xattn[2]) * _L2_xattn_ref(_layernorm(x, axis=-1), ctx_1024, ctx_1024, mask_1x1xSxS2_ik0, L2_xattn_wq, L2_xattn_wk, L2_xattn_wv, L2_xattn_wo, L2_xattn_bo)
    x = x + jnp.tanh(g_ffn[2]) * _L2_ffn_ref(_layernorm(x, axis=-1), L2_ffn_Wg, L2_ffn_W1, L2_ffn_b1, L2_ffn_A1, L2_ffn_B1, L2_ffn_W2, L2_ffn_b2, L2_ffn_A2, L2_ffn_B2, L2_ffn_W3, L2_ffn_b3, L2_ffn_A3, L2_ffn_B3)
    x = x + jnp.tanh(g_xattn[3]) * _L3_xattn_ref(ctx_1024, ctx_1024, _layernorm(x, axis=-1), L3_xattn_wi, L3_xattn_Wo, L3_xattn_bo)
    x = x + jnp.tanh(g_ffn[3]) * _L3_ffn_ref(_layernorm(x, axis=-1), L3_ffn_Wm, L3_ffn_bm, L3_ffn_expert_emb, L3_ffn_W1, L3_ffn_b1, L3_ffn_W2, L3_ffn_b2, L3_ffn_Wo, L3_ffn_bo)
    return x

_drawn_inputs = setup_inputs


def setup_inputs(seed=0):
    import zlib

    import numpy as np

    out = dict(_drawn_inputs(seed))
    spreads = {'L0_ffn_gate_bi': (0.0, 0.1),
     'L0_ffn_gate_bo': (0.0, 0.1),
     'L0_ffn_exp_bi': (0.0, 0.385),
     'L0_ffn_exp_bo': (0.0, 0.374),
     'L1_ffn_b1': (0.0, 0.1),
     'L1_ffn_b2': (0.0, 0.1),
     'L2_xattn_bo': (0.0, 0.1),
     'L2_ffn_b1': (0.0, 0.278),
     'L2_ffn_b2': (0.0, 0.1),
     'L2_ffn_b3': (0.0, 0.283),
     'L3_xattn_bo': (0.0, 0.1),
     'L3_ffn_bm': (0.0, 0.1),
     'L3_ffn_b1': (0.0, 0.348),
     'L3_ffn_b2': (0.0, 0.1),
     'L3_ffn_bo': (0.0, 0.1)}
    factors = {'L1_xattn_bk': 8.0,
     'L2_ffn_A1': 4.592,
     'L2_ffn_B1': 4.553,
     'L2_ffn_A2': 4.715,
     'L2_ffn_B2': 4.655,
     'L2_ffn_A3': 4.688,
     'L2_ffn_B3': 4.693}
    for name, (base, spread) in spreads.items():
        noise = np.random.default_rng([zlib.crc32(name.encode()), seed]).standard_normal(out[name].shape)
        drawn = base * np.exp(spread * noise) if base else spread * noise
        out[name] = jnp.asarray(drawn.astype(out[name].dtype))
    for name, factor in factors.items():
        out[name] = (out[name] * factor).astype(out[name].dtype)
    return out
```

```python
import math

import concourse.bass as bass
from concourse import mybir
from contextlib import ExitStack

P = 128
BATCH, S, D = 8, 256, 128
NB = 2
TURNS = BATCH // NB
NT = NB * S // P
T = NT * P
H, DH = 16, 8
G = 4
NJ = H // G
QD = 32
MROW = DH
SC = DH ** -0.5
E0, F0 = 8, 512
NC0 = F0 // P
E2, H2, R2 = 8, 256, 16
NH2 = H2 // P
DK3 = 64
H3, E3, HD3, I3 = 8, 16, 16, 64
NEP = E3 * I3 // P
LAMBDA = 1.0507009873554804934193349852946
ALPHA = 1.6732632423543772848170429916717
EPS = 1e-5
MAGIC = 12582912.0
NEG = -1.0e30
CAP = 1.0e25


class Chain:

    def __init__(self, eng, sem):
        self.eng, self.sem, self.n = eng, sem, 0

    def __call__(self, ins):
        self.n += 1
        ins.then_inc(self.sem, 1)
        self.eng.wait_ge(self.sem, self.n)


def flamingo(nc, A, out, turns=TURNS):
    f32, bf16, i32, u32 = mybir.dt.float32, mybir.dt.bfloat16, mybir.dt.int32, mybir.dt.uint32
    ALU, ACT, AX = mybir.AluOpType, mybir.ActivationFunctionType, mybir.AxisListType
    ctx = ExitStack()
    with ctx:
        def sb(name, shape, dt=f32):
            return ctx.enter_context(nc.sbuf_tensor(name, shape, dt))

        W = {}
        for name, (shape, dt) in WEIGHTS.items():
            if name not in SETUP_ONLY:
                W[name] = sb("w_" + name, shape, {"f": f32, "i": i32}[dt])
        ident_b = sb("ident_b", [P, P], bf16)
        tg = sb("tg", [P, 8])
        tgl = sb("tgl", [P, 1])
        l0_exp_bias = sb("l0_exp_bias", [P, (E0 + 1) * NC0])
        l0_gate_bo = sb("l0_gate_bo", [P, P])
        l0_exp_bo = sb("l0_exp_bo", [E0, P])
        q_bias = sb("q_bias", [P, NJ])
        k_bias = sb("k_bias", [P, 3, NJ])
        wsum = sb("wsum", [P, 2])
        wmean = sb("wmean", [P, 2])
        wscale = sb("wscale", [P, 2])
        w1q = sb("w1q", [P, F0], bf16)
        w2q = sb("w2q", [P, F0], bf16)
        wo3 = sb("wo3", [DK3, P])
        l2_bias_q = sb("l2_bias_q", [P, 2, S], bf16)
        l2_bias_k = sb("l2_bias_k", [P, 2, S], bf16)

        x = sb("x", [P, NT, D])
        ctxs = sb("ctxs", [P, NT, D])
        xn = sb("xn", [P, NT, D])
        xT = sb("xT", [P, T])
        cT = sb("cT", [P, T])
        stats = sb("stats", [P, NT, 6])
        mv = sb("mv", [P, NT, 2])
        vare = sb("vare", [P, NT])
        rstd = sb("rstd", [P, NT])
        mhalf = sb("mhalf", [P, NT])
        m1 = sb("m1", [P, 2, NT, S], i32)
        bfull = sb("bfull", [P, NT, S])
        b1q = sb("b1q", [P, 2, NT, S], bf16)
        b1k = sb("b1k", [P, 3, NT, S], bf16)
        qP = sb("qP", [P, NJ, T])
        kP = sb("kP", [P, NJ, T])
        qA = qP
        vE = sb("vE", [P, NT, H, DH + 1])
        nmp = sb("nmp", [P, NT, NJ, P])
        rc = sb("rc", [P, NT, H])
        att = sb("att", [P, NT, D])
        attT = sb("attT", [P, T])
        y = sb("y", [P, NT, D])
        ex = sb("ex", [P, 4, T])
        rl = sb("rl", [P, 4, T])
        hT = sb("hT", [P, 2, NC0, T])
        pT = hT[:].rearrange("p a c k -> p (a c k)")[:, 0:3 * 4 * S].rearrange("p (n k) -> p n k", n=3)
        acc = sb("acc", [P, NT, D])
        mx8 = sb("mx8", [P, 32, 8])
        ix8 = sb("ix8", [P, 32, 8], u32)
        ixf = sb("ixf", [P, 32, 2])
        tw = sb("tw", [P, NT, 2])
        tws = sb("tws", [P, NT])
        oh = sb("oh", [P, 2, NT, 8])
        gw = sb("gw", [P, NT, 8])
        gT = attT[0:8, :]
        lg = y[:].rearrange("p t d -> p (t d)")
        cols = sb("cols", [P, 8, NT])
        hh = rl
        kb = kP[:].rearrange("p j k -> p (j k)").bitcast(bf16)
        qh = kb[:, 0:NT * F0].rearrange("p (t f) -> p t f", t=NT)
        qhT = kb[:, NT * F0:].rearrange("p (t c k) -> p t c k", t=NT, c=NC0)
        oh16 = rl[:, 1:3, :].rearrange("p a (r e) -> p a r e", e=E3)
        gates = sb("gates", [P, 32, E3])
        gb = gates[:].rearrange("p r e -> p (r e)").bitcast(bf16)
        qx = gb[:, 0:T].rearrange("p (t d) -> p t d", t=NT)
        qxT = gb[:, T:2 * T]
        gsum = sb("gsum", [P, 32])
        GT = rl[:, 3, :]
        gated = ex[:].rearrange("p a (t k) -> p (a t k)", t=2).rearrange("p (a t k) -> p a t k", a=2, t=NT)
        hP = qP
        homes = {"hT": hT[:].rearrange("p a c k -> p (a c k)"), "qP": qP[:].rearrange("p j k -> p (j k)"),
                 "kP": kP[:].rearrange("p j k -> p (j k)"), "rl": rl[:].rearrange("p a k -> p (a k)"),
                 "m1": m1[:].rearrange("p a t k -> p (a t k)").bitcast(f32), "ex": ex[:].rearrange("p a k -> p (a k)")}
        for name, (home, at) in SETUP_ONLY.items():
            (rows_, *free), dt = WEIGHTS[name]
            flat = homes[home][0:rows_, at:at + math.prod(free)]
            if dt == "i":
                flat = flat.bitcast(i32)
            W[name] = flat.rearrange("p (a b) -> p a b", a=free[0]) if len(free) > 1 else flat

        ps = ctx.enter_context(nc.psum_tensor("ps", [P, 8, 512], f32))

        def bank(n, width=512):
            return ps[:, n, 0:width]

        sems = {}
        nums = []

        def sem(name):
            if name not in sems:
                sems[name] = ctx.enter_context(nc.semaphore(name))
            return sems[name]

        turn_end = sem("turn_end")
        GO = {e: sem("go_" + e) for e in ("pe", "act", "dve", "pool")}
        kept = set(sems)
        stored = sem("out_stored")
        block = ctx.enter_context(nc.Block())

        def end_turn(eng, who):
            eng.drain().then_inc(turn_end, 1)
            eng.wait_ge(GO[who], 1)
            eng.sem_clear(GO[who])

        FFN_LN = {0: 1, 1: 3, 2: 5, 3: 7}

        @block.gpsimd
        def _(pool):
            step = Chain(pool, sem("pool_step"))
            pool.memset(mhalf[:], -0.5)
            pool.memset(vE[:], 1.0)
            pool.memset(nmp[:], 0.0)
            pool.wait_ge(sem("weights_loaded"), 16 * N_WEIGHTS)
            for dst, src in ((l2_bias_q, W["mask0_q"]), (l2_bias_k, W["mask0_k"])):
                pool.tensor_scalar(dst[:], src, 0.0, NEG, ALU.is_equal, ALU.mult)
            end_turn(pool, "pool")
            with pool.Fori(0, turns):
                step = Chain(pool, sem("pool_step"))
                ln = iter(range(8))

                def root(n_ready, n):
                    pool.wait_ge(sem("var_ready"), n_ready)
                    step(pool.tensor_scalar(vare[:], vare[:], EPS, None, ALU.add))
                    pool.tensor_tensor(rstd[:], vare[:], mhalf[:], ALU.pow).then_inc(sem("rstd_ready"), 1)

                def biases():
                    pool.wait_ge(sem("masks_loaded"), 32)
                    for side, parts, dst, adj in ((0, 2, b1q, W["adj_q"]), (1, 3, b1k, W["adj_k"])):
                        step(pool.tensor_scalar(bfull[:], m1[:, side], 0.0, NEG, ALU.is_equal, ALU.mult))
                        for b in range(NB):
                            ins = pool.tensor_tensor(bfull[:, 2 * b:2 * b + 2, :], bfull[:, 2 * b:2 * b + 2, :],
                                                     adj[:], ALU.add)
                            step(ins)
                        for part in range(parts):
                            last = pool.tensor_copy(dst[:, part], bfull[:])
                            step(last)
                            if part + 1 < parts:
                                step(pool.tensor_tensor(bfull[:], bfull[:], dst[:, part], ALU.subtract))
                    pool.engine_nop().then_inc(sem("l1_bias_ready"), 1)

                root(1, 0)
                root(2, 1)
                biases()
                for n in range(3, 11):
                    root(n, n)
                end_turn(pool, "pool")

        @block.tensor
        def _(pe):
            pe.wait_ge(sem("weights_loaded"), 16 * N_WEIGHTS)
            for m, (a, b) in enumerate((("l2_a1", "l2_b1"), ("l2_a3", "l2_b3"))):
                for e in range(E2):
                    last = pe.matmul(ps[:, 4 * m + e // 2, (e % 2) * H2:(e % 2 + 1) * H2],
                                     W[a][:, e, :], W[b][:, e, :], start=True, stop=True)
                last.then_inc(sem("lora"), 1)
            pe.wait_ge(sem("merged"), 1)
            for e in range(E2):
                for hc in range(NH2):
                    i = NH2 * e + hc
                    last = pe.matmul(ps[:, i // 4, (i % 4) * P:(i % 4 + 1) * P],
                                     W["l2_a2"][:, e, hc * P:(hc + 1) * P], W["l2_b2"][:, e, :],
                                     start=True, stop=True)
            last.then_inc(sem("lora"), 1)
            pe.wait_ge(sem("merged"), 2)
            for fc in range(NC0):
                pe.matmul(bank(4, P), W["ones"][:], W["l0_wo"][:, 0, fc, :], start=fc == 0, stop=fc == NC0 - 1)
            for e in range(E0):
                for fc in range(NC0):
                    last = pe.matmul(ps[0:E0, 5, 0:P], W["pick"][:, e, :], W["l0_wo"][:, e + 1, fc, :],
                                     start=e + fc == 0, stop=e == E0 - 1 and fc == NC0 - 1)
            last.then_inc(sem("colsum"), 1)
            pe.wait_ge(sem("wsum_ready"), 1)
            pe.matmul(bank(6, 2), W["ones"][:], wsum[:], start=True, stop=True).then_inc(sem("wabs"), 1)
            end_turn(pe, "pe")

            with pe.Fori(0, turns):
                pe.wait_ge(sem("ctx_loaded"), 16)
                for t in range(NT):
                    last = pe.transpose(bank(3)[:, t * P:(t + 1) * P], ctxs[:, t, :], W["ident"][:])
                last.then_inc(sem("cT_ps"), 1)

                def norm_T(n):
                    pe.wait_ge(sem("xn_ready"), n + 1)
                    for t in range(NT):
                        last = pe.transpose(bank(0)[:, t * P:(t + 1) * P], xn[:, t, :], W["ident"][:])
                    last.then_inc(sem("xT_ps"), 1)

                def attention(a):
                    L = f"l{a}_"
                    if a:
                        pe.wait_ge(sem("x_done"), 2 * a)
                    pe.wait_ge(sem("cT_ready"), 1)
                    for j in range(NJ):
                        pe.matmul(bank(4 + j), W[L + "wk"][:, j, :], cT[:], start=True, stop=True)\
                          .then_inc(sem(L + "k_ps"), 1)
                    for t in range(NT):
                        last = pe.matmul(bank(1)[:, t * P:(t + 1) * P], cT[:, t * P:(t + 1) * P], W[L + "wv"][:],
                                         start=True, stop=True)
                    last.then_inc(sem(L + "v_ps"), 1)
                    norm_T(LN_OF_ATT[a])
                    pe.wait_ge(sem("xT_ready"), n_T(LN_OF_ATT[a]))
                    for j in range(NJ):
                        if j == NJ - 1:
                            pe.wait_ge(sem(L + "v_ready"), 1)
                        pe.matmul(bank(Q_BANK[j]), W[L + "wq"][:, j, :], xT[:], start=True, stop=True)\
                          .then_inc(sem(L + "q_ps"), 1)
                    pe.wait_ge(sem(L + "q_act"), 2)
                    pe.wait_ge(sem(L + "q_dve"), 2)
                    pe.wait_ge(sem(L + "k_ready"), NJ)
                    if a == 1:
                        pe.wait_ge(sem("l1_bias_ready"), 1)
                    for u in range(NJ * NB):
                        j, b = divmod(u, NB)
                        if u >= 2:
                            pe.wait_ge(sem(L + "max_ready"), u - 1)
                        s = 4 * (u % 2)
                        bias = {0: [], 1: [b1q[:, 0, 2 * b:2 * b + 2, :], b1q[:, 1, 2 * b:2 * b + 2, :]],
                                2: [l2_bias_q[:]]}[a]
                        for g in range(G):
                            for n, part in enumerate(bias):
                                pe.matmul(bank(s + g), ident_b[:], part.rearrange("p t k -> p (t k)"), start=n == 0,
                                          stop=False, skip_group_check=True)
                        for qt in range(2):
                            for g in range(G):
                                at = b * S + qt * P
                                last = pe.matmul(bank(s + g)[:, qt * S:(qt + 1) * S],
                                                 qP[QD * g:QD * g + QD, j, at:at + P],
                                                 kP[QD * g:QD * g + QD, j, b * S:(b + 1) * S],
                                                 start=not bias, stop=True, skip_group_check=bool(bias))
                        last.then_inc(sem(L + "s1"), 1)
                    pe.wait_ge(sem(L + "max_ready"), NJ * NB)
                    for j in range(NJ):
                        for t in range(NT):
                            last = pe.matmul(bank(j)[:, t * P:(t + 1) * P], nmp[:, t, j, :], W["ident"][:],
                                             start=True, stop=True)
                        last.then_inc(sem(L + "max_T"), 1)
                    def values(v):
                        j, b, half = v // (2 * NB), v // 2 % NB, v % 2
                        pe.wait_ge(sem(L + "p_ready"), v + 1)
                        if v == 0:
                            pe.wait_ge(sem(L + "v_ready"), 1)
                        for hh_ in range(2):
                            h = G * j + 2 * half + hh_
                            for qt in range(2):
                                col = (qt * H + h) * (DH + 1)
                                for kt in range(2):
                                    at = hh_ * 2 * S + kt * S + qt * P
                                    last = pe.matmul(ps[:, 6 + b, col:col + DH + 1], pT[:, v % 3, at:at + P],
                                                     vE[:, 2 * b + kt, h, :], start=kt == 0, stop=kt == 1)
                        last.then_inc(sem(L + "pv"), 1)

                    for v in range(4 * NJ):
                        j, b, half = v // (2 * NB), v // 2 % NB, v % 2
                        pe.wait_ge(sem(L + "q_aug"), NJ if v else 2)
                        if v >= 3:
                            pe.wait_ge(sem(L + "p_ready"), v - 2)
                        s = 2 * (v % 3)
                        bias = {0: [], 1: [b1k[:, n, 2 * b:2 * b + 2, :] for n in range(3)],
                                2: [l2_bias_k[:]]}[a]
                        for hh_ in range(2):
                            for n, part in enumerate(bias):
                                pe.matmul(bank(s + hh_), ident_b[:], part.rearrange("p t k -> p (t k)"), start=n == 0,
                                          stop=False, skip_group_check=True)
                        for kt in range(2):
                            for hh_ in range(2):
                                g = 2 * half + hh_
                                at = b * S + kt * P
                                last = pe.matmul(bank(s + hh_)[:, kt * S:(kt + 1) * S],
                                                 kP[QD * g:QD * g + QD, j, at:at + P],
                                                 qA[QD * g:QD * g + QD, j, b * S:(b + 1) * S],
                                                 start=not bias, stop=True, skip_group_check=bool(bias))
                        last.then_inc(sem(L + "s2"), 1)
                        if v >= 1:
                            values(v - 1)
                    values(4 * NJ - 1)
                    if a:
                        pe.wait_ge(sem(L + "att_ready"), 1)
                        for t in range(NT):
                            last = pe.transpose(bank(0)[:, t * P:(t + 1) * P], att[:, t, :], W["ident"][:])
                        last.then_inc(sem(L + "attT_ps"), 1)
                        pe.wait_ge(sem(L + "attT"), 1)
                        for t in range(NT):
                            last = pe.matmul(bank(1)[:, t * P:(t + 1) * P], attT[:, t * P:(t + 1) * P],
                                             W[L + "wo"][:], start=True, stop=True)
                        last.then_inc(sem(L + "o_ps"), 1)

                attention(0)

                norm_T(1)
                pe.wait_ge(sem("xT_ready"), n_T(1))
                pe.wait_ge(sem("x_done"), 1)

                def f0_out(e):
                    pe.wait_ge(sem("f0_h"), NC0 * (e + 1))
                    if e >= 2:
                        pe.wait_ge(sem("f0_out_read"), e - 1)
                    for t in range(NT):
                        for fc in range(NC0):
                            last = pe.matmul(bank(4 + e % 2)[:, t * P:(t + 1) * P],
                                             hT[:, e % 2, fc, t * P:(t + 1) * P], W["l0_wo"][:, e, fc, :],
                                             start=fc == 0, stop=fc == NC0 - 1)
                    last.then_inc(sem("f0_out"), 1)

                for e in range(E0 + 1):
                    for fc in range(NC0):
                        n = NC0 * e + fc
                        if n >= 4:
                            pe.wait_ge(sem("f0_act"), n - 3)
                        pe.matmul(bank(n % 4), W["l0_wi"][:, e, fc * P:(fc + 1) * P], xT[:], start=True, stop=True)\
                          .then_inc(sem("f0_in"), 1)
                    if e >= 1:
                        f0_out(e - 1)
                f0_out(E0)
                pe.wait_ge(sem("f0_gate"), 1)
                for t in range(NT):
                    last = pe.transpose(ps[0:8, 7, t * P:(t + 1) * P], gw[:, t, :], W["ident"][:])
                last.then_inc(sem("f0_gT_ps"), 1)
                pe.wait_ge(sem("f0_gT"), 1)
                for t in range(NT):
                    last = pe.matmul(bank(6)[:, t * P:(t + 1) * P], gT[:, t * P:(t + 1) * P], l0_exp_bo[:],
                                     start=True, stop=True)
                last.then_inc(sem("f0_b"), 1)

                attention(1)

                pe.wait_ge(sem("x_done"), 3)
                pe.wait_ge(sem("f1_qx"), 1)
                xb = bank(0).bitcast(bf16)
                for t in range(NT):
                    last = pe.transpose(xb[:, t * P:(t + 1) * P], qx[:, t, :], ident_b[:])
                last.then_inc(sem("f1_qxT_ps"), 1)
                pe.wait_ge(sem("f1_qxT"), 1)
                for t in range(NT):
                    pe.matmul(bank(1 + t), qxT[:, t * P:(t + 1) * P], w1q[:], start=True, stop=True)\
                      .then_inc(sem("f1_h_ps"), 1)
                pe.wait_ge(sem("f1_qh"), 1)
                for t in range(NT):
                    hb = bank(4 + t).bitcast(bf16)
                    for fc in range(NC0):
                        last = pe.transpose(hb[:, fc * P:(fc + 1) * P], qh[:, t, fc * P:(fc + 1) * P], ident_b[:])
                    last.then_inc(sem("f1_qhT_ps"), 1)
                for t in range(NT):
                    pe.wait_ge(sem("f1_qhT"), t + 1)
                    for fc in range(NC0):
                        last = pe.matmul(bank(0)[:, t * P:(t + 1) * P], qhT[:, t, fc, :],
                                         w2q[:, fc * P:(fc + 1) * P], start=fc == 0, stop=fc == NC0 - 1)
                last.then_inc(sem("f1_o_ps"), 1)

                attention(2)

                norm_T(5)
                pe.wait_ge(sem("xT_ready"), n_T(5))
                pe.wait_ge(sem("x_done"), 5)
                for t in range(NT):
                    last = pe.matmul(bank(7)[:, t * 8:(t + 1) * 8], xT[:, t * P:(t + 1) * P], W["l2_wg"][:],
                                     start=True, stop=True)
                last.then_inc(sem("f2_lg"), 1)

                def f2_out(e):
                    pe.wait_ge(sem("f2_g"), NH2 * (e + 1))
                    if e >= 2:
                        pe.wait_ge(sem("f2_out_read"), e - 1)
                    for t in range(NT):
                        for hc in range(NH2):
                            last = pe.matmul(bank(4 + e % 2)[:, t * P:(t + 1) * P],
                                             hT[:, e % 2, hc, t * P:(t + 1) * P], W["l2_w2"][:, e, hc, :],
                                             start=hc == 0, stop=hc == NH2 - 1)
                    last.then_inc(sem("f2_out"), 1)

                for e in range(E2):
                    for hc in range(NH2):
                        n = NH2 * e + hc
                        if n >= 2:
                            pe.wait_ge(sem("f2_g"), n - 1)
                        s = 2 * (n % 2)
                        pe.matmul(bank(s), W["l2_w1"][:, e, hc * P:(hc + 1) * P], xT[:], start=True, stop=True)\
                          .then_inc(sem("f2_h1"), 1)
                        pe.matmul(bank(s + 1), W["l2_w3"][:, e, hc * P:(hc + 1) * P], xT[:], start=True, stop=True)\
                          .then_inc(sem("f2_h3"), 1)
                    if e >= 1:
                        f2_out(e - 1)
                f2_out(E2 - 1)
                pe.wait_ge(sem("f2_gate"), 1)
                for t in range(NT):
                    last = pe.transpose(ps[0:8, 7, t * P:(t + 1) * P], gw[:, t, :], W["ident"][:])
                last.then_inc(sem("f2_gT_ps"), 1)
                pe.wait_ge(sem("f2_gT"), 1)
                for t in range(NT):
                    last = pe.matmul(bank(6)[:, t * P:(t + 1) * P], gT[:, t * P:(t + 1) * P], W["l2_bias2"][:], start=True, stop=True)
                last.then_inc(sem("f2_b"), 1)

                pe.wait_ge(sem("x_done"), 6)
                pe.matmul(ps[0:DK3, 1, :], W["l3_wi"][:], cT[:], start=True, stop=True).then_inc(sem("l3_k_ps"), 1)
                for t in range(NT):
                    last = pe.matmul(bank(2)[:, t * DK3:(t + 1) * DK3], cT[:, t * P:(t + 1) * P], W["l3_wi"][:],
                                     start=True, stop=True)
                last.then_inc(sem("l3_v_ps"), 1)
                norm_T(6)
                pe.wait_ge(sem("xT_ready"), n_T(6))
                pe.matmul(ps[0:DK3, 3, :], W["l3_wi"][:], xT[:], start=True, stop=True).then_inc(sem("l3_q_ps"), 1)
                pe.wait_ge(sem("l3_k"), 1)
                pe.wait_ge(sem("l3_q"), 1)
                for t in range(NT):
                    b = t // 2
                    last = pe.matmul(bank(4 + b)[:, (t % 2) * S:(t % 2 + 1) * S], attT[0:DK3, t * P:(t + 1) * P],
                                     GT[0:DK3, b * S:(b + 1) * S], start=True, stop=True)
                last.then_inc(sem("l3_s"), 1)
                pe.wait_ge(sem("l3_p"), 1)
                for kt in range(2):
                    for t in range(NT):
                        last = pe.transpose(bank(6 + kt)[:, t * P:(t + 1) * P],
                                            pT[:, 0, t * S + kt * P:t * S + kt * P + P], W["ident"][:])
                    last.then_inc(sem("l3_pT_ps"), 1)
                pe.wait_ge(sem("l3_pT_act"), 1)
                pe.wait_ge(sem("l3_pT_dve"), 1)
                for b in range(NB):
                    for kt in range(2):
                        last = pe.matmul(ps[0:DK3, 1, b * S:(b + 1) * S], y[:, 2 * b + kt, 0:DK3],
                                         pT[:, 1, kt * T + b * S:kt * T + (b + 1) * S], start=kt == 0, stop=kt == 1)
                last.then_inc(sem("l3_head_ps"), 1)
                pe.wait_ge(sem("l3_head"), 1)
                for t in range(NT):
                    last = pe.matmul(bank(2)[:, t * P:(t + 1) * P], lg[0:DK3, t * P:(t + 1) * P], wo3[:],
                                     start=True, stop=True)
                last.then_inc(sem("l3_o_ps"), 1)

                norm_T(7)
                pe.wait_ge(sem("xT_ready"), n_T(7))
                pe.wait_ge(sem("x_done"), 7)
                for p in range(2):
                    pe.matmul(bank(1 + p), W["l3_wm"][:, p, :], xT[:], start=True, stop=True)\
                      .then_inc(sem("f3_h_ps"), 1)
                pe.wait_ge(sem("f3_h"), 2)
                for t in range(NT):
                    for p in range(2):
                        last = pe.matmul(bank(3)[:, (2 * t + p) * 64:(2 * t + p + 1) * 64],
                                         hP[:, p, t * P:(t + 1) * P], W["l3_emb"][:], start=True, stop=True)
                last.then_inc(sem("f3_lg"), 1)

                def f3_out(n):
                    h, ep = divmod(n, NEP)
                    pe.wait_ge(sem("f3_mid"), n + 1)
                    if ep == 0 and h >= 2:
                        pe.wait_ge(sem("f3_gated"), h - 1)
                    for t in range(NT):
                        col = (t % 2) * E3 * HD3 + ep * 32
                        last = pe.matmul(ps[:, 4 + 2 * (h % 2) + t // 2, col:col + 32],
                                         hT[:, 0, n % 4, t * P:(t + 1) * P], W["l3_w2"][:, ep, :],
                                         start=True, stop=True)
                    last.then_inc(sem("f3_out"), 1)

                for n in range(H3 * NEP):
                    h, ep = divmod(n, NEP)
                    g, p = h % 4, h // 4
                    if n >= 3:
                        pe.wait_ge(sem("f3_mid"), n - 2)
                    pe.matmul(bank(n % 3), W["l3_w1"][QD * g:QD * g + HD3, ep * P:(ep + 1) * P],
                              hP[QD * g:QD * g + HD3, p, :], start=True, stop=True).then_inc(sem("f3_in"), 1)
                    if n >= 2:
                        f3_out(n - 2)
                    if n == 3 * NEP:
                        pe.wait_ge(sem("f3_gate"), 1)
                        for t in range(NT):
                            last = pe.transpose(bank(3)[:, t * P:(t + 1) * P],
                                                gates[:, 8 * t:8 * t + 8, :].rearrange("p h e -> p (h e)"),
                                                W["ident"][:])
                        last.then_inc(sem("f3_gT_ps"), 1)
                    if n == 4 * NEP:
                        pe.wait_ge(sem("f3_gT"), 1)
                        for t in range(NT):
                            last = pe.matmul(bank(3)[:, t * P:(t + 1) * P], GT[:, t * P:(t + 1) * P],
                                             W["l3_b2"][:], start=True, stop=True)
                        last.then_inc(sem("f3_b"), 1)
                f3_out(H3 * NEP - 2)
                f3_out(H3 * NEP - 1)
                pe.wait_ge(sem("f3_comb"), 1)
                for t in range(NT):
                    last = pe.transpose(bank(0)[:, t * P:(t + 1) * P], acc[:, t, :], W["ident"][:])
                last.then_inc(sem("f3_cT_ps"), 1)
                pe.wait_ge(sem("f3_cT"), 1)
                for t in range(NT):
                    last = pe.matmul(bank(1)[:, t * P:(t + 1) * P], attT[:, t * P:(t + 1) * P], W["l3_fo"][:],
                                     start=True, stop=True)
                last.then_inc(sem("f3_o_ps"), 1)
                end_turn(pe, "pe")

        @block.scalar
        def _(act):
            act.wait_ge(sem("weights_loaded"), 16 * N_WEIGHTS)
            act.activation(tg[:], W["g"][:], ACT.Tanh).then_inc(sem("tg_ready"), 1)
            act.activation(ident_b[:], W["ident"][:], ACT.Copy)
            end_turn(act, "act")

            with act.Fori(0, turns):
                act.wait_ge(sem("cT_ps"), 1)
                act.activation(cT[:], bank(3), ACT.Copy).then_inc(sem("cT_ready"), 1)

                def norm_T(n):
                    act.wait_ge(sem("xT_ps"), n_T(n))
                    act.activation(xT[:], bank(0), ACT.Copy).then_inc(sem("xT_ready"), 1)

                def attention(a):
                    L = f"l{a}_"
                    func = ACT.Relu if a == 0 else ACT.Identity
                    for j in range(NJ):
                        act.wait_ge(sem(L + "k_ps"), j + 1)
                        act.activation(kP[:, j, :], bank(4 + j), func, bias=k_bias[:, a, j:j + 1])\
                           .then_inc(sem(L + "k_ready"), 1)
                    norm_T(LN_OF_ATT[a])
                    for j in range(2):
                        act.wait_ge(sem(L + "q_ps"), j + 1)
                        if a == 1:
                            ins = act.activation(qP[:, j, :], bank(Q_BANK[j]), func, bias=q_bias[:, j:j + 1],
                                                 scale=SC)
                        else:
                            ins = act.activation(qP[:, j, :], bank(Q_BANK[j]), func, scale=SC)
                        ins.then_inc(sem(L + "q_act"), 1)
                    for v in range(4 * NJ):
                        act.wait_ge(sem(L + "s2"), v + 1)
                        if v >= 3:
                            act.wait_ge(sem(L + "pv"), v - 2)
                        s = 2 * (v % 3)
                        act.activation(pT[:, v % 3, :], ps[:, s:s + 2, :].rearrange("p n k -> p (n k)"), ACT.Exp)\
                           .then_inc(sem(L + "p_ready"), 1)
                    if a:
                        act.wait_ge(sem(L + "attT_ps"), 1)
                        act.activation(attT[:], bank(0), ACT.Copy).then_inc(sem(L + "attT"), 1)

                attention(0)

                norm_T(1)
                for n in range(NC0 * (E0 + 1)):
                    act.wait_ge(sem("f0_in"), n + 1)
                    if n >= 4:
                        act.wait_ge(sem("f0_h"), n - 3)
                    act.activation(ex[:, n % 4, :], bank(n % 4), ACT.Exp, bias=l0_exp_bias[:, n:n + 1])
                    act.activation(rl[:, n % 4, :], bank(n % 4), ACT.Relu, bias=W["l0_bi"][:, n:n + 1])\
                       .then_inc(sem("f0_act"), 1)
                act.wait_ge(sem("f0_gT_ps"), 1)
                act.activation(gT, ps[0:8, 7, :], ACT.Copy).then_inc(sem("f0_gT"), 1)

                attention(1)

                act.wait_ge(sem("f1_qxT_ps"), 1)
                act.activation(qxT, bank(0).bitcast(bf16)[:, 0:T], ACT.Copy).then_inc(sem("f1_qxT"), 1)
                for t in range(NT):
                    act.wait_ge(sem("f1_y"), t + 1)
                    act.activation(hh[:, t, :], hT[:, 0, t, :], ACT.Gelu).then_inc(sem("f1_gelu"), 1)
                    act.wait_ge(sem("f1_gelu"), t + 1)
                    act.activation(hT[:, 1, t, :], hh[:, t, :], ACT.Square, accum_out=cols[:, 0, t:t + 1])\
                       .then_inc(sem("f1_sq"), 1)
                for t in range(NT):
                    act.wait_ge(sem("f1_qhT_ps"), t + 1)
                    act.activation(qhT[:, t].rearrange("p c k -> p (c k)"), bank(4 + t).bitcast(bf16)[:, 0:F0],
                                   ACT.Copy).then_inc(sem("f1_qhT"), 1)

                attention(2)

                norm_T(5)
                act.wait_ge(sem("f2_gap"), 1)
                act.activation(tw[:, :, 1], tws[:], ACT.Exp).then_inc(sem("f2_gap_exp"), 1)
                for n in range(NH2 * E2):
                    act.wait_ge(sem("f2_h1"), n + 1)
                    if n >= 2:
                        act.wait_ge(sem("f2_g"), n - 1)
                    act.activation(ex[:, n % 2, :], bank(2 * (n % 2)), ACT.Silu, bias=W["l2_bias1"][:, n:n + 1]).then_inc(sem("f2_silu"), 1)
                act.wait_ge(sem("f2_gT_ps"), 1)
                act.activation(gT, ps[0:8, 7, :], ACT.Copy).then_inc(sem("f2_gT"), 1)

                act.wait_ge(sem("l3_k_ps"), 1)
                act.activation(GT[0:DK3, :], ps[0:DK3, 1, :], ACT.Copy, scale=DK3 ** -0.5).then_inc(sem("l3_k"), 1)
                norm_T(6)
                act.wait_ge(sem("l3_q_ps"), 1)
                act.activation(attT[0:DK3, :], ps[0:DK3, 3, :], ACT.Copy).then_inc(sem("l3_q"), 1)
                act.wait_ge(sem("l3_max"), 1)
                for t in range(NT):
                    act.activation(ex[:, t // 2, (t % 2) * S:(t % 2 + 1) * S],
                                   bank(4 + t // 2)[:, (t % 2) * S:(t % 2 + 1) * S], ACT.Exp,
                                   bias=cols[:, 0, t:t + 1], accum_out=cols[:, 1, t:t + 1])\
                       .then_inc(sem("l3_exp"), 1)
                act.wait_ge(sem("l3_pT_ps"), 1)
                act.activation(pT[:, 1, 0:T], bank(6), ACT.Copy).then_inc(sem("l3_pT_act"), 1)

                norm_T(7)
                for p in range(2):
                    act.wait_ge(sem("f3_h_ps"), p + 1)
                    act.activation(hP[:, p, :], bank(1 + p), ACT.Identity, bias=W["l3_bm"][:, p:p + 1])\
                       .then_inc(sem("f3_h"), 1)
                act.wait_ge(sem("f3_lgm"), 1)
                act.activation(gates[:].rearrange("p h e -> p (h e)"), rl[:, 0, :], ACT.Exp).then_inc(sem("f3_exp"), 1)
                for n in range(H3 * NEP):
                    act.wait_ge(sem("f3_in"), n + 1)
                    if n >= 4:
                        act.wait_ge(sem("f3_out"), n - 3)
                    act.activation(hT[:, 0, n % 4, :], bank(n % 3), ACT.Gelu,
                                   bias=W["l3_b1"][:, n % NEP:n % NEP + 1]).then_inc(sem("f3_mid"), 1)
                    if n == 3 * NEP + 4:
                        act.wait_ge(sem("f3_gT_ps"), 1)
                        act.activation(GT, bank(3), ACT.Copy).then_inc(sem("f3_gT"), 1)
                act.wait_ge(sem("f3_cT_ps"), 1)
                act.activation(attT[:], bank(0), ACT.Copy).then_inc(sem("f3_cT"), 1)
                end_turn(act, "act")

        @block.vector
        def _(dve):
            step = Chain(dve, sem("dve_step"))
            dve.wait_ge(sem("weights_loaded"), 16 * N_WEIGHTS)
            for n, name in enumerate(("l1_w1", "l1_w2")):
                step(dve.tensor_reduce(wsum[:, n:n + 1], W[name], AX.X, ALU.add, apply_absolute_value=True))
            dve.engine_nop().then_inc(sem("wsum_ready"), 1)
            dve.tensor_scalar(l0_exp_bias[:], W["l0_bi"][:], math.log(ALPHA), None, ALU.add)
            dve.tensor_scalar(q_bias[:], W["l1_bq"][:], SC, None, ALU.mult)
            dve.tensor_scalar(k_bias[:, 1, :], W["l1_bk"][:], W["mrow"][:], None, ALU.add)
            for a in (0, 2):
                dve.tensor_copy(k_bias[:, a, :], W["mrow"][:].to_broadcast([P, NJ]))
            dve.tensor_reduce(wo3[:], W["l3_wo"].rearrange("p n d -> p d n"), AX.X, ALU.add)
            for m, name in enumerate(("l2_w1", "l2_w3")):
                dve.wait_ge(sem("lora"), m + 1)
                w = W[name][:].rearrange("p e h -> p (e h)")
                dve.tensor_tensor(w, w, ps[:, 4 * m:4 * m + 4, :].rearrange("p n k -> p (n k)"), ALU.add)\
                   .then_inc(sem("merged"), 1)
            dve.wait_ge(sem("lora"), 3)
            w = W["l2_w2"][:].rearrange("p e c d -> p (e c d)")
            dve.tensor_tensor(w, w, ps[:, 0:4, :].rearrange("p n k -> p (n k)"), ALU.add)
            dve.wait_ge(sem("colsum"), 1)
            dve.scalar_tensor_tensor(l0_gate_bo[:], bank(4, P), -LAMBDA * ALPHA, W["l0_gbo"][:], ALU.mult, ALU.add)
            dve.scalar_tensor_tensor(l0_exp_bo[:], ps[0:E0, 5, 0:P], -LAMBDA * ALPHA, W["l0_ebo"][:],
                                     ALU.mult, ALU.add)
            dve.wait_ge(sem("wabs"), 1)
            step(dve.tensor_scalar(wmean[:], bank(6, 2), 1.0 / (D * F0), 1e-5, ALU.mult, ALU.max))
            step(dve.reciprocal(wscale[:], wmean[:]))
            for n, (name, dst) in enumerate((("l1_w1", w1q), ("l1_w2", w2q))):
                step(dve.tensor_scalar(W[name], W[name], wscale[:, n:n + 1], -1.0, ALU.mult, ALU.max))
                step(dve.tensor_scalar(W[name], W[name], 1.0, MAGIC, ALU.min, ALU.add))
                step(dve.tensor_scalar(dst[:], W[name], -MAGIC, None, ALU.add))
            dve.wait_ge(sem("tg_ready"), 1)
            dve.tensor_scalar(tgl[:], tg[:, 4:5], LAMBDA, None, ALU.mult)
            end_turn(dve, "dve")

            with dve.Fori(0, turns):
                step = Chain(dve, sem("dve_step"))
                roots = [0]

                def root():
                    roots[0] += 1
                    dve.wait_ge(sem("rstd_ready"), roots[0])

                def layernorm():
                    for t in range(NT):
                        ins = dve.bn_stats(stats[:, t, :], x[:, t, :])
                    step(ins)
                    for t in range(NT):
                        ins = dve.bn_aggr(mv[:, t, :], stats[:, t, :])
                    step(ins)
                    dve.tensor_copy(vare[:], mv[:, :, 1]).then_inc(sem("var_ready"), 1)
                    root()
                    for t in range(NT):
                        ins = dve.tensor_scalar(xn[:, t, :], x[:, t, :], mv[:, t, 0:1], rstd[:, t:t + 1],
                                                ALU.subtract, ALU.mult)
                    ins.then_inc(sem("xn_ready"), 1)

                def add_projected(banks_, bias, n, gate):
                    step(dve.tensor_tensor(y[:], banks_.rearrange("p (t d) -> p t d", t=NT),
                                           bias[:].unsqueeze(1).to_broadcast([P, NT, D]), ALU.add))
                    dve.scalar_tensor_tensor(x[:], y[:], tg[:, gate:gate + 1], x[:], ALU.mult, ALU.add)\
                       .then_inc(sem("x_done"), 1)
                    dve.wait_ge(sem("x_done"), n)

                def attention(a):
                    L = f"l{a}_"
                    layernorm()
                    dve.wait_ge(sem(L + "v_ps"), 1)
                    vps = bank(1).rearrange("p (t h d) -> p t h d", t=NT, h=H)
                    for t in range(NT):
                        vdst, vsrc = vE[:, t, :, 0:DH], vps[:, t]
                        if a == 0:
                            ins = dve.tensor_scalar(vdst, vsrc, 0.0, None, ALU.max)
                        elif a == 1:
                            ins = dve.tensor_tensor(vdst, vsrc, W["l1_bv"][:].rearrange("p (h d) -> p h d", h=H),
                                                    ALU.add)
                        else:
                            ins = dve.tensor_copy(vdst, vsrc)
                    ins.then_inc(sem(L + "v_ready"), 1)
                    for j in range(2, NJ):
                        dve.wait_ge(sem(L + "q_ps"), j + 1)
                        src = bank(Q_BANK[j])
                        if a == 0:
                            ins = dve.tensor_scalar(qP[:, j, :], src, 0.0, SC, ALU.max, ALU.mult)
                        elif a == 1:
                            ins = dve.tensor_scalar(qP[:, j, :], src, W["l1_bq"][:, j:j + 1], SC, ALU.add, ALU.mult)
                        else:
                            ins = dve.tensor_scalar(qP[:, j, :], src, SC, None, ALU.mult)
                        ins.then_inc(sem(L + "q_dve"), 1)
                    for u in range(NJ * NB):
                        j, b = divmod(u, NB)
                        dve.wait_ge(sem(L + "s1"), u + 1)
                        s = 4 * (u % 2)
                        dve.tensor_reduce(nmp[:, 2 * b:2 * b + 2, j, MROW::QD].rearrange("p t g -> p g t"),
                                          ps[:, s:s + 4, :].rearrange("p g (t k) -> p g t k", t=2),
                                          AX.X, ALU.max, negate=True).then_inc(sem(L + "max_ready"), 1)
                    for j in range(NJ):
                        dve.wait_ge(sem(L + "max_T"), j + 1)
                        dve.scalar_tensor_tensor(qA[:, j, :], bank(j), CAP, qP[:, j, :], ALU.min, ALU.add)\
                           .then_inc(sem(L + "q_aug"), 1)
                    dve.wait_ge(sem(L + "pv"), 4 * NJ)
                    o = ps[:, 6:8, 0:2 * H * (DH + 1)].rearrange("p b (r d) -> p b r d", d=DH + 1)
                    rcv = rc[:].rearrange("p (b t) h -> p b (t h)", b=NB)
                    step(dve.reciprocal(rcv, o[:, :, :, DH]))
                    av = att[:].rearrange("p (b t) (h d) -> p b (t h) d", b=NB, h=H)
                    for b in range(NB):
                        ins = dve.tensor_tensor(av[:, b], o[:, b, :, 0:DH],
                                                rcv[:, b].unsqueeze(2).to_broadcast([P, 2 * H, DH]), ALU.mult)
                    if a == 0:
                        step(ins)
                        dve.scalar_tensor_tensor(x[:], att[:], tg[:, 0:1], x[:], ALU.mult, ALU.add)\
                           .then_inc(sem("x_done"), 1)
                        dve.wait_ge(sem("x_done"), 1)
                    else:
                        ins.then_inc(sem(L + "att_ready"), 1)
                        dve.wait_ge(sem(L + "o_ps"), 1)
                        add_projected(bank(1), W[L + "bo"], 2 * a + 1, a)

                def top2(src, n):
                    for r in range(n):
                        ins = dve.max(mx8[:, r, :], src[:, r, :])
                    step(ins)
                    for r in range(n):
                        ins = dve.max_index(ix8[:, r, :], mx8[:, r, :], src[:, r, :])
                    step(ins)
                    step(dve.tensor_copy(ixf[:, 0:n, :], ix8[:, 0:n, 0:2]))

                def expert_weights(done):
                    for k in range(2):
                        dve.tensor_tensor(oh[:, k], W["iota"][:, 0:8].unsqueeze(1).to_broadcast([P, NT, 8]),
                                          ixf[:, 0:NT, k].unsqueeze(2).to_broadcast([P, NT, 8]), ALU.is_equal)\
                           .then_inc(sem("dve_step"), 1)
                    step.n += 2
                    dve.wait_ge(step.sem, step.n)
                    for k in range(2):
                        ins = dve.tensor_tensor(oh[:, k], oh[:, k], tw[:, :, k].unsqueeze(2).to_broadcast([P, NT, 8]),
                                                ALU.mult)
                    step(ins)
                    dve.tensor_tensor(gw[:], oh[:, 0], oh[:, 1], ALU.add).then_inc(sem(done), 1)

                def expert_sum(read, n):
                    for t in range(NT):
                        src = bank(4 + (n[0]) % 2)[:, t * P:(t + 1) * P]
                        if n[1] == 0:
                            ins = dve.tensor_scalar(acc[:, t, :], src, gw[:, t, n[1]:n[1] + 1], None, ALU.mult)
                        else:
                            ins = dve.scalar_tensor_tensor(acc[:, t, :], src, gw[:, t, n[1]:n[1] + 1],
                                                           acc[:, t, :], ALU.mult, ALU.add)
                    ins.then_inc(sem(read), 1)

                def quantise(src, dst, F, n):
                    step(dve.tensor_scalar(vare[:], cols[:, 0, :], 1.0 / F, None, ALU.mult))
                    dve.engine_nop().then_inc(sem("var_ready"), 1)
                    root()
                    step(dve.tensor_tensor(cols[:, 2, :], cols[:, 1, :], rstd[:], ALU.mult))
                    step(dve.tensor_scalar(cols[:, 3, :], cols[:, 2, :], 1e-5, None, ALU.max))
                    step(dve.reciprocal(cols[:, 4, :], cols[:, 3, :]))
                    step(dve.scalar_tensor_tensor(cols[:, 5, :], cols[:, 4, :], 127.0, rstd[:], ALU.mult, ALU.mult))
                    step(dve.tensor_scalar(cols[:, 6, :], cols[:, 3, :], wmean[:, n:n + 1], 1.0 / 127.0,
                                           ALU.mult, ALU.mult))
                    for t in range(NT):
                        ins = dve.tensor_scalar(src[:, t, :], src[:, t, :], cols[:, 5, t:t + 1], -128.0,
                                                ALU.mult, ALU.max)
                    step(ins)
                    step(dve.tensor_scalar(src, src, 127.0, MAGIC, ALU.min, ALU.add))
                    return dve.tensor_scalar(dst, src, -MAGIC, None, ALU.add)

                dve.wait_ge(sem("x_loaded"), 16)
                attention(0)

                layernorm()
                for e in range(E0 + 2):
                    if e <= E0:
                        for fc in range(NC0):
                            n = NC0 * e + fc
                            dve.wait_ge(sem("f0_act"), n + 1)
                            if e >= 2 and fc == 0:
                                dve.wait_ge(sem("f0_out"), e - 1)
                            dve.scalar_tensor_tensor(hT[:, e % 2, fc, :], ex[:, n % 4, :], ALPHA, rl[:, n % 4, :],
                                                     ALU.min, ALU.add).then_inc(sem("f0_h"), 1)
                    if e == 1:
                        dve.wait_ge(sem("f0_out"), 1)
                        lgv = lg.rearrange("p (t d) -> p t d", t=NT)
                        dve.scalar_tensor_tensor(lgv, bank(4).rearrange("p (t d) -> p t d", t=NT), LAMBDA,
                                                 l0_gate_bo[:].unsqueeze(1).to_broadcast([P, NT, D]),
                                                 ALU.mult, ALU.add).then_inc(sem("f0_out_read"), 1)
                        dve.wait_ge(sem("f0_out_read"), 1)
                        top2(lgv, NT)
                        step(dve.tensor_tensor(tws[:], mx8[:, 0:NT, 0], mx8[:, 0:NT, 1], ALU.add))
                        step(dve.reciprocal(tws[:], tws[:]))
                        step(dve.tensor_tensor(tw[:], mx8[:, 0:NT, 0:2], tws[:].unsqueeze(2).to_broadcast([P, NT, 2]),
                                               ALU.mult))
                        expert_weights("f0_gate")
                        dve.wait_ge(sem("f0_gate"), 1)
                    if e >= 2:
                        dve.wait_ge(sem("f0_out"), e)
                        if e >= 3:
                            dve.wait_ge(sem("f0_out_read"), e - 1)
                        expert_sum("f0_out_read", (e - 1, e - 2))
                dve.wait_ge(sem("f0_out_read"), E0 + 1)
                step(dve.scalar_tensor_tensor(x[:], acc[:], tgl[:], x[:], ALU.mult, ALU.add))
                dve.wait_ge(sem("f0_b"), 1)
                dve.scalar_tensor_tensor(x[:], bank(6).rearrange("p (t d) -> p t d", t=NT), tg[:, 4:5], x[:],
                                         ALU.mult, ALU.add).then_inc(sem("x_done"), 1)
                dve.wait_ge(sem("x_done"), 2)

                attention(1)

                layernorm()
                dve.wait_ge(sem("xn_ready"), 4)
                step(dve.tensor_tensor(y[:], xn[:], xn[:], ALU.mult))
                dve.tensor_reduce(cols[:, 1, :], xn[:], AX.X, ALU.max, apply_absolute_value=True)
                step(dve.tensor_reduce(cols[:, 0, :], y[:], AX.X, ALU.add))
                quantise(xn[:], qx, D, 0).then_inc(sem("f1_qx"), 1)
                for t in range(NT):
                    dve.wait_ge(sem("f1_h_ps"), t + 1)
                    dve.scalar_tensor_tensor(hT[:, 0, t, :], bank(1 + t), cols[:, 6, t:t + 1], W["l1_b1"][:],
                                             ALU.mult, ALU.add).then_inc(sem("f1_y"), 1)
                dve.wait_ge(sem("f1_gelu"), NT)
                dve.wait_ge(sem("f1_sq"), NT)
                step(dve.tensor_reduce(cols[:, 1, :], hh[:], AX.X, ALU.max, apply_absolute_value=True))
                quantise(hh[:], qh, F0, 1).then_inc(sem("f1_qh"), 1)
                dve.wait_ge(sem("f1_o_ps"), 1)
                for t in range(NT):
                    ins = dve.scalar_tensor_tensor(y[:, t, :], bank(0)[:, t * P:(t + 1) * P], cols[:, 6, t:t + 1],
                                                   W["l1_b2"][:], ALU.mult, ALU.add)
                step(ins)
                dve.scalar_tensor_tensor(x[:], y[:], tg[:, 5:6], x[:], ALU.mult, ALU.add)\
                   .then_inc(sem("x_done"), 1)
                dve.wait_ge(sem("x_done"), 4)

                attention(2)

                layernorm()
                dve.wait_ge(sem("f2_lg"), 1)
                lgv = lg[:, 0:NT * 8].rearrange("p (t e) -> p t e", t=NT)
                step(dve.tensor_copy(lg[:, 0:NT * 8], bank(7, NT * 8)))
                top2(lgv, NT)
                dve.tensor_tensor(tws[:], mx8[:, 0:NT, 1], mx8[:, 0:NT, 0], ALU.subtract)\
                   .then_inc(sem("f2_gap"), 1)
                dve.wait_ge(sem("f2_gap_exp"), 1)
                step(dve.tensor_scalar(tws[:], tw[:, :, 1], 1.0, None, ALU.add))
                step(dve.reciprocal(tw[:, :, 0], tws[:]))
                step(dve.tensor_tensor(tw[:, :, 1], tw[:, :, 1], tw[:, :, 0], ALU.mult))
                expert_weights("f2_gate")
                dve.wait_ge(sem("f2_gate"), 1)
                for e in range(E2 + 1):
                    if e < E2:
                        for hc in range(NH2):
                            n = NH2 * e + hc
                            dve.wait_ge(sem("f2_silu"), n + 1)
                            dve.wait_ge(sem("f2_h3"), n + 1)
                            if e >= 2 and hc == 0:
                                dve.wait_ge(sem("f2_out"), e - 1)
                            dve.scalar_tensor_tensor(hT[:, e % 2, hc, :], bank(2 * (n % 2) + 1),
                                                     W["l2_bias3"][:, n:n + 1], ex[:, n % 2, :],
                                                     ALU.add, ALU.mult).then_inc(sem("f2_g"), 1)
                    if e >= 1:
                        dve.wait_ge(sem("f2_out"), e)
                        if e >= 2:
                            dve.wait_ge(sem("f2_out_read"), e - 1)
                        expert_sum("f2_out_read", (e - 1, e - 1))
                dve.wait_ge(sem("f2_out_read"), E2)
                step(dve.scalar_tensor_tensor(x[:], acc[:], tg[:, 6:7], x[:], ALU.mult, ALU.add))
                dve.wait_ge(sem("f2_b"), 1)
                dve.scalar_tensor_tensor(x[:], bank(6).rearrange("p (t d) -> p t d", t=NT), tg[:, 6:7], x[:],
                                         ALU.mult, ALU.add).then_inc(sem("x_done"), 1)
                dve.wait_ge(sem("x_done"), 6)

                layernorm()
                dve.wait_ge(sem("l3_v_ps"), 1)
                dve.tensor_copy(y[:, :, 0:DK3], bank(2, NT * DK3).rearrange("p (t d) -> p t d", t=NT))
                dve.wait_ge(sem("l3_s"), 1)
                dve.tensor_reduce(cols[:, 0, :].rearrange("p (b t) -> p b t", b=2),
                                  ps[:, 4:6, :].rearrange("p b (t k) -> p b t k", t=2),
                                  AX.X, ALU.max, negate=True).then_inc(sem("l3_max"), 1)
                dve.wait_ge(sem("l3_exp"), NT)
                step(dve.reciprocal(cols[:, 2, :], cols[:, 1, :]))
                for t in range(NT):
                    ins = dve.tensor_scalar(pT[:, 0, t * S:(t + 1) * S], ex[:, t // 2, (t % 2) * S:(t % 2 + 1) * S],
                                            cols[:, 2, t:t + 1], None, ALU.mult)
                ins.then_inc(sem("l3_p"), 1)
                dve.wait_ge(sem("l3_pT_ps"), 2)
                dve.tensor_copy(pT[:, 1, T:2 * T], bank(7)).then_inc(sem("l3_pT_dve"), 1)
                dve.wait_ge(sem("l3_head_ps"), 1)
                dve.tensor_tensor(lg[0:DK3, :], ps[0:DK3, 1, :], attT[0:DK3, :], ALU.add).then_inc(sem("l3_head"), 1)
                dve.wait_ge(sem("l3_o_ps"), 1)
                add_projected(bank(2), W["l3_bo"], 7, 3)

                layernorm()
                dve.wait_ge(sem("f3_lg"), 1)
                step(dve.tensor_copy(lg, bank(3)))
                lgv = lg.rearrange("p (r e) -> p r e", e=E3)
                for r in range(32):
                    ins = dve.max(mx8[:, r, :], lgv[:, r, :])
                step(ins)
                dve.tensor_tensor(rl[:, 0, :].rearrange("p (r e) -> p r e", e=E3), lgv,
                                  mx8[:, :, 0:1].to_broadcast([P, 32, E3]), ALU.subtract)\
                   .then_inc(sem("f3_lgm"), 1)
                for r in range(32):
                    ins = dve.max_index(ix8[:, r, :], mx8[:, r, :], lgv[:, r, :])
                step(ins)
                step(dve.tensor_copy(ixf[:], ix8[:, :, 0:2]))
                for k in range(2):
                    ins = dve.tensor_tensor(oh16[:, k], W["iota"][:].unsqueeze(1).to_broadcast([P, 32, E3]),
                                            ixf[:, :, k:k + 1].to_broadcast([P, 32, E3]), ALU.is_equal)
                step(ins)
                step(dve.tensor_tensor(oh16[:, 0], oh16[:, 0], oh16[:, 1], ALU.add))
                dve.wait_ge(sem("f3_exp"), 1)
                step(dve.tensor_reduce(gsum[:], gates[:], AX.X, ALU.add))
                step(dve.reciprocal(gsum[:], gsum[:]))
                step(dve.tensor_tensor(gates[:], gates[:], oh16[:, 0], ALU.mult))
                dve.tensor_tensor(gates[:], gates[:], gsum[:].unsqueeze(2).to_broadcast([P, 32, E3]), ALU.mult)\
                   .then_inc(sem("f3_gate"), 1)
                dve.wait_ge(sem("f3_gate"), 1)
                gv = gates[:].rearrange("p (t h) e -> p t h e", t=NT)
                for h in range(H3):
                    dve.wait_ge(sem("f3_out"), NEP * (h + 1))
                    eo = ps[:, 4 + 2 * (h % 2):6 + 2 * (h % 2), :].rearrange("p b k -> p (b k)")
                    dve.tensor_tensor(gated[:, h % 2].rearrange("p t (e o) -> p t e o", e=E3),
                                      eo.rearrange("p (t e o) -> p t e o", t=NT, e=E3),
                                      gv[:, :, h, :].unsqueeze(3).to_broadcast([P, NT, E3, HD3]), ALU.mult)\
                       .then_inc(sem("f3_gated"), 1)
                    dve.wait_ge(sem("f3_gated"), h + 1)
                    ins = dve.tensor_reduce(acc[:, :, h * HD3:(h + 1) * HD3],
                                            gated[:, h % 2].rearrange("p t (e o) -> p t o e", e=E3), AX.X, ALU.add)
                step(ins)
                dve.wait_ge(sem("f3_b"), 1)
                dve.tensor_tensor(acc[:], acc[:], bank(3).rearrange("p (t d) -> p t d", t=NT), ALU.add)\
                   .then_inc(sem("f3_comb"), 1)
                dve.wait_ge(sem("f3_o_ps"), 1)
                add_projected(bank(1), W["l3_fbo"], 8, 7)
                end_turn(dve, "dve")

        @block.sync
        def _(sp):
            for name in WEIGHTS:
                w = W[name]
                sp.dma_start(w if name in SETUP_ONLY else w[:], A[name]).then_inc(sem("weights_loaded"), 16)
            sp.wait_ge(sem("weights_loaded"), 16 * N_WEIGHTS)
            numbers = sorted(s.num for n, s in sems.items() if n not in kept)
            assert numbers[-1] - numbers[0] + 1 == len(numbers)

            def clear():
                sp.wait_ge(turn_end, 4)
                sp.sem_clear(turn_end)
                sp.sem_clear(range(numbers[0], numbers[-1] + 1))
                for e in GO:
                    sp.sem_inc(GO[e], 1)

            xv = A["x"].rearrange("(n p) d -> p n d", p=P)
            cv = A["ctx"].rearrange("(n p) d -> p n d", p=P)
            ov = out.rearrange("(n p) d -> p n d", p=P)
            mq = A["mask1_q"].rearrange("(n p) k -> p n k", p=P)
            mk = A["mask1_k"].rearrange("(n p) k -> p n k", p=P)
            clear()
            with sp.Fori(0, turns) as i:
                sp.dma_start(x[:], xv[:, bass.ds(i * NT, NT), :]).then_inc(sem("x_loaded"), 16)
                sp.dma_start(ctxs[:], cv[:, bass.ds(i * NT, NT), :]).then_inc(sem("ctx_loaded"), 16)
                sp.dma_start(m1[:, 0], mq[:, bass.ds(i * NT, NT), :]).then_inc(sem("masks_loaded"), 16)
                sp.dma_start(m1[:, 1], mk[:, bass.ds(i * NT, NT), :]).then_inc(sem("masks_loaded"), 16)
                sp.wait_ge(sem("x_done"), 8)
                sp.dma_start(ov[:, bass.ds(i * NT, NT), :], x[:]).then_inc(sem("out_stored"), 16)
                sp.wait_ge(sem("out_stored"), 16)
                clear()


LN_OF_ATT = (0, 2, 4)


def n_T(n):
    return n + 1 - (n > 3)


Q_BANK = (0, 2, 3, 1)

WEIGHTS = {
    "ident": ([P, P], "f"), "ones": ([P, P], "f"), "pick": ([P, E0, E0], "f"), "iota": ([P, E3], "f"),
    "mrow": ([P, 1], "f"), "g": ([P, 8], "f"),
    "l0_wq": ([P, NJ, P], "f"), "l0_wk": ([P, NJ, P], "f"), "l0_wv": ([P, P], "f"),
    "l1_wq": ([P, NJ, P], "f"), "l1_wk": ([P, NJ, P], "f"), "l1_wv": ([P, P], "f"), "l1_wo": ([P, P], "f"),
    "l1_bq": ([P, NJ], "f"), "l1_bk": ([P, NJ], "f"), "l1_bv": ([P, P], "f"), "l1_bo": ([P, P], "f"),
    "l2_wq": ([P, NJ, P], "f"), "l2_wk": ([P, NJ, P], "f"), "l2_wv": ([P, P], "f"), "l2_wo": ([P, P], "f"),
    "l2_bo": ([P, P], "f"),
    "adj_q": ([P, 2, S], "f"), "adj_k": ([P, 2, S], "f"), "mask0_q": ([P, 2, S], "i"), "mask0_k": ([P, 2, S], "i"),
    "l0_wi": ([P, E0 + 1, F0], "f"), "l0_bi": ([P, (E0 + 1) * NC0], "f"), "l0_wo": ([P, E0 + 1, NC0, P], "f"),
    "l0_gbo": ([P, P], "f"), "l0_ebo": ([E0, P], "f"),
    "l1_w1": ([P, F0], "f"), "l1_b1": ([P, F0], "f"), "l1_w2": ([P, F0], "f"), "l1_b2": ([P, P], "f"),
    "l2_wg": ([P, E2], "f"), "l2_w1": ([P, E2, H2], "f"), "l2_w3": ([P, E2, H2], "f"),
    "l2_w2": ([P, E2, NH2, P], "f"), "l2_a1": ([R2, E2, P], "f"), "l2_a3": ([R2, E2, P], "f"),
    "l2_a2": ([R2, E2, H2], "f"), "l2_b1": ([R2, E2, H2], "f"), "l2_b3": ([R2, E2, H2], "f"),
    "l2_b2": ([R2, E2, P], "f"), "l2_bias1": ([P, E2 * NH2], "f"), "l2_bias3": ([P, E2 * NH2], "f"),
    "l2_bias2": ([E2, P], "f"),
    "l3_wi": ([P, DK3], "f"), "l3_wo": ([DK3, 16, P], "f"), "l3_bo": ([P, P], "f"),
    "l3_wm": ([P, 2, P], "f"), "l3_bm": ([P, 2], "f"), "l3_emb": ([P, 64], "f"), "l3_w1": ([P, E3 * I3], "f"),
    "l3_b1": ([P, NEP], "f"), "l3_w2": ([P, NEP, 32], "f"), "l3_b2": ([P, P], "f"), "l3_fo": ([P, P], "f"),
    "l3_fbo": ([P, P], "f"),
}
N_WEIGHTS = len(WEIGHTS)
SETUP_ONLY = {
    "l1_w1": ("m1", 0), "l1_w2": ("m1", F0), "l2_a1": ("hT", 0), "l2_b1": ("hT", E2 * P), "l2_a3": ("hT", E2 * (P + H2)), "l2_b3": ("qP", 0),
    "l2_a2": ("kP", 0), "l2_b2": ("rl", 0), "l3_wo": ("ex", 0),
    "mask0_q": ("rl", E2 * P), "mask0_k": ("rl", E2 * P + 2 * S),
}


def layout(I):
    import numpy as np
    f = np.float32

    def rows(v):
        return np.repeat(v.reshape(1, -1), P, 0)

    def packed(w):
        r = np.zeros((w.shape[1], NJ, G, QD), w.dtype)
        r[..., :DH] = w.T.reshape(w.shape[1], NJ, G, DH)
        return r.reshape(w.shape[1], NJ, P)

    def packed_bias(v):
        r = np.zeros((NJ, G, QD), v.dtype)
        r[..., :DH] = v.reshape(NJ, G, DH)
        return r.reshape(NJ, P).T

    def tiles(m):
        return m.reshape(2, P, -1).transpose(1, 0, 2)

    o = {"ident": np.eye(P, dtype=f), "ones": np.ones((P, P), f),
         "pick": np.repeat(np.eye(E0, dtype=f)[None], P, 0), "iota": rows(np.arange(E3, dtype=f))}
    mrow = np.zeros((P, 1), f)
    mrow[MROW::QD] = 1.0
    o["mrow"] = mrow
    o["g"] = rows(np.concatenate([I["g_xattn"], I["g_ffn"]]))
    for a, (q, k, v) in enumerate((("Wq", "Wk", "Wv"), ("Wq", "Wk", "Wv"), ("wq", "wk", "wv"))):
        o[f"l{a}_wq"], o[f"l{a}_wk"] = packed(I[f"L{a}_xattn_{q}"]), packed(I[f"L{a}_xattn_{k}"])
        o[f"l{a}_wv"] = I[f"L{a}_xattn_{v}"].T
    o["l1_wo"], o["l2_wo"] = I["L1_xattn_Wo"].T, I["L2_xattn_wo"].T
    o["l1_bq"], o["l1_bk"] = packed_bias(I["L1_xattn_bq"]), packed_bias(I["L1_xattn_bk"])
    o["l1_bv"], o["l1_bo"], o["l2_bo"] = rows(I["L1_xattn_bv"]), rows(I["L1_xattn_bo"]), rows(I["L2_xattn_bo"])
    o["adj_q"], o["adj_k"] = tiles(I["L1_xattn_adj"]), tiles(I["L1_xattn_adj"].T)
    m0 = I["mask_1x1xSxS2_ik0"][0, 0]
    o["mask0_q"], o["mask0_k"] = tiles(m0), tiles(m0.T)
    m1 = I["mask_Bx1xSxS2_ik1"][:, 0]
    o["mask1_q"] = m1.reshape(BATCH * S, S)
    o["mask1_k"] = m1.transpose(0, 2, 1).reshape(BATCH * S, S)
    wi = np.concatenate([I["L0_ffn_gate_wi"][None], I["L0_ffn_exp_wi"]])
    bi = np.concatenate([I["L0_ffn_gate_bi"][None], I["L0_ffn_exp_bi"]])
    wo = np.concatenate([I["L0_ffn_gate_wo"][None], I["L0_ffn_exp_wo"]])
    o["l0_wi"] = wi.transpose(1, 0, 2)
    o["l0_bi"] = bi.reshape(-1, P).T
    o["l0_wo"] = wo.reshape(E0 + 1, NC0, P, P).transpose(2, 0, 1, 3)
    o["l0_gbo"], o["l0_ebo"] = rows(I["L0_ffn_gate_bo"]), I["L0_ffn_exp_bo"]
    o["l1_w1"], o["l1_b1"] = I["L1_ffn_w1"].T, rows(I["L1_ffn_b1"])
    o["l1_w2"] = I["L1_ffn_w2"].T.reshape(NC0, P, P).transpose(1, 0, 2).reshape(P, F0)
    o["l1_b2"] = rows(I["L1_ffn_b2"])
    o["l2_wg"] = I["L2_ffn_Wg"].T
    for n in "13":
        o["l2_w" + n] = I["L2_ffn_W" + n].transpose(2, 0, 1)
        o["l2_a" + n] = I["L2_ffn_A" + n].transpose(1, 0, 2)
        o["l2_b" + n] = I["L2_ffn_B" + n].transpose(2, 0, 1)
        o[f"l2_bias{n}"] = I["L2_ffn_b" + n].reshape(-1, P).T
    o["l2_w2"] = I["L2_ffn_W2"].transpose(2, 0, 1).reshape(NH2, P, E2, P).transpose(1, 2, 0, 3)
    o["l2_a2"] = I["L2_ffn_A2"].transpose(1, 0, 2)
    o["l2_b2"] = I["L2_ffn_B2"].transpose(2, 0, 1)
    o["l2_bias2"] = I["L2_ffn_b2"]
    o["l3_wi"] = I["L3_xattn_wi"]
    o["l3_wo"] = I["L3_xattn_Wo"].reshape(16, DK3, P).transpose(1, 0, 2)
    o["l3_bo"] = rows(I["L3_xattn_bo"])
    wm = np.zeros((P, 2, G, QD), f)
    wm[..., :HD3] = I["L3_ffn_Wm"].reshape(P, 2, G, HD3)
    o["l3_wm"] = wm.reshape(P, 2, P)
    bm = np.zeros((2, G, QD), f)
    bm[..., :HD3] = I["L3_ffn_bm"].reshape(2, G, HD3)
    o["l3_bm"] = bm.reshape(2, P).T
    emb = np.zeros((G, QD, G, E3), f)
    w1 = np.zeros((G, QD, E3 * I3), f)
    for g in range(G):
        emb[g, :HD3, g] = I["L3_ffn_expert_emb"]
        w1[g, :HD3] = I["L3_ffn_W1"].transpose(1, 0, 2).reshape(HD3, E3 * I3)
    o["l3_emb"], o["l3_w1"] = emb.reshape(P, G * E3), w1.reshape(P, E3 * I3)
    o["l3_b1"] = I["L3_ffn_b1"].reshape(NEP, P).T
    w2 = np.zeros((2, I3, NEP, 2, HD3), f)
    for k in range(2):
        w2[k, :, :, k] = I["L3_ffn_W2"][k::2].transpose(1, 0, 2)
    o["l3_w2"] = w2.reshape(P, NEP, 32)
    b2 = np.zeros((H3, E3, H3, HD3), f)
    for h in range(H3):
        b2[h, :, h] = I["L3_ffn_b2"]
    o["l3_b2"] = b2.reshape(P, P)
    o["l3_fo"], o["l3_fbo"] = I["L3_ffn_Wo"], rows(I["L3_ffn_bo"])
    o["x"], o["ctx"] = I["x"].reshape(BATCH * S, D), I["ctx_1024"].reshape(BATCH * S, D)
    return o


def kernel(**inputs):
    import numpy as np
    import concourse.bacc as bacc
    from concourse.bass_utils import run_bass_kernel_spmd as run

    nc = bacc.Bacc("TRN2", target_bir_lowering=False, num_devices=1)
    arrays = {k: np.ascontiguousarray(v) for k, v in layout({k: np.asarray(v) for k, v in inputs.items()}).items()}
    A = {k: nc.dram_tensor("in_" + k, v.shape, mybir.dt.from_np(v.dtype), kind="ExternalInput").ap()
         for k, v in arrays.items()}
    out = nc.dram_tensor("out_x", (BATCH * S, D), mybir.dt.float32, kind="ExternalOutput").ap()
    flamingo(nc, A, out)
    r = run(nc, [{"in_" + k: v for k, v in arrays.items()}], core_ids=[0])
    return r.results[0]["out_x"].reshape(BATCH, S, D)
```

```python
import math

import concourse.bass as bass
from concourse import mybir
from contextlib import ExitStack

P = 128
BATCH, S, D = 8, 256, 128
NB = 2
TURNS = BATCH // NB
NT = NB * S // P
T = NT * P
H, DH = 16, 8
X_PARTS = (0, 0, 1, 1, 0, 2)
Y_PARTS = (0, 1, 0, 1, 2, 0)
NSEG = len(X_PARTS)
HP = 2
NK = H // HP
KS = NSEG * DH
KS3 = NSEG * 16
VW = 3 * (DH + 1)
SC = DH ** -0.5
E0, F0 = 8, 512
NC0 = F0 // P
E2, H2, R2 = 8, 256, 16
NH2 = H2 // P
DK3 = 64
H3, E3, HD3, I3 = 8, 16, 16, 64
NEP = E3 * I3 // P
LAMBDA = 1.0507009873554804934193349852946
ALPHA = 1.6732632423543772848170429916717
EPS = 1e-5
MAGIC = 12582912.0
NEG = -1.0e30
CAP = 1.0e25


class Chain:

    def __init__(self, eng, sem):
        self.eng, self.sem, self.n = eng, sem, 0

    def __call__(self, ins):
        self.n += 1
        ins.then_inc(self.sem, 1)
        self.eng.wait_ge(self.sem, self.n)


def flamingo(nc, A, out, turns=TURNS):
    f32, bf16, i32, u32 = mybir.dt.float32, mybir.dt.bfloat16, mybir.dt.int32, mybir.dt.uint32
    ALU, ACT, AX = mybir.AluOpType, mybir.ActivationFunctionType, mybir.AxisListType
    ctx = ExitStack()
    with ctx:
        def sb(name, shape, dt=f32):
            return ctx.enter_context(nc.sbuf_tensor(name, shape, dt))

        W = {}
        for name, (shape, dt) in WEIGHTS.items():
            if name not in SETUP_ONLY:
                W[name] = sb("w_" + name, shape, {"f": f32, "i": i32, "b": bf16}[dt])
        ident_b = sb("ident_b", [P, P], bf16)
        tg = sb("tg", [P, 8])
        tgl = sb("tgl", [P, 1])
        l0_exp_bias = sb("l0_exp_bias", [P, (E0 + 1) * NC0])
        l0_gate_bo = sb("l0_gate_bo", [P, P])
        l0_exp_bo = sb("l0_exp_bo", [E0, P])
        q_bias = sb("q_bias", [P, 1])
        w1s = sb("w1s", [KS3, E3 * I3], bf16)
        wsum = sb("wsum", [P, 2])
        wmean = sb("wmean", [P, 2])
        wscale = sb("wscale", [P, 2])
        w1q = sb("w1q", [P, F0], bf16)
        w2q = sb("w2q", [P, F0], bf16)
        wo3 = sb("wo3", [DK3, P])
        l2_bias_q = sb("l2_bias_q", [P, 2, S], bf16)
        l2_bias_k = sb("l2_bias_k", [P, 2, S], bf16)

        x = sb("x", [P, NT, D])
        xn = sb("xn", [P, NT, D])
        xT = sb("xT", [P, T])
        cT = sb("cT", [P, T])
        stats = sb("stats", [P, NT, 6])
        mv = sb("mv", [P, NT, 2])
        vare = sb("vare", [P, NT])
        rstd = sb("rstd", [P, NT])
        mhalf = sb("mhalf", [P, NT])
        m1 = sb("m1", [P, NT, S], i32)
        bfull = sb("bfull", [P, NT, S])
        b1q = sb("b1q", [P, 2, NT, S], bf16)
        b1k = sb("b1k", [P, 3, NT, S], bf16)
        qS = sb("qS", [P, NK, T], bf16)
        kS = sb("kS", [P, NK, T], bf16)
        kf = sb("kf", [P, T])
        vf = sb("vf", [P, NT, D])
        qp = sb("qp", [P, 3, T], bf16)
        kp = qp
        vE = sb("vE", [P, NT, H, 3, DH + 1], bf16)
        nm = sb("nm", [P, NT, H])
        nmp = sb("nmp", [P, NT, 2, H], bf16)
        nmT = sb("nmT", [2 * H, T], bf16)
        osum = sb("osum", [P, NT, H, DH + 1])
        rc = sb("rc", [P, NT, H])
        att = sb("att", [P, NT, D])
        ctxs = att
        attT = sb("attT", [P, T])
        qf = attT
        y = sb("y", [P, NT, D])
        ex = sb("ex", [P, 4, T])
        rl = sb("rl", [P, 4, T])
        f16 = mybir.dt.float16
        pH = ex[:].rearrange("p a k -> p (a k)")[:, 0:6 * S].bitcast(f16).rearrange("p (n k) -> p n k", n=3)
        pL = rl[:].rearrange("p a k -> p (a k)")[:, 0:6 * S].bitcast(f16).rearrange("p (n k) -> p n k", n=3)
        hT = sb("hT", [P, 2, NC0, T])
        pT = hT[:].rearrange("p a c k -> p (a c k)")[:, 0:3 * 4 * S].rearrange("p (n k) -> p n k", n=3)
        acc = sb("acc", [P, NT, D])
        mx8 = sb("mx8", [P, 32, 8])
        ix8 = sb("ix8", [P, 32, 8], u32)
        ixf = sb("ixf", [P, 32, 2])
        tw = sb("tw", [P, NT, 2])
        tws = sb("tws", [P, NT])
        oh = sb("oh", [P, 2, NT, 8])
        gw = sb("gw", [P, NT, 8])
        gT = attT[0:8, :]
        lg = y[:].rearrange("p t d -> p (t d)")
        cols = sb("cols", [P, 8, NT])
        hh = rl
        kb = qS[:].rearrange("p j k -> p (j k)")
        qh = kb[:, 0:NT * F0].rearrange("p (t f) -> p t f", t=NT)
        qhT = kb[:, NT * F0:].rearrange("p (t c k) -> p t c k", t=NT, c=NC0)
        oh16 = rl[:, 1:3, :].rearrange("p a (r e) -> p a r e", e=E3)
        gates = sb("gates", [P, 32, E3])
        gb = gates[:].rearrange("p r e -> p (r e)").bitcast(bf16)
        qx = gb[:, 0:T].rearrange("p (t d) -> p t d", t=NT)
        qxT = gb[:, T:2 * T]
        gsum = sb("gsum", [P, 32])
        GT = rl[:, 3, :]
        gated = ex[:].rearrange("p a (t k) -> p (a t k)", t=2).rearrange("p (a t k) -> p a t k", a=2, t=NT)
        homes = {"hT": hT[:].rearrange("p a c k -> p (a c k)"), "qP": qS[:].rearrange("p j k -> p (j k)").bitcast(f32),
                 "kP": kS[:].rearrange("p j k -> p (j k)").bitcast(f32), "rl": rl[:].rearrange("p a k -> p (a k)"),
                 "m1": m1[:].rearrange("p t k -> p (t k)").bitcast(f32), "ex": ex[:].rearrange("p a k -> p (a k)"),
                 "vfree": bfull[:].rearrange("p t k -> p (t k)")}
        for name, (home, at) in SETUP_ONLY.items():
            (rows_, *free), dt = WEIGHTS[name]
            flat = homes[home][0:rows_, at:at + math.prod(free)]
            if dt == "i":
                flat = flat.bitcast(i32)
            W[name] = flat.rearrange("p (a b) -> p a b", a=free[0]) if len(free) > 1 else flat

        ps = ctx.enter_context(nc.psum_tensor("ps", [P, 8, 512], f32))

        def bank(n, width=512):
            return ps[:, n, 0:width]

        sems = {}
        nums = []

        def sem(name):
            if name not in sems:
                sems[name] = ctx.enter_context(nc.semaphore(name))
            return sems[name]

        def upto(name, a, n):
            return sem(name), PER_ATTENTION[name] * (a - (name in PROJECTED)) + n

        turn_end = sem("turn_end")
        GO = {e: sem("go_" + e) for e in ("pe", "act", "dve", "pool")}
        kept = set(sems)
        stored = sem("out_stored")
        block = ctx.enter_context(nc.Block())

        def end_turn(eng, who):
            eng.drain().then_inc(turn_end, 1)
            eng.wait_ge(GO[who], 1)
            eng.sem_clear(GO[who])

        FFN_LN = {0: 1, 1: 3, 2: 5, 3: 7}

        @block.gpsimd
        def _(pool):
            step = Chain(pool, sem("pool_step"))
            pool.memset(mhalf[:], -0.5)
            step(pool.memset(vE[:], 0.0))
            pool.memset(vE[:, :, :, 0, DH:DH + 1], 1.0)
            pool.wait_ge(sem("weights_loaded"), 16 * N_WEIGHTS)
            for dst, src in ((l2_bias_q, W["mask0_q"]), (l2_bias_k, W["mask0_k"])):
                pool.tensor_scalar(dst[:], src, 0.0, NEG, ALU.is_equal, ALU.mult)
            end_turn(pool, "pool")
            with pool.Fori(0, turns):
                step = Chain(pool, sem("pool_step"))
                ln = iter(range(8))

                def root(n_ready, n):
                    pool.wait_ge(sem("var_ready"), n_ready)
                    step(pool.tensor_scalar(vare[:], vare[:], EPS, None, ALU.add))
                    pool.tensor_tensor(rstd[:], vare[:], mhalf[:], ALU.pow).then_inc(sem("rstd_ready"), 1)

                def biases():
                    for side, parts, dst, adj in ((0, 2, b1q, W["adj_q"]), (1, 3, b1k, W["adj_k"])):
                        pool.wait_ge(sem("masks_loaded"), 16 * (side + 1))
                        pool.tensor_scalar(bfull[:], m1[:], 0.0, NEG, ALU.is_equal, ALU.mult)\
                            .then_inc(sem("mask_read"), 1)
                        pool.wait_ge(sem("mask_read"), side + 1)
                        for b in range(NB):
                            ins = pool.tensor_tensor(bfull[:, 2 * b:2 * b + 2, :], bfull[:, 2 * b:2 * b + 2, :],
                                                     adj[:], ALU.add)
                            step(ins)
                        for part in range(parts):
                            last = pool.tensor_copy(dst[:, part], bfull[:])
                            step(last)
                            if part + 1 < parts:
                                step(pool.tensor_tensor(bfull[:], bfull[:], dst[:, part], ALU.subtract))
                    pool.engine_nop().then_inc(sem("l1_bias_ready"), 1)

                def split(src, part):
                    step(pool.tensor_copy(part(0), src))
                    step(pool.tensor_tensor(src, src, part(0), ALU.subtract))
                    step(pool.tensor_copy(part(1), src))
                    return pool.tensor_tensor(part(2), src, part(1), ALU.subtract)

                def keys_values(a):
                    L = f"l{a}_"
                    pool.wait_ge(*upto("kf", a, 1))
                    split(kf[:], lambda n: kp[:, n, :]).then_inc(sem("kp"), 1)
                    pool.wait_ge(*upto("vf", a, 1))
                    split(vf[:].rearrange("p t (h d) -> p (t h) d", h=H),
                          lambda n: vE[:, :, :, n, 0:DH].rearrange("p t h d -> p (t h) d"))\
                        .then_inc(sem("v_ready"), 1)

                root(1, 0)
                keys_values(0)
                root(2, 1)
                keys_values(1)
                biases()
                root(3, 2)
                root(4, 3)
                root(5, 3)
                keys_values(2)
                root(6, 3)
                root(7, 4)
                for n in range(8, 11):
                    root(n, n)
                end_turn(pool, "pool")

        @block.tensor
        def _(pe):
            pe.wait_ge(sem("weights_loaded"), 16 * N_WEIGHTS)
            for m, (a, b) in enumerate((("l2_a1", "l2_b1"), ("l2_a3", "l2_b3"))):
                for e in range(E2):
                    last = pe.matmul(ps[:, 4 * m + e // 2, (e % 2) * H2:(e % 2 + 1) * H2],
                                     W[a][:, e, :], W[b][:, e, :], start=True, stop=True)
                last.then_inc(sem("lora"), 1)
            pe.wait_ge(sem("merged"), 1)
            for e in range(E2):
                for hc in range(NH2):
                    i = NH2 * e + hc
                    last = pe.matmul(ps[:, i // 4, (i % 4) * P:(i % 4 + 1) * P],
                                     W["l2_a2"][:, e, hc * P:(hc + 1) * P], W["l2_b2"][:, e, :],
                                     start=True, stop=True)
            last.then_inc(sem("lora"), 1)
            pe.wait_ge(sem("merged"), 2)
            for fc in range(NC0):
                pe.matmul(bank(4, P), W["ones"][:], W["l0_wo"][:, 0, fc, :], start=fc == 0, stop=fc == NC0 - 1)
            for e in range(E0):
                for fc in range(NC0):
                    last = pe.matmul(ps[0:E0, 5, 0:P], W["pick"][:, e, :], W["l0_wo"][:, e + 1, fc, :],
                                     start=e + fc == 0, stop=e == E0 - 1 and fc == NC0 - 1)
            last.then_inc(sem("colsum"), 1)
            pe.wait_ge(sem("wsum_ready"), 1)
            pe.matmul(bank(6, 2), W["ones"][:], wsum[:], start=True, stop=True).then_inc(sem("wabs"), 1)
            end_turn(pe, "pe")

            with pe.Fori(0, turns):
                pe.wait_ge(sem("ctx_loaded"), 16)
                for t in range(NT):
                    last = pe.transpose(bank(3)[:, t * P:(t + 1) * P], ctxs[:, t, :], W["ident"][:])
                last.then_inc(sem("cT_ps"), 1)
                pe.wait_ge(sem("cT_ready"), 1)

                def norm_T(n):
                    pe.wait_ge(sem("xn_ready"), n + 1)
                    for t in range(NT):
                        last = pe.transpose(bank(0)[:, t * P:(t + 1) * P], xn[:, t, :], W["ident"][:])
                    last.then_inc(sem("xT_ps"), 1)

                def keys_values(a):
                    L = f"l{a}_"
                    pe.matmul(bank(6), W[L + "wk"][:], cT[:], start=True, stop=True).then_inc(sem("k_ps"), 1)
                    for t in range(NT):
                        last = pe.matmul(bank(7)[:, t * P:(t + 1) * P], cT[:, t * P:(t + 1) * P], W[L + "wv"][:],
                                         start=True, stop=True)
                    last.then_inc(sem("v_ps"), 1)

                def key_stack(a, j):
                    L = f"l{a}_"
                    if j == 0:
                        pe.wait_ge(*upto("kp", a, 1))
                        pe.wait_ge(*upto("vf", a, 1))
                    if j >= 2:
                        pe.wait_ge(*upto(("ks_act", "ks_dve")[j % 2], a, j // 2))
                    for n in range(3):
                        last = pe.matmul(bank(6 + j % 2), W["sel_y"][:, n, j, :], kp[:, n, :],
                                         start=n == 0, stop=n == 2)
                    last.then_inc(sem("ks_ps"), 1)

                def attention(a):
                    L = f"l{a}_"
                    norm_T(LN_OF_ATT[a])
                    pe.wait_ge(sem("xT_ready"), n_T(LN_OF_ATT[a]))
                    pe.matmul(bank(1), W[L + "wq"][:], xT[:], start=True, stop=True).then_inc(sem("q_ps"), 1)
                    pe.wait_ge(*upto("qp", a, 1))
                    for j in range(NK):
                        if j >= 4:
                            pe.wait_ge(*upto(("qs_act", "qs_dve")[j % 2], a, j // 2 - 1))
                        for n in range(3):
                            last = pe.matmul(bank(2 + j % 4), W["sel_x"][:, n, j, :], qp[:, n, :],
                                             start=n == 0, stop=n == 2)
                        last.then_inc(sem("qs_ps"), 1)
                    for name in ("qs_act", "qs_dve", "ks_act", "ks_dve"):
                        pe.wait_ge(*upto(name, a, NK // 2))
                    if a == 1:
                        pe.wait_ge(sem("l1_bias_ready"), 1)
                    for u in range(H // 4 * NB):
                        quad, b = divmod(u, NB)
                        if u >= 2:
                            pe.wait_ge(*upto("max_ready", a, u - 1))
                        s = 4 * (u % 2)
                        bias = {0: [], 1: [b1q[:, 0, 2 * b:2 * b + 2, :], b1q[:, 1, 2 * b:2 * b + 2, :]],
                                2: [l2_bias_q[:]]}[a]
                        for g in range(4):
                            for n, part in enumerate(bias):
                                pe.matmul(bank(s + g), ident_b[:], part.rearrange("p t k -> p (t k)"), start=n == 0,
                                          stop=False, skip_group_check=True)
                        for qt in range(2):
                            for g in range(4):
                                j, row = 2 * quad + g // 2, 64 * (g % 2)
                                at = b * S + qt * P
                                last = pe.matmul(bank(s + g)[:, qt * S:(qt + 1) * S],
                                                 qS[row:row + KS, j, at:at + P],
                                                 kS[row:row + KS, j, b * S:(b + 1) * S],
                                                 start=not bias, stop=True, skip_group_check=bool(bias))
                        last.then_inc(sem("s1"), 1)
                    pe.wait_ge(*upto("max_parts", a, 1))
                    nb = ps[0:2 * H, 0, :].bitcast(bf16)
                    for t in range(NT):
                        last = pe.transpose(nb[:, t * P:(t + 1) * P], nmp[:, t].rearrange("p n h -> p (n h)"),
                                            ident_b[:])
                    last.then_inc(sem("max_T"), 1)

                    def values(v):
                        j, b = divmod(v, NB)
                        pe.wait_ge(*upto("p_low", a, v + 1))
                        if v == 0:
                            pe.wait_ge(*upto("v_ready", a, 1))
                        for hh_ in range(HP):
                            h = HP * j + hh_
                            for qt in range(2):
                                for kt in range(2):
                                    at = hh_ * 2 * S + kt * S + qt * P
                                    for n, part in enumerate((pH, pL)):
                                        last = pe.matmul(bank(4 + 2 * b + qt)[:, h * VW:(h + 1) * VW],
                                                         part[:, v % 3, at:at + P],
                                                         vE[:, 2 * b + kt, h].rearrange("p n d -> p (n d)"),
                                                         start=kt + n == 0, stop=kt + n == 2)
                        last.then_inc(sem("pv"), 1)

                    pe.wait_ge(*upto("nmT", a, 1))
                    for v in range(2 * NK):
                        j, b = divmod(v, NB)
                        if v >= 2:
                            pe.wait_ge(*upto("p_ready", a, v - 1))
                        s = 2 * (v % 2)
                        bias = {0: [], 1: [b1k[:, n, 2 * b:2 * b + 2, :] for n in range(3)],
                                2: [l2_bias_k[:]]}[a]
                        for hh_ in range(HP):
                            shift = nmT[:, b * S:(b + 1) * S].unsqueeze(1).to_broadcast([2 * H, 2, S])
                            pe.matmul(bank(s + hh_).rearrange("p (t k) -> p t k", t=2),
                                      W["sel_m"][:, HP * j + hh_:HP * j + hh_ + 1].to_broadcast([2 * H, P]), shift, start=True,
                                      stop=False, skip_group_check=True)
                            for part in bias:
                                pe.matmul(bank(s + hh_), ident_b[:], part.rearrange("p t k -> p (t k)"), start=False,
                                          stop=False, skip_group_check=True)
                        for kt in range(2):
                            for hh_ in range(HP):
                                row, at = 64 * hh_, b * S + kt * P
                                last = pe.matmul(bank(s + hh_)[:, kt * S:(kt + 1) * S],
                                                 kS[row:row + KS, j, at:at + P],
                                                 qS[row:row + KS, j, b * S:(b + 1) * S],
                                                 start=False, stop=True, skip_group_check=True)
                        last.then_inc(sem("s2"), 1)
                        if v >= 2:
                            values(v - 2)
                    values(2 * NK - 2)
                    values(2 * NK - 1)
                    if a:
                        pe.wait_ge(*upto("att_ready", a, 1))
                        for t in range(NT):
                            last = pe.transpose(bank(0)[:, t * P:(t + 1) * P], att[:, t, :], W["ident"][:])
                        last.then_inc(sem("attT_ps"), 1)
                        pe.wait_ge(*upto("attT", a, 1))
                        for t in range(NT):
                            last = pe.matmul(bank(1)[:, t * P:(t + 1) * P], attT[:, t * P:(t + 1) * P],
                                             W[L + "wo"][:], start=True, stop=True)
                        last.then_inc(sem("o_ps"), 1)

                keys_values(0)
                for j in range(NK):
                    key_stack(0, j)
                attention(0)

                pe.wait_ge(sem("x_done"), 1)
                keys_values(1)
                norm_T(1)
                pe.wait_ge(sem("xT_ready"), n_T(1))

                def f0_out(e):
                    pe.wait_ge(sem("f0_h"), NC0 * (e + 1))
                    if e >= 2:
                        pe.wait_ge(sem("f0_out_read"), e - 1)
                    for t in range(NT):
                        for fc in range(NC0):
                            last = pe.matmul(bank(4 + e % 2)[:, t * P:(t + 1) * P],
                                             hT[:, e % 2, fc, t * P:(t + 1) * P], W["l0_wo"][:, e, fc, :],
                                             start=fc == 0, stop=fc == NC0 - 1)
                    last.then_inc(sem("f0_out"), 1)

                for e in range(E0 + 1):
                    for fc in range(NC0):
                        n = NC0 * e + fc
                        if n >= 4:
                            pe.wait_ge(sem("f0_act"), n - 3)
                        pe.matmul(bank(n % 4), W["l0_wi"][:, e, fc * P:(fc + 1) * P], xT[:], start=True, stop=True)\
                          .then_inc(sem("f0_in"), 1)
                    if e >= 1:
                        f0_out(e - 1)
                        key_stack(1, e - 1)
                f0_out(E0)
                pe.wait_ge(*upto("ks_act", 1, NK // 2))
                pe.wait_ge(*upto("ks_dve", 1, NK // 2))
                pe.wait_ge(sem("f0_gate"), 1)
                for t in range(NT):
                    last = pe.transpose(ps[0:8, 7, t * P:(t + 1) * P], gw[:, t, :], W["ident"][:])
                last.then_inc(sem("f0_gT_ps"), 1)
                pe.wait_ge(sem("f0_gT"), 1)
                for t in range(NT):
                    last = pe.matmul(bank(6)[:, t * P:(t + 1) * P], gT[:, t * P:(t + 1) * P], l0_exp_bo[:],
                                     start=True, stop=True)
                last.then_inc(sem("f0_b"), 1)

                attention(1)

                pe.wait_ge(sem("x_done"), 3)
                keys_values(2)
                pe.wait_ge(sem("f1_qx"), 1)
                xb = bank(0).bitcast(bf16)
                for t in range(NT):
                    last = pe.transpose(xb[:, t * P:(t + 1) * P], qx[:, t, :], ident_b[:])
                last.then_inc(sem("f1_qxT_ps"), 1)
                pe.wait_ge(sem("f1_qxT"), 1)
                for t in range(NT):
                    pe.matmul(bank(1 + t), qxT[:, t * P:(t + 1) * P], w1q[:], start=True, stop=True)\
                      .then_inc(sem("f1_h_ps"), 1)
                for j in range(NK):
                    key_stack(2, j)
                pe.wait_ge(sem("f1_qh"), 1)
                for t in range(NT):
                    hb = bank(1 + t).bitcast(bf16)
                    for fc in range(NC0):
                        last = pe.transpose(hb[:, fc * P:(fc + 1) * P], qh[:, t, fc * P:(fc + 1) * P], ident_b[:])
                    last.then_inc(sem("f1_qhT_ps"), 1)
                for t in range(NT):
                    pe.wait_ge(sem("f1_qhT"), t + 1)
                    for fc in range(NC0):
                        last = pe.matmul(bank(0)[:, t * P:(t + 1) * P], qhT[:, t, fc, :],
                                         w2q[:, fc * P:(fc + 1) * P], start=fc == 0, stop=fc == NC0 - 1)
                last.then_inc(sem("f1_o_ps"), 1)

                attention(2)

                norm_T(5)
                pe.wait_ge(sem("xT_ready"), n_T(5))
                pe.wait_ge(sem("x_done"), 5)
                for t in range(NT):
                    last = pe.matmul(bank(7)[:, t * 8:(t + 1) * 8], xT[:, t * P:(t + 1) * P], W["l2_wg"][:],
                                     start=True, stop=True)
                last.then_inc(sem("f2_lg"), 1)

                def f2_out(e):
                    pe.wait_ge(sem("f2_g"), NH2 * (e + 1))
                    if e >= 2:
                        pe.wait_ge(sem("f2_out_read"), e - 1)
                    for t in range(NT):
                        for hc in range(NH2):
                            last = pe.matmul(bank(4 + e % 2)[:, t * P:(t + 1) * P],
                                             hT[:, e % 2, hc, t * P:(t + 1) * P], W["l2_w2"][:, e, hc, :],
                                             start=hc == 0, stop=hc == NH2 - 1)
                    last.then_inc(sem("f2_out"), 1)

                for e in range(E2):
                    for hc in range(NH2):
                        n = NH2 * e + hc
                        if n >= 2:
                            pe.wait_ge(sem("f2_g"), n - 1)
                        s = 2 * (n % 2)
                        pe.matmul(bank(s), W["l2_w1"][:, e, hc * P:(hc + 1) * P], xT[:], start=True, stop=True)\
                          .then_inc(sem("f2_h1"), 1)
                        pe.matmul(bank(s + 1), W["l2_w3"][:, e, hc * P:(hc + 1) * P], xT[:], start=True, stop=True)\
                          .then_inc(sem("f2_h3"), 1)
                    if e >= 1:
                        f2_out(e - 1)
                f2_out(E2 - 1)
                pe.wait_ge(sem("f2_gate"), 1)
                for t in range(NT):
                    last = pe.transpose(ps[0:8, 7, t * P:(t + 1) * P], gw[:, t, :], W["ident"][:])
                last.then_inc(sem("f2_gT_ps"), 1)
                pe.wait_ge(sem("f2_gT"), 1)
                for t in range(NT):
                    last = pe.matmul(bank(6)[:, t * P:(t + 1) * P], gT[:, t * P:(t + 1) * P], W["l2_bias2"][:], start=True, stop=True)
                last.then_inc(sem("f2_b"), 1)

                pe.wait_ge(sem("x_done"), 6)
                pe.matmul(ps[0:DK3, 1, :], W["l3_wi"][:], cT[:], start=True, stop=True).then_inc(sem("l3_k_ps"), 1)
                for t in range(NT):
                    last = pe.matmul(bank(2)[:, t * DK3:(t + 1) * DK3], cT[:, t * P:(t + 1) * P], W["l3_wi"][:],
                                     start=True, stop=True)
                last.then_inc(sem("l3_v_ps"), 1)
                norm_T(6)
                pe.wait_ge(sem("xT_ready"), n_T(6))
                pe.matmul(ps[0:DK3, 3, :], W["l3_wi"][:], xT[:], start=True, stop=True).then_inc(sem("l3_q_ps"), 1)
                pe.wait_ge(sem("l3_k"), 1)
                pe.wait_ge(sem("l3_q"), 1)
                for t in range(NT):
                    b = t // 2
                    last = pe.matmul(bank(4 + b)[:, (t % 2) * S:(t % 2 + 1) * S], attT[0:DK3, t * P:(t + 1) * P],
                                     GT[0:DK3, b * S:(b + 1) * S], start=True, stop=True)
                last.then_inc(sem("l3_s"), 1)
                pe.wait_ge(sem("l3_p"), 1)
                for kt in range(2):
                    for t in range(NT):
                        last = pe.transpose(bank(6 + kt)[:, t * P:(t + 1) * P],
                                            pT[:, 0, t * S + kt * P:t * S + kt * P + P], W["ident"][:])
                    last.then_inc(sem("l3_pT_ps"), 1)
                pe.wait_ge(sem("l3_pT_act"), 1)
                pe.wait_ge(sem("l3_pT_dve"), 1)
                for b in range(NB):
                    for kt in range(2):
                        last = pe.matmul(ps[0:DK3, 1, b * S:(b + 1) * S], y[:, 2 * b + kt, 0:DK3],
                                         pT[:, 1, kt * T + b * S:kt * T + (b + 1) * S], start=kt == 0, stop=kt == 1)
                last.then_inc(sem("l3_head_ps"), 1)
                pe.wait_ge(sem("l3_head"), 1)
                for t in range(NT):
                    last = pe.matmul(bank(2)[:, t * P:(t + 1) * P], lg[0:DK3, t * P:(t + 1) * P], wo3[:],
                                     start=True, stop=True)
                last.then_inc(sem("l3_o_ps"), 1)

                norm_T(7)
                pe.wait_ge(sem("xT_ready"), n_T(7))
                pe.wait_ge(sem("x_done"), 7)
                pe.matmul(bank(1), W["l3_wm"][:], xT[:], start=True, stop=True).then_inc(sem("f3_h_ps"), 1)
                pe.wait_ge(sem("f3_h"), 1)
                for t in range(NT):
                    last = pe.matmul(bank(3)[:, t * P:(t + 1) * P], qf[:, t * P:(t + 1) * P], W["l3_emb"][:],
                                     start=True, stop=True)
                last.then_inc(sem("f3_lg"), 1)
                pe.wait_ge(sem("f3_hp"), 1)
                for h in range(H3):
                    if h >= 4:
                        pe.wait_ge(sem(("f3_hs_act", "f3_hs_dve")[h % 2]), h // 2 - 1)
                    for n in range(3):
                        last = pe.matmul(ps[0:KS3, 4 + h % 4, :], W["sel_h"][:, n, h, :], qp[:, n, :],
                                         start=n == 0, stop=n == 2)
                    last.then_inc(sem("f3_hs_ps"), 1)
                pe.wait_ge(sem("f3_hs_act"), H3 // 2)
                pe.wait_ge(sem("f3_hs_dve"), H3 // 2)

                def f3_out(n):
                    h, ep = divmod(n, NEP)
                    pe.wait_ge(sem("f3_mid"), n + 1)
                    if ep == 0 and h >= 2:
                        pe.wait_ge(sem("f3_gated"), h - 1)
                    for t in range(NT):
                        col = (t % 2) * E3 * HD3 + ep * 32
                        last = pe.matmul(ps[:, 4 + 2 * (h % 2) + t // 2, col:col + 32],
                                         hT[:, 0, n % 4, t * P:(t + 1) * P], W["l3_w2"][:, ep, :],
                                         start=True, stop=True)
                    last.then_inc(sem("f3_out"), 1)

                for n in range(H3 * NEP):
                    h, ep = divmod(n, NEP)
                    if n >= 3:
                        pe.wait_ge(sem("f3_mid"), n - 2)
                    pe.matmul(bank(n % 3), w1s[:, ep * P:(ep + 1) * P], qS[0:KS3, h, :], start=True, stop=True)\
                      .then_inc(sem("f3_in"), 1)
                    if n >= 2:
                        f3_out(n - 2)
                    if n == 3 * NEP:
                        pe.wait_ge(sem("f3_gate"), 1)
                        for t in range(NT):
                            last = pe.transpose(bank(3)[:, t * P:(t + 1) * P],
                                                gates[:, 8 * t:8 * t + 8, :].rearrange("p h e -> p (h e)"),
                                                W["ident"][:])
                        last.then_inc(sem("f3_gT_ps"), 1)
                    if n == 4 * NEP:
                        pe.wait_ge(sem("f3_gT"), 1)
                        for t in range(NT):
                            last = pe.matmul(bank(3)[:, t * P:(t + 1) * P], GT[:, t * P:(t + 1) * P],
                                             W["l3_b2"][:], start=True, stop=True)
                        last.then_inc(sem("f3_b"), 1)
                f3_out(H3 * NEP - 2)
                f3_out(H3 * NEP - 1)
                pe.wait_ge(sem("f3_comb"), 1)
                for t in range(NT):
                    last = pe.transpose(bank(0)[:, t * P:(t + 1) * P], acc[:, t, :], W["ident"][:])
                last.then_inc(sem("f3_cT_ps"), 1)
                pe.wait_ge(sem("f3_cT"), 1)
                for t in range(NT):
                    last = pe.matmul(bank(1)[:, t * P:(t + 1) * P], attT[:, t * P:(t + 1) * P], W["l3_fo"][:],
                                     start=True, stop=True)
                last.then_inc(sem("f3_o_ps"), 1)
                end_turn(pe, "pe")

        @block.scalar
        def _(act):
            act.wait_ge(sem("weights_loaded"), 16 * N_WEIGHTS)
            act.activation(tg[:], W["g"][:], ACT.Tanh).then_inc(sem("tg_ready"), 1)
            act.activation(ident_b[:], W["ident"][:], ACT.Copy)
            end_turn(act, "act")

            with act.Fori(0, turns):
                act.wait_ge(sem("cT_ps"), 1)
                act.activation(cT[:], bank(3), ACT.Copy).then_inc(sem("cT_ready"), 1)

                def norm_T(n):
                    act.wait_ge(sem("xT_ps"), n_T(n))
                    act.activation(xT[:], bank(0), ACT.Copy).then_inc(sem("xT_ready"), 1)

                def keys(a):
                    L = f"l{a}_"
                    act.wait_ge(*upto("k_ps", a, 1))
                    if a == 1:
                        ins = act.activation(kf[:], bank(6), ACT.Identity, bias=W["l1_bk"][:])
                    else:
                        ins = act.activation(kf[:], bank(6), ACT.Copy if a else ACT.Relu)
                    ins.then_inc(sem("kf"), 1)

                def key_stack(a, j):
                    L = f"l{a}_"
                    act.wait_ge(*upto("ks_ps", a, j + 1))
                    act.activation(kS[:, j, :], bank(6 + j % 2), ACT.Copy).then_inc(sem("ks_act"), 1)

                def attention(a):
                    L = f"l{a}_"
                    norm_T(LN_OF_ATT[a])
                    act.wait_ge(*upto("q_ps", a, 1))
                    if a == 1:
                        ins = act.activation(qf[:], bank(1), ACT.Identity, bias=q_bias[:], scale=SC)
                    else:
                        ins = act.activation(qf[:], bank(1), ACT.Copy if a else ACT.Relu, scale=SC)
                    ins.then_inc(sem("qf"), 1)
                    for j in range(0, NK, 2):
                        act.wait_ge(*upto("qs_ps", a, j + 1))
                        act.activation(qS[:, j, :], bank(2 + j % 4), ACT.Copy).then_inc(sem("qs_act"), 1)
                    act.wait_ge(*upto("max_T", a, 1))
                    act.activation(nmT[:], ps[0:2 * H, 0, :].bitcast(bf16)[:, 0:T], ACT.Copy)\
                       .then_inc(sem("nmT"), 1)
                    for v in range(2 * NK):
                        act.wait_ge(*upto("s2", a, v + 1))
                        if v >= 3:
                            act.wait_ge(*upto("p_low", a, v - 2))
                        scores = ps[:, 2 * (v % 2):2 * (v % 2) + 2, :].rearrange("p n k -> p (n k)")
                        if HIGH_BY_ACT(v):
                            if v >= 3:
                                act.wait_ge(*upto("pv", a, v - 2))
                            act.activation(pH[:, v % 3, :], scores, ACT.Exp)
                        act.activation(pT[:, v % 3, :], scores, ACT.Exp).then_inc(sem("p_ready"), 1)
                    if a:
                        act.wait_ge(*upto("attT_ps", a, 1))
                        act.activation(attT[:], bank(0), ACT.Copy).then_inc(sem("attT"), 1)

                keys(0)
                for j in range(0, NK, 2):
                    key_stack(0, j)
                attention(0)

                keys(1)
                norm_T(1)
                for n in range(NC0 * (E0 + 1)):
                    act.wait_ge(sem("f0_in"), n + 1)
                    if n >= 4:
                        act.wait_ge(sem("f0_h"), n - 3)
                    act.activation(ex[:, n % 4, :], bank(n % 4), ACT.Exp, bias=l0_exp_bias[:, n:n + 1])
                    act.activation(rl[:, n % 4, :], bank(n % 4), ACT.Relu, bias=W["l0_bi"][:, n:n + 1])\
                       .then_inc(sem("f0_act"), 1)
                    e, fc = divmod(n, NC0)
                    if fc == 0 and e >= 2 and e % 2 == 0:
                        key_stack(1, e - 2)
                act.wait_ge(sem("f0_gT_ps"), 1)
                act.activation(gT, ps[0:8, 7, :], ACT.Copy).then_inc(sem("f0_gT"), 1)

                attention(1)

                keys(2)
                act.wait_ge(sem("f1_qxT_ps"), 1)
                act.activation(qxT, bank(0).bitcast(bf16)[:, 0:T], ACT.Copy).then_inc(sem("f1_qxT"), 1)
                for j in range(0, NK, 2):
                    key_stack(2, j)
                for t in range(NT):
                    act.wait_ge(sem("f1_y"), t + 1)
                    act.activation(hh[:, t, :], hT[:, 0, t, :], ACT.Gelu).then_inc(sem("f1_gelu"), 1)
                    act.wait_ge(sem("f1_gelu"), t + 1)
                    act.activation(hT[:, 1, t, :], hh[:, t, :], ACT.Square, accum_out=cols[:, 0, t:t + 1])\
                       .then_inc(sem("f1_sq"), 1)
                for t in range(NT):
                    act.wait_ge(sem("f1_qhT_ps"), t + 1)
                    act.activation(qhT[:, t].rearrange("p c k -> p (c k)"), bank(1 + t).bitcast(bf16)[:, 0:F0],
                                   ACT.Copy).then_inc(sem("f1_qhT"), 1)

                attention(2)

                norm_T(5)
                act.wait_ge(sem("f2_gap"), 1)
                act.activation(tw[:, :, 1], tws[:], ACT.Exp).then_inc(sem("f2_gap_exp"), 1)
                for n in range(NH2 * E2):
                    act.wait_ge(sem("f2_h1"), n + 1)
                    if n >= 2:
                        act.wait_ge(sem("f2_g"), n - 1)
                    act.activation(ex[:, n % 2, :], bank(2 * (n % 2)), ACT.Silu, bias=W["l2_bias1"][:, n:n + 1]).then_inc(sem("f2_silu"), 1)
                act.wait_ge(sem("f2_gT_ps"), 1)
                act.activation(gT, ps[0:8, 7, :], ACT.Copy).then_inc(sem("f2_gT"), 1)

                act.wait_ge(sem("l3_k_ps"), 1)
                act.activation(GT[0:DK3, :], ps[0:DK3, 1, :], ACT.Copy, scale=DK3 ** -0.5).then_inc(sem("l3_k"), 1)
                norm_T(6)
                act.wait_ge(sem("l3_q_ps"), 1)
                act.activation(attT[0:DK3, :], ps[0:DK3, 3, :], ACT.Copy).then_inc(sem("l3_q"), 1)
                act.wait_ge(sem("l3_max"), 1)
                for t in range(NT):
                    act.activation(ex[:, t // 2, (t % 2) * S:(t % 2 + 1) * S],
                                   bank(4 + t // 2)[:, (t % 2) * S:(t % 2 + 1) * S], ACT.Exp,
                                   bias=cols[:, 0, t:t + 1], accum_out=cols[:, 1, t:t + 1])\
                       .then_inc(sem("l3_exp"), 1)
                act.wait_ge(sem("l3_pT_ps"), 1)
                act.activation(pT[:, 1, 0:T], bank(6), ACT.Copy).then_inc(sem("l3_pT_act"), 1)

                norm_T(7)
                act.wait_ge(sem("f3_h_ps"), 1)
                act.activation(qf[:], bank(1), ACT.Identity, bias=W["l3_bm"][:]).then_inc(sem("f3_h"), 1)
                for h in range(0, H3, 2):
                    act.wait_ge(sem("f3_hs_ps"), h + 1)
                    act.activation(qS[0:KS3, h, :], ps[0:KS3, 4 + h % 4, :], ACT.Copy).then_inc(sem("f3_hs_act"), 1)
                act.wait_ge(sem("f3_lgm"), 1)
                act.activation(gates[:].rearrange("p h e -> p (h e)"), rl[:, 0, :], ACT.Exp).then_inc(sem("f3_exp"), 1)
                for n in range(H3 * NEP):
                    act.wait_ge(sem("f3_in"), n + 1)
                    if n >= 4:
                        act.wait_ge(sem("f3_out"), n - 3)
                    act.activation(hT[:, 0, n % 4, :], bank(n % 3), ACT.Gelu,
                                   bias=W["l3_b1"][:, n % NEP:n % NEP + 1]).then_inc(sem("f3_mid"), 1)
                    if n == 3 * NEP + 4:
                        act.wait_ge(sem("f3_gT_ps"), 1)
                        act.activation(GT, bank(3), ACT.Copy).then_inc(sem("f3_gT"), 1)
                act.wait_ge(sem("f3_cT_ps"), 1)
                act.activation(attT[:], bank(0), ACT.Copy).then_inc(sem("f3_cT"), 1)
                end_turn(act, "act")

        @block.vector
        def _(dve):
            step = Chain(dve, sem("dve_step"))
            dve.wait_ge(sem("weights_loaded"), 16 * N_WEIGHTS)
            for n, name in enumerate(("l1_w1", "l1_w2")):
                step(dve.tensor_reduce(wsum[:, n:n + 1], W[name], AX.X, ALU.add, apply_absolute_value=True))
            dve.engine_nop().then_inc(sem("wsum_ready"), 1)
            dve.tensor_scalar(l0_exp_bias[:], W["l0_bi"][:], math.log(ALPHA), None, ALU.add)
            dve.tensor_scalar(q_bias[:], W["l1_bq"][:], SC, None, ALU.mult)
            w = W["l3_w1"]
            step(dve.tensor_copy(w1s[:], w))
            step(dve.scalar_tensor_tensor(w, w1s[:], W["less"][0:KS3, 0:1], w, ALU.mult, ALU.add))
            step(dve.tensor_copy(w1s[:], w))
            step(dve.scalar_tensor_tensor(w, w1s[:], W["less"][0:KS3, 1:2], w, ALU.mult, ALU.add))
            dve.tensor_copy(w1s[:], w)
            dve.tensor_reduce(wo3[:], W["l3_wo"].rearrange("p n d -> p d n"), AX.X, ALU.add)
            for m, name in enumerate(("l2_w1", "l2_w3")):
                dve.wait_ge(sem("lora"), m + 1)
                w = W[name][:].rearrange("p e h -> p (e h)")
                dve.tensor_tensor(w, w, ps[:, 4 * m:4 * m + 4, :].rearrange("p n k -> p (n k)"), ALU.add)\
                   .then_inc(sem("merged"), 1)
            dve.wait_ge(sem("lora"), 3)
            w = W["l2_w2"][:].rearrange("p e c d -> p (e c d)")
            dve.tensor_tensor(w, w, ps[:, 0:4, :].rearrange("p n k -> p (n k)"), ALU.add)
            dve.wait_ge(sem("colsum"), 1)
            dve.scalar_tensor_tensor(l0_gate_bo[:], bank(4, P), -LAMBDA * ALPHA, W["l0_gbo"][:], ALU.mult, ALU.add)
            dve.scalar_tensor_tensor(l0_exp_bo[:], ps[0:E0, 5, 0:P], -LAMBDA * ALPHA, W["l0_ebo"][:],
                                     ALU.mult, ALU.add)
            dve.wait_ge(sem("wabs"), 1)
            step(dve.tensor_scalar(wmean[:], bank(6, 2), 1.0 / (D * F0), 1e-5, ALU.mult, ALU.max))
            step(dve.reciprocal(wscale[:], wmean[:]))
            for n, (name, dst) in enumerate((("l1_w1", w1q), ("l1_w2", w2q))):
                step(dve.tensor_scalar(W[name], W[name], wscale[:, n:n + 1], -1.0, ALU.mult, ALU.max))
                step(dve.tensor_scalar(W[name], W[name], 1.0, MAGIC, ALU.min, ALU.add))
                step(dve.tensor_scalar(dst[:], W[name], -MAGIC, None, ALU.add))
            dve.wait_ge(sem("tg_ready"), 1)
            dve.tensor_scalar(tgl[:], tg[:, 4:5], LAMBDA, None, ALU.mult)
            end_turn(dve, "dve")

            with dve.Fori(0, turns):
                step = Chain(dve, sem("dve_step"))
                roots = [0]

                def root():
                    roots[0] += 1
                    dve.wait_ge(sem("rstd_ready"), roots[0])

                def layernorm():
                    for t in range(NT):
                        ins = dve.bn_stats(stats[:, t, :], x[:, t, :])
                    step(ins)
                    for t in range(NT):
                        ins = dve.bn_aggr(mv[:, t, :], stats[:, t, :])
                    step(ins)
                    dve.tensor_copy(vare[:], mv[:, :, 1]).then_inc(sem("var_ready"), 1)
                    root()
                    for t in range(NT):
                        ins = dve.tensor_scalar(xn[:, t, :], x[:, t, :], mv[:, t, 0:1], rstd[:, t:t + 1],
                                                ALU.subtract, ALU.mult)
                    ins.then_inc(sem("xn_ready"), 1)

                def add_projected(banks_, bias, n, gate):
                    step(dve.tensor_tensor(y[:], banks_.rearrange("p (t d) -> p t d", t=NT),
                                           bias[:].unsqueeze(1).to_broadcast([P, NT, D]), ALU.add))
                    dve.scalar_tensor_tensor(x[:], y[:], tg[:, gate:gate + 1], x[:], ALU.mult, ALU.add)\
                       .then_inc(sem("x_done"), 1)
                    dve.wait_ge(sem("x_done"), n)

                def values(a):
                    L = f"l{a}_"
                    dve.wait_ge(*upto("v_ps", a, 1))
                    src = bank(7).rearrange("p (t d) -> p t d", t=NT)
                    if a == 0:
                        ins = dve.tensor_scalar(vf[:], src, 0.0, None, ALU.max)
                    elif a == 1:
                        ins = dve.tensor_tensor(vf[:], src, W["l1_bv"][:].unsqueeze(1).to_broadcast([P, NT, D]), ALU.add)
                    else:
                        ins = dve.tensor_copy(vf[:], src)
                    ins.then_inc(sem("vf"), 1)

                def key_stack(a, j):
                    L = f"l{a}_"
                    dve.wait_ge(*upto("ks_ps", a, j + 1))
                    dve.tensor_copy(kS[:, j, :], bank(6 + j % 2)).then_inc(sem("ks_dve"), 1)

                def split(src):
                    step(dve.tensor_copy(qp[:, 0, :], src))
                    step(dve.tensor_tensor(lg, src, qp[:, 0, :], ALU.subtract))
                    step(dve.tensor_copy(qp[:, 1, :], lg))
                    return dve.tensor_tensor(qp[:, 2, :], lg, qp[:, 1, :], ALU.subtract)

                def attention(a):
                    L = f"l{a}_"
                    dve.wait_ge(*upto("qf", a, 1))
                    split(qf[:]).then_inc(sem("qp"), 1)
                    for j in range(1, NK, 2):
                        dve.wait_ge(*upto("qs_ps", a, j + 1))
                        dve.tensor_copy(qS[:, j, :], bank(2 + j % 4)).then_inc(sem("qs_dve"), 1)
                    for u in range(H // 4 * NB):
                        quad, b = divmod(u, NB)
                        dve.wait_ge(*upto("s1", a, u + 1))
                        s = 4 * (u % 2)
                        dve.tensor_reduce(nm[:, 2 * b:2 * b + 2, 4 * quad:4 * quad + 4].rearrange("p t g -> p g t"),
                                          ps[:, s:s + 4, :].rearrange("p g (t k) -> p g t k", t=2),
                                          AX.X, ALU.max, negate=True).then_inc(sem("max_ready"), 1)
                    dve.wait_ge(*upto("max_ready", a, H // 4 * NB))
                    step(dve.tensor_scalar(nmp[:, :, 0, :], nm[:], CAP, None, ALU.min))
                    dve.scalar_tensor_tensor(nmp[:, :, 1, :], nm[:], CAP, nmp[:, :, 0, :], ALU.min, ALU.subtract)\
                       .then_inc(sem("max_parts"), 1)
                    for v in range(2 * NK):
                        dve.wait_ge(*upto("p_ready", a, v + 1))
                        if v >= 3:
                            dve.wait_ge(*upto("pv", a, v - 2))
                        if not HIGH_BY_ACT(v):
                            step(dve.tensor_copy(pH[:, v % 3, :], pT[:, v % 3, :]))
                        dve.tensor_tensor(pL[:, v % 3, :], pT[:, v % 3, :], pH[:, v % 3, :], ALU.subtract)\
                           .then_inc(sem("p_low"), 1)
                    dve.wait_ge(*upto("pv", a, 2 * NK))
                    for t in range(NT):
                        ins = dve.tensor_reduce(osum[:, t], ps[:, 4 + t, 0:H * VW].rearrange("p (h n d) -> p h d n", h=H, n=3),
                                                AX.X, ALU.add)
                    step(ins)
                    step(dve.reciprocal(rc[:], osum[:, :, :, DH]))
                    ins = dve.tensor_tensor(att[:].rearrange("p t (h d) -> p (t h) d", h=H),
                                            osum[:, :, :, 0:DH].rearrange("p t h d -> p (t h) d"),
                                            rc[:].rearrange("p t h -> p (t h)").unsqueeze(2).to_broadcast([P, NT * H, DH]), ALU.mult)
                    if a == 0:
                        step(ins)
                        dve.scalar_tensor_tensor(x[:], att[:], tg[:, 0:1], x[:], ALU.mult, ALU.add)\
                           .then_inc(sem("x_done"), 1)
                        dve.wait_ge(sem("x_done"), 1)
                    else:
                        ins.then_inc(sem("att_ready"), 1)
                        dve.wait_ge(*upto("o_ps", a, 1))
                        add_projected(bank(1), W[L + "bo"], 2 * a + 1, a)

                def top2(src, n):
                    for r in range(n):
                        ins = dve.max(mx8[:, r, :], src[:, r, :])
                    step(ins)
                    for r in range(n):
                        ins = dve.max_index(ix8[:, r, :], mx8[:, r, :], src[:, r, :])
                    step(ins)
                    step(dve.tensor_copy(ixf[:, 0:n, :], ix8[:, 0:n, 0:2]))

                def expert_weights(done):
                    for k in range(2):
                        dve.tensor_tensor(oh[:, k], W["iota"][:, 0:8].unsqueeze(1).to_broadcast([P, NT, 8]),
                                          ixf[:, 0:NT, k].unsqueeze(2).to_broadcast([P, NT, 8]), ALU.is_equal)\
                           .then_inc(sem("dve_step"), 1)
                    step.n += 2
                    dve.wait_ge(step.sem, step.n)
                    for k in range(2):
                        ins = dve.tensor_tensor(oh[:, k], oh[:, k], tw[:, :, k].unsqueeze(2).to_broadcast([P, NT, 8]),
                                                ALU.mult)
                    step(ins)
                    dve.tensor_tensor(gw[:], oh[:, 0], oh[:, 1], ALU.add).then_inc(sem(done), 1)

                def expert_sum(read, n):
                    for t in range(NT):
                        src = bank(4 + (n[0]) % 2)[:, t * P:(t + 1) * P]
                        if n[1] == 0:
                            ins = dve.tensor_scalar(acc[:, t, :], src, gw[:, t, n[1]:n[1] + 1], None, ALU.mult)
                        else:
                            ins = dve.scalar_tensor_tensor(acc[:, t, :], src, gw[:, t, n[1]:n[1] + 1],
                                                           acc[:, t, :], ALU.mult, ALU.add)
                    ins.then_inc(sem(read), 1)

                def quantise(src, dst, F, n):
                    step(dve.tensor_scalar(vare[:], cols[:, 0, :], 1.0 / F, None, ALU.mult))
                    dve.engine_nop().then_inc(sem("var_ready"), 1)
                    root()
                    step(dve.tensor_tensor(cols[:, 2, :], cols[:, 1, :], rstd[:], ALU.mult))
                    step(dve.tensor_scalar(cols[:, 3, :], cols[:, 2, :], 1e-5, None, ALU.max))
                    step(dve.reciprocal(cols[:, 4, :], cols[:, 3, :]))
                    step(dve.scalar_tensor_tensor(cols[:, 5, :], cols[:, 4, :], 127.0, rstd[:], ALU.mult, ALU.mult))
                    step(dve.tensor_scalar(cols[:, 6, :], cols[:, 3, :], wmean[:, n:n + 1], 1.0 / 127.0,
                                           ALU.mult, ALU.mult))
                    for t in range(NT):
                        ins = dve.tensor_scalar(src[:, t, :], src[:, t, :], cols[:, 5, t:t + 1], -128.0,
                                                ALU.mult, ALU.max)
                    step(ins)
                    step(dve.tensor_scalar(src, src, 127.0, MAGIC, ALU.min, ALU.add))
                    return dve.tensor_scalar(dst, src, -MAGIC, None, ALU.add)

                dve.wait_ge(sem("x_loaded"), 16)
                layernorm()
                values(0)
                for j in range(1, NK, 2):
                    key_stack(0, j)
                attention(0)

                values(1)
                layernorm()
                for e in range(E0 + 2):
                    if e <= E0:
                        for fc in range(NC0):
                            n = NC0 * e + fc
                            dve.wait_ge(sem("f0_act"), n + 1)
                            if e >= 2 and fc == 0:
                                dve.wait_ge(sem("f0_out"), e - 1)
                            dve.scalar_tensor_tensor(hT[:, e % 2, fc, :], ex[:, n % 4, :], ALPHA, rl[:, n % 4, :],
                                                     ALU.min, ALU.add).then_inc(sem("f0_h"), 1)
                    if e == 1:
                        dve.wait_ge(sem("f0_out"), 1)
                        lgv = lg.rearrange("p (t d) -> p t d", t=NT)
                        dve.scalar_tensor_tensor(lgv, bank(4).rearrange("p (t d) -> p t d", t=NT), LAMBDA,
                                                 l0_gate_bo[:].unsqueeze(1).to_broadcast([P, NT, D]),
                                                 ALU.mult, ALU.add).then_inc(sem("f0_out_read"), 1)
                        dve.wait_ge(sem("f0_out_read"), 1)
                        top2(lgv, NT)
                        step(dve.tensor_tensor(tws[:], mx8[:, 0:NT, 0], mx8[:, 0:NT, 1], ALU.add))
                        step(dve.reciprocal(tws[:], tws[:]))
                        step(dve.tensor_tensor(tw[:], mx8[:, 0:NT, 0:2], tws[:].unsqueeze(2).to_broadcast([P, NT, 2]),
                                               ALU.mult))
                        expert_weights("f0_gate")
                        dve.wait_ge(sem("f0_gate"), 1)
                    if e >= 2 and e % 2 == 1:
                        key_stack(1, e - 2)
                    if e >= 2:
                        dve.wait_ge(sem("f0_out"), e)
                        if e >= 3:
                            dve.wait_ge(sem("f0_out_read"), e - 1)
                        expert_sum("f0_out_read", (e - 1, e - 2))
                dve.wait_ge(sem("f0_out_read"), E0 + 1)
                step(dve.scalar_tensor_tensor(x[:], acc[:], tgl[:], x[:], ALU.mult, ALU.add))
                dve.wait_ge(sem("f0_b"), 1)
                dve.scalar_tensor_tensor(x[:], bank(6).rearrange("p (t d) -> p t d", t=NT), tg[:, 4:5], x[:],
                                         ALU.mult, ALU.add).then_inc(sem("x_done"), 1)
                dve.wait_ge(sem("x_done"), 2)

                layernorm()
                attention(1)

                values(2)
                layernorm()
                dve.wait_ge(sem("xn_ready"), 4)
                step(dve.tensor_tensor(y[:], xn[:], xn[:], ALU.mult))
                dve.tensor_reduce(cols[:, 1, :], xn[:], AX.X, ALU.max, apply_absolute_value=True)
                step(dve.tensor_reduce(cols[:, 0, :], y[:], AX.X, ALU.add))
                quantise(xn[:], qx, D, 0).then_inc(sem("f1_qx"), 1)
                for t in range(NT):
                    dve.wait_ge(sem("f1_h_ps"), t + 1)
                    dve.scalar_tensor_tensor(hT[:, 0, t, :], bank(1 + t), cols[:, 6, t:t + 1], W["l1_b1"][:],
                                             ALU.mult, ALU.add).then_inc(sem("f1_y"), 1)
                for j in range(1, NK, 2):
                    key_stack(2, j)
                dve.wait_ge(sem("f1_gelu"), NT)
                dve.wait_ge(sem("f1_sq"), NT)
                step(dve.tensor_reduce(cols[:, 1, :], hh[:], AX.X, ALU.max, apply_absolute_value=True))
                quantise(hh[:], qh, F0, 1).then_inc(sem("f1_qh"), 1)
                dve.wait_ge(sem("f1_o_ps"), 1)
                for t in range(NT):
                    ins = dve.scalar_tensor_tensor(y[:, t, :], bank(0)[:, t * P:(t + 1) * P], cols[:, 6, t:t + 1],
                                                   W["l1_b2"][:], ALU.mult, ALU.add)
                step(ins)
                dve.scalar_tensor_tensor(x[:], y[:], tg[:, 5:6], x[:], ALU.mult, ALU.add)\
                   .then_inc(sem("x_done"), 1)
                dve.wait_ge(sem("x_done"), 4)

                layernorm()
                attention(2)

                layernorm()
                dve.wait_ge(sem("f2_lg"), 1)
                lgv = lg[:, 0:NT * 8].rearrange("p (t e) -> p t e", t=NT)
                step(dve.tensor_copy(lg[:, 0:NT * 8], bank(7, NT * 8)))
                top2(lgv, NT)
                dve.tensor_tensor(tws[:], mx8[:, 0:NT, 1], mx8[:, 0:NT, 0], ALU.subtract)\
                   .then_inc(sem("f2_gap"), 1)
                dve.wait_ge(sem("f2_gap_exp"), 1)
                step(dve.tensor_scalar(tws[:], tw[:, :, 1], 1.0, None, ALU.add))
                step(dve.reciprocal(tw[:, :, 0], tws[:]))
                step(dve.tensor_tensor(tw[:, :, 1], tw[:, :, 1], tw[:, :, 0], ALU.mult))
                expert_weights("f2_gate")
                dve.wait_ge(sem("f2_gate"), 1)
                for e in range(E2 + 1):
                    if e < E2:
                        for hc in range(NH2):
                            n = NH2 * e + hc
                            dve.wait_ge(sem("f2_silu"), n + 1)
                            dve.wait_ge(sem("f2_h3"), n + 1)
                            if e >= 2 and hc == 0:
                                dve.wait_ge(sem("f2_out"), e - 1)
                            dve.scalar_tensor_tensor(hT[:, e % 2, hc, :], bank(2 * (n % 2) + 1),
                                                     W["l2_bias3"][:, n:n + 1], ex[:, n % 2, :],
                                                     ALU.add, ALU.mult).then_inc(sem("f2_g"), 1)
                    if e >= 1:
                        dve.wait_ge(sem("f2_out"), e)
                        if e >= 2:
                            dve.wait_ge(sem("f2_out_read"), e - 1)
                        expert_sum("f2_out_read", (e - 1, e - 1))
                dve.wait_ge(sem("f2_out_read"), E2)
                step(dve.scalar_tensor_tensor(x[:], acc[:], tg[:, 6:7], x[:], ALU.mult, ALU.add))
                dve.wait_ge(sem("f2_b"), 1)
                dve.scalar_tensor_tensor(x[:], bank(6).rearrange("p (t d) -> p t d", t=NT), tg[:, 6:7], x[:],
                                         ALU.mult, ALU.add).then_inc(sem("x_done"), 1)
                dve.wait_ge(sem("x_done"), 6)

                layernorm()
                dve.wait_ge(sem("l3_v_ps"), 1)
                dve.tensor_copy(y[:, :, 0:DK3], bank(2, NT * DK3).rearrange("p (t d) -> p t d", t=NT))
                dve.wait_ge(sem("l3_s"), 1)
                dve.tensor_reduce(cols[:, 0, :].rearrange("p (b t) -> p b t", b=2),
                                  ps[:, 4:6, :].rearrange("p b (t k) -> p b t k", t=2),
                                  AX.X, ALU.max, negate=True).then_inc(sem("l3_max"), 1)
                dve.wait_ge(sem("l3_exp"), NT)
                step(dve.reciprocal(cols[:, 2, :], cols[:, 1, :]))
                for t in range(NT):
                    ins = dve.tensor_scalar(pT[:, 0, t * S:(t + 1) * S], ex[:, t // 2, (t % 2) * S:(t % 2 + 1) * S],
                                            cols[:, 2, t:t + 1], None, ALU.mult)
                ins.then_inc(sem("l3_p"), 1)
                dve.wait_ge(sem("l3_pT_ps"), 2)
                dve.tensor_copy(pT[:, 1, T:2 * T], bank(7)).then_inc(sem("l3_pT_dve"), 1)
                dve.wait_ge(sem("l3_head_ps"), 1)
                dve.tensor_tensor(lg[0:DK3, :], ps[0:DK3, 1, :], attT[0:DK3, :], ALU.add).then_inc(sem("l3_head"), 1)
                dve.wait_ge(sem("l3_o_ps"), 1)
                add_projected(bank(2), W["l3_bo"], 7, 3)

                layernorm()
                dve.wait_ge(sem("f3_h"), 1)
                split(qf[:]).then_inc(sem("f3_hp"), 1)
                for h in range(1, H3, 2):
                    dve.wait_ge(sem("f3_hs_ps"), h + 1)
                    dve.tensor_copy(qS[0:KS3, h, :], ps[0:KS3, 4 + h % 4, :]).then_inc(sem("f3_hs_dve"), 1)
                dve.wait_ge(sem("f3_lg"), 1)
                step(dve.tensor_copy(lg, bank(3)))
                lgv = lg.rearrange("p (r e) -> p r e", e=E3)
                for r in range(32):
                    ins = dve.max(mx8[:, r, :], lgv[:, r, :])
                step(ins)
                dve.tensor_tensor(rl[:, 0, :].rearrange("p (r e) -> p r e", e=E3), lgv,
                                  mx8[:, :, 0:1].to_broadcast([P, 32, E3]), ALU.subtract)\
                   .then_inc(sem("f3_lgm"), 1)
                for r in range(32):
                    ins = dve.max_index(ix8[:, r, :], mx8[:, r, :], lgv[:, r, :])
                step(ins)
                step(dve.tensor_copy(ixf[:], ix8[:, :, 0:2]))
                for k in range(2):
                    ins = dve.tensor_tensor(oh16[:, k], W["iota"][:].unsqueeze(1).to_broadcast([P, 32, E3]),
                                            ixf[:, :, k:k + 1].to_broadcast([P, 32, E3]), ALU.is_equal)
                step(ins)
                step(dve.tensor_tensor(oh16[:, 0], oh16[:, 0], oh16[:, 1], ALU.add))
                dve.wait_ge(sem("f3_exp"), 1)
                step(dve.tensor_reduce(gsum[:], gates[:], AX.X, ALU.add))
                step(dve.reciprocal(gsum[:], gsum[:]))
                step(dve.tensor_tensor(gates[:], gates[:], oh16[:, 0], ALU.mult))
                dve.tensor_tensor(gates[:], gates[:], gsum[:].unsqueeze(2).to_broadcast([P, 32, E3]), ALU.mult)\
                   .then_inc(sem("f3_gate"), 1)
                dve.wait_ge(sem("f3_gate"), 1)
                gv = gates[:].rearrange("p (t h) e -> p t h e", t=NT)
                for h in range(H3):
                    dve.wait_ge(sem("f3_out"), NEP * (h + 1))
                    eo = ps[:, 4 + 2 * (h % 2):6 + 2 * (h % 2), :].rearrange("p b k -> p (b k)")
                    dve.tensor_tensor(gated[:, h % 2].rearrange("p t (e o) -> p t e o", e=E3),
                                      eo.rearrange("p (t e o) -> p t e o", t=NT, e=E3),
                                      gv[:, :, h, :].unsqueeze(3).to_broadcast([P, NT, E3, HD3]), ALU.mult)\
                       .then_inc(sem("f3_gated"), 1)
                    dve.wait_ge(sem("f3_gated"), h + 1)
                    ins = dve.tensor_reduce(acc[:, :, h * HD3:(h + 1) * HD3],
                                            gated[:, h % 2].rearrange("p t (e o) -> p t o e", e=E3), AX.X, ALU.add)
                step(ins)
                dve.wait_ge(sem("f3_b"), 1)
                dve.tensor_tensor(acc[:], acc[:], bank(3).rearrange("p (t d) -> p t d", t=NT), ALU.add)\
                   .then_inc(sem("f3_comb"), 1)
                dve.wait_ge(sem("f3_o_ps"), 1)
                add_projected(bank(1), W["l3_fbo"], 8, 7)
                end_turn(dve, "dve")

        @block.sync
        def _(sp):
            for name in WEIGHTS:
                w = W[name]
                sp.dma_start(w if name in SETUP_ONLY else w[:], A[name] if WEIGHTS[name][1] != "b" else A[name].bitcast(bf16)).then_inc(
                    sem("weights_loaded"), 16)
            sp.wait_ge(sem("weights_loaded"), 16 * N_WEIGHTS)
            numbers = sorted(s.num for n, s in sems.items() if n not in kept)
            assert numbers[-1] - numbers[0] + 1 == len(numbers)

            def clear():
                sp.wait_ge(turn_end, 4)
                sp.sem_clear(turn_end)
                sp.sem_clear(range(numbers[0], numbers[-1] + 1))
                for e in GO:
                    sp.sem_inc(GO[e], 1)

            xv = A["x"].rearrange("(n p) d -> p n d", p=P)
            cv = A["ctx"].rearrange("(n p) d -> p n d", p=P)
            ov = out.rearrange("(n p) d -> p n d", p=P)
            mq = A["mask1_q"].rearrange("(n p) k -> p n k", p=P)
            mk = A["mask1_k"].rearrange("(n p) k -> p n k", p=P)
            clear()
            with sp.Fori(0, turns) as i:
                sp.dma_start(x[:], xv[:, bass.ds(i * NT, NT), :]).then_inc(sem("x_loaded"), 16)
                sp.dma_start(ctxs[:], cv[:, bass.ds(i * NT, NT), :]).then_inc(sem("ctx_loaded"), 16)
                sp.dma_start(m1[:], mq[:, bass.ds(i * NT, NT), :]).then_inc(sem("masks_loaded"), 16)
                sp.wait_ge(sem("mask_read"), 1)
                sp.wait_ge(sem("masks_loaded"), 16)
                sp.dma_start(m1[:], mk[:, bass.ds(i * NT, NT), :]).then_inc(sem("masks_loaded"), 16)
                sp.wait_ge(sem("x_done"), 8)
                sp.dma_start(ov[:, bass.ds(i * NT, NT), :], x[:]).then_inc(sem("out_stored"), 16)
                sp.wait_ge(sem("out_stored"), 16)
                clear()




def HIGH_BY_ACT(v):
    return v % 2 == 0


PER_ATTENTION = {
    "k_ps": 1, "kf": 1, "kp": 1, "ks_ps": NK, "ks_act": NK // 2, "ks_dve": NK // 2,
    "v_ps": 1, "vf": 1, "v_ready": 1,
    "q_ps": 1, "qf": 1, "qp": 1, "qs_ps": NK, "qs_act": NK // 2, "qs_dve": NK // 2,
    "s1": H // 4 * NB, "max_ready": H // 4 * NB, "max_parts": 1, "max_T": 1, "nmT": 1,
    "s2": 2 * NK, "p_ready": 2 * NK, "p_low": 2 * NK, "pv": 2 * NK,
    "att_ready": 1, "attT_ps": 1, "attT": 1, "o_ps": 1,
}
PROJECTED = ("att_ready", "attT_ps", "attT", "o_ps")
LN_OF_ATT = (0, 2, 4)


def n_T(n):
    return n + 1 - (n > 3)



BF16_ONE = 0x3F80

WEIGHTS = {
    "ident": ([P, P], "f"), "ones": ([P, P], "f"), "pick": ([P, E0, E0], "f"), "iota": ([P, E3], "f"),
    "less": ([P, 2], "f"), "g": ([P, 8], "f"),
    "sel_x": ([P, 3, NK, P], "b"), "sel_y": ([P, 3, NK, P], "b"), "sel_h": ([P, 3, H3, KS3], "b"),
    "sel_m": ([2 * H, H], "b"),
    "l0_wq": ([P, P], "f"), "l0_wk": ([P, P], "f"), "l0_wv": ([P, P], "f"),
    "l1_wq": ([P, P], "f"), "l1_wk": ([P, P], "f"), "l1_wv": ([P, P], "f"), "l1_wo": ([P, P], "f"),
    "l1_bq": ([P, 1], "f"), "l1_bk": ([P, 1], "f"), "l1_bv": ([P, P], "f"), "l1_bo": ([P, P], "f"),
    "l2_wq": ([P, P], "f"), "l2_wk": ([P, P], "f"), "l2_wv": ([P, P], "f"), "l2_wo": ([P, P], "f"),
    "l2_bo": ([P, P], "f"),
    "adj_q": ([P, 2, S], "f"), "adj_k": ([P, 2, S], "f"), "mask0_q": ([P, 2, S], "i"), "mask0_k": ([P, 2, S], "i"),
    "l0_wi": ([P, E0 + 1, F0], "f"), "l0_bi": ([P, (E0 + 1) * NC0], "f"), "l0_wo": ([P, E0 + 1, NC0, P], "f"),
    "l0_gbo": ([P, P], "f"), "l0_ebo": ([E0, P], "f"),
    "l1_w1": ([P, F0], "f"), "l1_b1": ([P, F0], "f"), "l1_w2": ([P, F0], "f"), "l1_b2": ([P, P], "f"),
    "l2_wg": ([P, E2], "f"), "l2_w1": ([P, E2, H2], "f"), "l2_w3": ([P, E2, H2], "f"),
    "l2_w2": ([P, E2, NH2, P], "f"), "l2_a1": ([R2, E2, P], "f"), "l2_a3": ([R2, E2, P], "f"),
    "l2_a2": ([R2, E2, H2], "f"), "l2_b1": ([R2, E2, H2], "f"), "l2_b3": ([R2, E2, H2], "f"),
    "l2_b2": ([R2, E2, P], "f"), "l2_bias1": ([P, E2 * NH2], "f"), "l2_bias3": ([P, E2 * NH2], "f"),
    "l2_bias2": ([E2, P], "f"),
    "l3_wi": ([P, DK3], "f"), "l3_wo": ([DK3, 16, P], "f"), "l3_bo": ([P, P], "f"),
    "l3_wm": ([P, P], "f"), "l3_bm": ([P, 1], "f"), "l3_emb": ([P, P], "f"), "l3_w1": ([KS3, E3 * I3], "f"),
    "l3_b1": ([P, NEP], "f"), "l3_w2": ([P, NEP, 32], "f"), "l3_b2": ([P, P], "f"), "l3_fo": ([P, P], "f"),
    "l3_fbo": ([P, P], "f"),
}
N_WEIGHTS = len(WEIGHTS)
SETUP_ONLY = {
    "l1_w1": ("m1", 0), "l1_w2": ("m1", F0), "l2_a1": ("hT", 0), "l2_b1": ("hT", E2 * P), "l2_a3": ("hT", E2 * (P + H2)), "l2_b3": ("qP", 0),
    "l3_w1": ("vfree", 0), "l2_a2": ("kP", 0), "l2_b2": ("rl", 0), "l3_wo": ("ex", 0),
    "mask0_q": ("rl", E2 * P), "mask0_k": ("rl", E2 * P + 2 * S),
}


def layout(I):
    import numpy as np
    f = np.float32

    def rows(v):
        return np.repeat(v.reshape(1, -1), P, 0)

    def tiles(m):
        return m.reshape(2, P, -1).transpose(1, 0, 2)

    o = {"ident": np.eye(P, dtype=f), "ones": np.ones((P, P), f),
         "pick": np.repeat(np.eye(E0, dtype=f)[None], P, 0), "iota": rows(np.arange(E3, dtype=f))}
    less = np.zeros((P, 2), f)
    for c, part in enumerate(Y_PARTS):
        less[16 * c:16 * c + 16, 0] = -1.0 * (part >= 1)
        less[16 * c:16 * c + 16, 1] = -1.0 * (part >= 2)
    o["less"] = less

    def select(parts, n, width, places, rows_):
        r = np.zeros((P, 3, n, rows_), np.uint16)
        for j in range(n):
            for g, place in enumerate(places):
                for c, part in enumerate(parts):
                    for d in range(width):
                        r[(j * len(places) + g) * width + d, part, j, place + c * width + d] = BF16_ONE
        return r

    o["sel_x"] = select(X_PARTS, NK, DH, (0, 64), P)
    o["sel_y"] = select(Y_PARTS, NK, DH, (0, 64), P)
    o["sel_h"] = select(X_PARTS, H3, HD3, (0,), KS3)
    o["sel_m"] = np.tile(np.eye(H, dtype=np.uint16) * np.uint16(BF16_ONE), (2, 1))
    o["g"] = rows(np.concatenate([I["g_xattn"], I["g_ffn"]]))
    for a, (q, k, v) in enumerate((("Wq", "Wk", "Wv"), ("Wq", "Wk", "Wv"), ("wq", "wk", "wv"))):
        for name, w in (("q", q), ("k", k), ("v", v)):
            o[f"l{a}_w{name}"] = I[f"L{a}_xattn_{w}"].T
    o["l1_wo"], o["l2_wo"] = I["L1_xattn_Wo"].T, I["L2_xattn_wo"].T
    o["l1_bq"], o["l1_bk"] = I["L1_xattn_bq"].reshape(P, 1), I["L1_xattn_bk"].reshape(P, 1)
    o["l1_bv"], o["l1_bo"], o["l2_bo"] = rows(I["L1_xattn_bv"]), rows(I["L1_xattn_bo"]), rows(I["L2_xattn_bo"])
    o["adj_q"], o["adj_k"] = tiles(I["L1_xattn_adj"]), tiles(I["L1_xattn_adj"].T)
    m0 = I["mask_1x1xSxS2_ik0"][0, 0]
    o["mask0_q"], o["mask0_k"] = tiles(m0), tiles(m0.T)
    m1 = I["mask_Bx1xSxS2_ik1"][:, 0]
    o["mask1_q"] = m1.reshape(BATCH * S, S)
    o["mask1_k"] = m1.transpose(0, 2, 1).reshape(BATCH * S, S)
    wi = np.concatenate([I["L0_ffn_gate_wi"][None], I["L0_ffn_exp_wi"]])
    bi = np.concatenate([I["L0_ffn_gate_bi"][None], I["L0_ffn_exp_bi"]])
    wo = np.concatenate([I["L0_ffn_gate_wo"][None], I["L0_ffn_exp_wo"]])
    o["l0_wi"] = wi.transpose(1, 0, 2)
    o["l0_bi"] = bi.reshape(-1, P).T
    o["l0_wo"] = wo.reshape(E0 + 1, NC0, P, P).transpose(2, 0, 1, 3)
    o["l0_gbo"], o["l0_ebo"] = rows(I["L0_ffn_gate_bo"]), I["L0_ffn_exp_bo"]
    o["l1_w1"], o["l1_b1"] = I["L1_ffn_w1"].T, rows(I["L1_ffn_b1"])
    o["l1_w2"] = I["L1_ffn_w2"].T.reshape(NC0, P, P).transpose(1, 0, 2).reshape(P, F0)
    o["l1_b2"] = rows(I["L1_ffn_b2"])
    o["l2_wg"] = I["L2_ffn_Wg"].T
    for n in "13":
        o["l2_w" + n] = I["L2_ffn_W" + n].transpose(2, 0, 1)
        o["l2_a" + n] = I["L2_ffn_A" + n].transpose(1, 0, 2)
        o["l2_b" + n] = I["L2_ffn_B" + n].transpose(2, 0, 1)
        o[f"l2_bias{n}"] = I["L2_ffn_b" + n].reshape(-1, P).T
    o["l2_w2"] = I["L2_ffn_W2"].transpose(2, 0, 1).reshape(NH2, P, E2, P).transpose(1, 2, 0, 3)
    o["l2_a2"] = I["L2_ffn_A2"].transpose(1, 0, 2)
    o["l2_b2"] = I["L2_ffn_B2"].transpose(2, 0, 1)
    o["l2_bias2"] = I["L2_ffn_b2"]
    o["l3_wi"] = I["L3_xattn_wi"]
    o["l3_wo"] = I["L3_xattn_Wo"].reshape(16, DK3, P).transpose(1, 0, 2)
    o["l3_bo"] = rows(I["L3_xattn_bo"])
    o["l3_wm"], o["l3_bm"] = I["L3_ffn_Wm"], I["L3_ffn_bm"].reshape(P, 1)
    emb = np.zeros((H3, HD3, H3, E3), f)
    for h in range(H3):
        emb[h, :, h] = I["L3_ffn_expert_emb"]
    o["l3_emb"] = emb.reshape(P, H3 * E3)
    o["l3_w1"] = np.tile(I["L3_ffn_W1"].transpose(1, 0, 2).reshape(HD3, E3 * I3), (NSEG, 1))
    o["l3_b1"] = I["L3_ffn_b1"].reshape(NEP, P).T
    w2 = np.zeros((2, I3, NEP, 2, HD3), f)
    for k in range(2):
        w2[k, :, :, k] = I["L3_ffn_W2"][k::2].transpose(1, 0, 2)
    o["l3_w2"] = w2.reshape(P, NEP, 32)
    b2 = np.zeros((H3, E3, H3, HD3), f)
    for h in range(H3):
        b2[h, :, h] = I["L3_ffn_b2"]
    o["l3_b2"] = b2.reshape(P, P)
    o["l3_fo"], o["l3_fbo"] = I["L3_ffn_Wo"], rows(I["L3_ffn_bo"])
    o["x"], o["ctx"] = I["x"].reshape(BATCH * S, D), I["ctx_1024"].reshape(BATCH * S, D)
    return o


def kernel(**inputs):
    import numpy as np
    import concourse.bacc as bacc
    from concourse.bass_utils import run_bass_kernel_spmd as run

    nc = bacc.Bacc("TRN2", target_bir_lowering=False, num_devices=1)
    arrays = {k: np.ascontiguousarray(v) for k, v in layout({k: np.asarray(v) for k, v in inputs.items()}).items()}
    A = {k: nc.dram_tensor("in_" + k, v.shape, mybir.dt.from_np(v.dtype), kind="ExternalInput").ap()
         for k, v in arrays.items()}
    out = nc.dram_tensor("out_x", (BATCH * S, D), mybir.dt.float32, kind="ExternalOutput").ap()
    flamingo(nc, A, out)
    r = run(nc, [{"in_" + k: v for k, v in arrays.items()}], core_ids=[0])
    return r.results[0]["out_x"].reshape(BATCH, S, D)
```

```python
import math

import concourse.bass as bass
from concourse import mybir
from contextlib import ExitStack

P = 128
BATCH, S, D = 8, 256, 128
NB = 2
TURNS = BATCH // NB
NT = NB * S // P
T = NT * P
H, DH = 16, 8
X_PARTS = (0, 0, 1, 1, 0, 2)
Y_PARTS = (0, 1, 0, 1, 2, 0)
NSEG = len(X_PARTS)
HP = 2
NK = H // HP
NPB = 4
KS = P // HP
KS3 = NSEG * 16
VW = 3 * (DH + 1)
SC = DH ** -0.5
E0, F0 = 8, 512
NC0 = F0 // P
E2, H2, R2 = 8, 256, 16
NH2 = H2 // P
DK3 = 64
H3, E3, HD3, I3 = 8, 16, 16, 64
NEP = E3 * I3 // P
LAMBDA = 1.0507009873554804934193349852946
ALPHA = 1.6732632423543772848170429916717
EPS = 1e-5
MAGIC = 12582912.0
NEG = -1.0e30
CAP = 1.0e25


class Chain:

    def __init__(self, eng, sem):
        self.eng, self.sem, self.n = eng, sem, 0

    def __call__(self, ins):
        self.n += 1
        ins.then_inc(self.sem, 1)
        self.eng.wait_ge(self.sem, self.n)


def flamingo(nc, A, out, turns=TURNS):
    f32, bf16, i32, u32 = mybir.dt.float32, mybir.dt.bfloat16, mybir.dt.int32, mybir.dt.uint32
    ALU, ACT, AX = mybir.AluOpType, mybir.ActivationFunctionType, mybir.AxisListType
    ctx = ExitStack()
    with ctx:
        def sb(name, shape, dt=f32):
            return ctx.enter_context(nc.sbuf_tensor(name, shape, dt))

        W = {}
        for name, (shape, dt) in WEIGHTS.items():
            if name not in SETUP_ONLY:
                W[name] = sb("w_" + name, shape, {"f": f32, "i": i32, "b": bf16}[dt])
        ident_b = sb("ident_b", [P, P], bf16)
        tg = sb("tg", [P, 8])
        tgl = sb("tgl", [P, 1])
        l0_exp_bias = sb("l0_exp_bias", [P, (E0 + 1) * NC0])
        l0_gate_bo = sb("l0_gate_bo", [P, P])
        l0_exp_bo = sb("l0_exp_bo", [E0, P])
        q_bias = sb("q_bias", [P, 1])
        w1s = sb("w1s", [KS3, E3 * I3], bf16)
        wsum = sb("wsum", [P, 2])
        wmean = sb("wmean", [P, 2])
        wscale = sb("wscale", [P, 2])
        w1q = sb("w1q", [P, F0], bf16)
        w2q = sb("w2q", [P, F0], bf16)
        wo3 = sb("wo3", [DK3, P])
        l2_bias_q = sb("l2_bias_q", [P, 2, S], bf16)
        l2_bias_k = sb("l2_bias_k", [P, 2, S], bf16)

        x = sb("x", [P, NT, D])
        xn = sb("xn", [P, NT, D])
        xT = sb("xT", [P, T])
        cT = sb("cT", [P, T])
        stats = sb("stats", [P, NT, 6])
        mv = sb("mv", [P, NT, 2])
        vare = sb("vare", [P, NT])
        rstd = sb("rstd", [P, NT])
        spare = sb("spare", [P, 1])
        mhalf = sb("mhalf", [P, NT])
        m1 = sb("m1", [P, NT, S], i32)
        m1f = m1[:].rearrange("p t k -> p (t k)").bitcast(f32).rearrange("p (t k) -> p t k", t=NT)
        bfull = sb("bfull", [P, NT, S])
        b1q = sb("b1q", [P, 2, NT, S], bf16)
        b1k = sb("b1k", [P, 3, NT, S], bf16)
        wo_sum = b1k[:].rearrange("p n t k -> p (n t k)").bitcast(f32)[:, 0:(E0 + 1) * P].rearrange(
            "p (e d) -> p e d", d=P)
        qS = sb("qS", [P, NK, T], bf16)
        kS = sb("kS", [P, NK, T], bf16)
        kf = sb("kf", [P, T])
        vf = sb("vf", [P, NT, D])
        qp = sb("qp", [P, 3, T], bf16)
        kp0 = bfull[:].rearrange("p t k -> p (t k)").bitcast(bf16)[:, 0:3 * T].rearrange("p (n k) -> p n k", n=3)
        kp = (kp0, qS[:, NK - 3:NK, :], kp0)
        vE = sb("vE", [P, NT, H, 3, DH + 1], bf16)
        nm = sb("nm", [P, NT, H])
        nmp = sb("nmp", [P, NT, 2, H], bf16)
        nmT = sb("nmT", [P, T], bf16)
        osum = sb("osum", [P, NT, H, DH + 1])
        rc = sb("rc", [P, NT, H])
        att = sb("att", [P, NT, D])
        ctxs = att
        attT = sb("attT", [P, T])
        qf = attT
        y = sb("y", [P, NT, D])
        ex = sb("ex", [P, 4, T])
        rl = sb("rl", [P, 4, T])
        f16 = mybir.dt.float16
        pH = ex[:].rearrange("p a k -> p (a k)").bitcast(f16).rearrange("p (n k) -> p n k", n=NPB)
        pL = rl[:].rearrange("p a k -> p (a k)").bitcast(f16).rearrange("p (n k) -> p n k", n=NPB)
        hT = sb("hT", [P, 2, NC0, T])
        pT = hT[:].rearrange("p a c k -> p (a c k)").rearrange("p (n k) -> p n k", n=NPB)
        acc = sb("acc", [P, NT, D])
        mx8 = sb("mx8", [P, 32, 8])
        ix8 = sb("ix8", [P, 32, 8], u32)
        ixf = sb("ixf", [P, 32, 2])
        tw = sb("tw", [P, NT, 2])
        tws = sb("tws", [P, NT])
        oh = sb("oh", [P, 2, NT, 8])
        gw = sb("gw", [P, NT, 8])
        gT = attT[0:8, :]
        lg = y[:].rearrange("p t d -> p (t d)")
        cols = sb("cols", [P, 8, NT])
        hh = rl
        kb = qS[:].rearrange("p j k -> p (j k)")
        qh = kb[:, 0:NT * F0].rearrange("p (t f) -> p t f", t=NT)
        qhT = kb[:, NT * F0:].rearrange("p (t c k) -> p t c k", t=NT, c=NC0)
        oh16 = rl[:, 1:3, :].rearrange("p a (r e) -> p a r e", e=E3)
        gates = sb("gates", [P, 32, E3])
        gb = gates[:].rearrange("p r e -> p (r e)").bitcast(bf16)
        qx = gb[:, 0:T].rearrange("p (t d) -> p t d", t=NT)
        qxT = gb[:, T:2 * T]
        gsum = sb("gsum", [P, 32])
        GT = rl[:, 3, :]
        kb16 = kS[:].rearrange("p j k -> p (j k)").bitcast(f16)
        spread = kb16[:, 0:P * HD3].rearrange("p (r d) -> p r d", d=HD3)
        GTh, GTl = (kb16[:, P * HD3 + n * T:P * HD3 + (n + 1) * T] for n in range(2))
        homes = {"hT": hT[:].rearrange("p a c k -> p (a c k)"), "qP": qS[:].rearrange("p j k -> p (j k)").bitcast(f32),
                 "kP": kS[:].rearrange("p j k -> p (j k)").bitcast(f32), "rl": rl[:].rearrange("p a k -> p (a k)"),
                 "m1": m1[:].rearrange("p t k -> p (t k)").bitcast(f32), "ex": ex[:].rearrange("p a k -> p (a k)"),
                 "y": y[:].rearrange("p t d -> p (t d)"), "vfree": bfull[:].rearrange("p t k -> p (t k)")}
        for name, (home, at) in SETUP_ONLY.items():
            (rows_, *free), dt = WEIGHTS[name]
            flat = homes[home][0:rows_, at:at + math.prod(free)]
            if dt == "i":
                flat = flat.bitcast(i32)
            W[name] = flat.rearrange("p (a b) -> p a b", a=free[0]) if len(free) > 1 else flat

        ps = ctx.enter_context(nc.psum_tensor("ps", [P, 8, 512], f32))

        def bank(n, width=512):
            return ps[:, n, 0:width]

        sems = {}

        def sem(name):
            if name not in sems:
                sems[name] = ctx.enter_context(nc.semaphore(name))
            return sems[name]

        def upto(name, a, n):
            return sem(name), PER_ATTENTION[name] * (a - (name in PROJECTED)) + n

        def slot_read(a, k):
            kind, n = SLOTS[k]
            return upto({"max": "max_ready", "shift": "nmT", "exp": "p_ready"}[kind], a, n + 1)

        turn_end = sem("turn_end")
        GO = {e: sem("go_" + e) for e in ("pe", "act", "dve", "pool")}
        stored = sem("out_stored")
        kept = set(sems)
        block = ctx.enter_context(nc.Block())

        def end_turn(eng, who):
            eng.drain().then_inc(turn_end, 1)
            eng.wait_ge(GO[who], 1)
            eng.sem_clear(GO[who])

        @block.gpsimd
        def _(pool):
            step = Chain(pool, sem("pool_step"))
            pool.memset(mhalf[:], -0.5)
            pool.memset(nmT[:], 0.0)
            step(pool.memset(vE[:], 0.0))
            pool.memset(vE[:, :, :, 0, DH:DH + 1], 1.0)
            pool.wait_ge(sem("setup_loaded"), 16 * len(SETUP_WEIGHTS))
            wo = W["l0_wo"]
            step(pool.tensor_tensor(wo_sum, wo[:, :, 0, :], wo[:, :, 1, :], ALU.add))
            for fc in range(2, NC0):
                step(pool.tensor_tensor(wo_sum, wo_sum, wo[:, :, fc, :], ALU.add))
            pool.engine_nop().then_inc(sem("wo_sum"), 1)
            for dst, src in ((l2_bias_q, W["mask0_q"]), (l2_bias_k, W["mask0_k"])):
                pool.tensor_scalar(dst[:], src, 0.0, NEG, ALU.is_equal, ALU.mult)
            end_turn(pool, "pool")
            with pool.Fori(0, turns):
                step = Chain(pool, sem("pool_step"))

                def root(n):
                    pool.wait_ge(sem("var_ready"), n)
                    pool.tensor_tensor(rstd[:], vare[:], mhalf[:], ALU.pow).then_inc(sem("rstd_ready"), 1)

                def biases():
                    for side, parts, dst, adj in ((0, 2, b1q, W["adj_q"]), (1, 3, b1k, W["adj_k"])):
                        pool.wait_ge(sem("masks_loaded"), 16 * (side + 1))
                        pool.tensor_scalar(bfull[:], m1[:], 0.0, NEG, ALU.is_equal, ALU.mult)\
                            .then_inc(sem("mask_read"), 1)
                        pool.wait_ge(sem("mask_read"), side + 1)
                        for b in range(NB):
                            ins = pool.tensor_tensor(bfull[:, 2 * b:2 * b + 2, :], bfull[:, 2 * b:2 * b + 2, :],
                                                     adj[:], ALU.add)
                            step(ins)
                        full = bfull[:] if side == 0 else m1f
                        step(pool.tensor_copy(dst[:, 0], bfull[:]))
                        step(pool.tensor_tensor(full, bfull[:], dst[:, 0], ALU.subtract))
                        for part in range(1, parts):
                            last = pool.tensor_copy(dst[:, part], full)
                            step(last)
                            if part + 1 < parts:
                                step(pool.tensor_tensor(full, full, dst[:, part], ALU.subtract))
                    pool.engine_nop().then_inc(sem("l1_bias_ready"), 1)

                def split(src, part):
                    step(pool.tensor_copy(part(0), src))
                    step(pool.tensor_tensor(src, src, part(0), ALU.subtract))
                    step(pool.tensor_copy(part(1), src))
                    return pool.tensor_tensor(part(2), src, part(1), ALU.subtract)

                def keys_values(a):
                    if a:
                        pool.wait_ge(*upto("kf", a, 1))
                        split(kf[:], lambda n: kp[a][:, n, :]).then_inc(sem("kp"), 1)
                    pool.wait_ge(*upto("vf", a, 1))
                    split(vf[:].rearrange("p t (h d) -> p (t h) d", h=H),
                          lambda n: vE[:, :, :, n, 0:DH].rearrange("p t h d -> p (t h) d"))\
                        .then_inc(sem("v_ready"), 1)

                root(1)
                keys_values(0)
                root(2)
                keys_values(1)
                biases()
                root(3)
                root(4)
                root(5)
                keys_values(2)
                root(6)
                root(7)
                pool.wait_ge(*upto("s2", 2, 2 * NK))
                pool.tensor_copy(spread, W["ident"][:].unsqueeze(2).to_broadcast([P, P, HD3]))\
                    .then_inc(sem("spread"), 1)
                for n in range(8, 11):
                    root(n)
                pool.wait_ge(sem("f3_h"), 1)
                step(pool.tensor_copy(qp[:, 0, :], qf[:]))
                pool.wait_ge(sem("f3_lg"), 1)
                step(pool.tensor_tensor(qf[:], qf[:], qp[:, 0, :], ALU.subtract))
                step(pool.tensor_copy(qp[:, 1, :], qf[:]))
                pool.tensor_tensor(qp[:, 2, :], qf[:], qp[:, 1, :], ALU.subtract).then_inc(sem("f3_hp"), 1)
                end_turn(pool, "pool")

        @block.tensor
        def _(pe):
            pe.wait_ge(sem("setup_loaded"), 16 * len(SETUP_WEIGHTS))
            for m, (a, b) in enumerate((("l2_a1", "l2_b1"), ("l2_a3", "l2_b3"))):
                for e in range(E2):
                    last = pe.matmul(ps[:, 4 * m + e // 2, (e % 2) * H2:(e % 2 + 1) * H2],
                                     W[a][:, e, :], W[b][:, e, :], start=True, stop=True)
                last.then_inc(sem("lora"), 1)
            pe.wait_ge(sem("merged"), 1)
            for e in range(E2):
                for hc in range(NH2):
                    i = NH2 * e + hc
                    last = pe.matmul(ps[:, i // 4, (i % 4) * P:(i % 4 + 1) * P],
                                     W["l2_a2"][:, e, hc * P:(hc + 1) * P], W["l2_b2"][:, e, :],
                                     start=True, stop=True)
            last.then_inc(sem("lora"), 1)
            pe.wait_ge(sem("merged"), 2)
            pe.wait_ge(sem("wo_sum"), 1)
            pe.matmul(bank(4, P), W["ones"], wo_sum[:, 0, :], start=True, stop=True)
            for e in range(E0):
                last = pe.matmul(ps[0:E0, 5, 0:P], W["pick"][:, e, :], wo_sum[:, e + 1, :],
                                 start=e == 0, stop=e == E0 - 1)
            last.then_inc(sem("colsum"), 1)
            pe.wait_ge(sem("wsum_ready"), 1)
            pe.matmul(bank(6, 2), W["ones"], wsum[:], start=True, stop=True).then_inc(sem("wabs"), 1)
            end_turn(pe, "pe")

            with pe.Fori(0, turns):
                for t in range(NT):
                    last = pe.transpose(bank(3)[:, t * P:(t + 1) * P], ctxs[:, t, :], W["ident"][:])
                last.then_inc(sem("cT_ps"), 1)
                pe.wait_ge(sem("cT_ready"), 1)

                def norm_T(n):
                    pe.wait_ge(sem("xn_ready"), n + 1)
                    for t in range(NT):
                        last = pe.transpose(bank(0)[:, t * P:(t + 1) * P], xn[:, t, :], W["ident"][:])
                    last.then_inc(sem("xT_ps"), 1)

                def keys_values(a):
                    L = f"l{a}_"
                    pe.matmul(bank(6), W[L + "wk"][:], cT[:], start=True, stop=True).then_inc(sem("k_ps"), 1)
                    for t in range(NT):
                        last = pe.matmul(bank(7)[:, t * P:(t + 1) * P], cT[:, t * P:(t + 1) * P], W[L + "wv"][:],
                                         start=True, stop=True)
                    last.then_inc(sem("v_ps"), 1)

                def key_stack(a, j):
                    if j == 0:
                        pe.wait_ge(*upto("kp", a, 1))
                        pe.wait_ge(*upto("vf", a, 1))
                    if j >= 2:
                        pe.wait_ge(*upto(("ks_even", "ks_odd")[j % 2], a, j // 2))
                    for n in range(3):
                        last = pe.matmul(bank(6 + j % 2), W["sel_y"][:, n, j, :], kp[a][:, n, :],
                                         start=n == 0, stop=n == 2)
                    last.then_inc(sem("ks_ps"), 1)

                def queries(a):
                    norm_T(LN_OF_ATT[a])
                    pe.wait_ge(sem("xT_ready"), n_T(LN_OF_ATT[a]))
                    pe.matmul(bank(1), W[f"l{a}_wq"][:], xT[:], start=True, stop=True).then_inc(sem("q_ps"), 1)

                def attention(a):
                    L = f"l{a}_"
                    pe.wait_ge(*upto("qp", a, 1))
                    for name in ("ks_even", "ks_odd"):
                        pe.wait_ge(*upto(name, a, NK // 2))

                    def query_stack(j):
                        for n in range(3):
                            last = pe.matmul(bank(6 + j % 2), W["sel_x"][:, n, j, :], qp[:, n, :],
                                             start=n == 0, stop=n == 2)
                        last.then_inc(sem("qs_ps"), 1)

                    query_stack(0)
                    query_stack(1)
                    if a == 1:
                        pe.wait_ge(sem("l1_bias_ready"), 1)

                    def scores_for_max(s, n):
                        b, j = divmod(n, NK)
                        bias = {0: [], 1: [b1q[:, 0, 2 * b:2 * b + 2, :], b1q[:, 1, 2 * b:2 * b + 2, :]],
                                2: [l2_bias_q[:]]}[a]
                        for g in range(HP):
                            for i, part in enumerate(bias):
                                pe.matmul(bank(s + g), ident_b[:], part.rearrange("p t k -> p (t k)"), start=i == 0,
                                          stop=False, skip_group_check=True)
                        for qt in range(2):
                            for g in range(HP):
                                row, at = 64 * g, b * S + qt * P
                                last = pe.matmul(bank(s + g)[:, qt * S:(qt + 1) * S],
                                                 qS[row:row + KS, j, at:at + P],
                                                 kS[row:row + KS, j, b * S:(b + 1) * S],
                                                 start=not bias, stop=True, skip_group_check=bool(bias))
                        last.then_inc(sem("s1"), 1)

                    def maxima_T(s, b):
                        pe.wait_ge(*upto("max_parts", a, b + 1))
                        for qt in range(2):
                            last = pe.transpose(ps[0:2 * H, s, :].bitcast(bf16)[:, qt * P:(qt + 1) * P],
                                                nmp[:, 2 * b + qt].rearrange("p n h -> p (n h)"), ident_b[:])
                        last.then_inc(sem("max_T"), 1)

                    def values(v):
                        b, j = divmod(v, NK)
                        if j == 0 and b:
                            pe.wait_ge(*upto("o_read", a, b))
                        pe.wait_ge(*upto("p_low", a, v + 1))
                        if v == 0:
                            pe.wait_ge(*upto("v_ready", a, 1))
                        for hh_ in range(HP):
                            h = HP * j + hh_
                            for qt in range(2):
                                for kt in range(2):
                                    at = hh_ * 2 * S + kt * S + qt * P
                                    for n, part in enumerate((pH, pL)):
                                        last = pe.matmul(bank(6 + qt)[:, h * VW:(h + 1) * VW],
                                                         part[:, v % NPB, at:at + P],
                                                         vE[:, 2 * b + kt, h].rearrange("p n d -> p (n d)"),
                                                         start=kt + n == 0, stop=kt + n == 2)
                        last.then_inc(sem("pv"), 1)

                    def scores_for_exp(s, v):
                        b, j = divmod(v, NK)
                        pe.wait_ge(*upto("nmT", a, b + 1))
                        bias = {0: [], 1: [b1k[:, n, 2 * b:2 * b + 2, :] for n in range(3)],
                                2: [l2_bias_k[:]]}[a]
                        for hh_ in range(HP):
                            shift = nmT[:, b * S:(b + 1) * S].unsqueeze(1).to_broadcast([P, 2, S])
                            pe.matmul(bank(s + hh_).rearrange("p (t k) -> p t k", t=2),
                                      W["sel_m"][:, HP * j + hh_:HP * j + hh_ + 1].to_broadcast([P, P]), shift,
                                      start=True, stop=False, skip_group_check=True)
                            for part in bias if a != 1 or hh_ == 0 else []:
                                pe.matmul(bank(s + hh_), ident_b[:], part.rearrange("p t k -> p (t k)"), start=False,
                                          stop=False, skip_group_check=True)
                        for kt in range(2):
                            for hh_ in range(HP):
                                row, at = 64 * hh_, b * S + kt * P
                                last = pe.matmul(bank(s + hh_)[:, kt * S:(kt + 1) * S],
                                                 kS[row:row + KS, j, at:at + P],
                                                 qS[row:row + KS, j, b * S:(b + 1) * S],
                                                 start=False, stop=True, skip_group_check=True)
                        last.then_inc(sem("s2"), 1)

                    for k, (kind, n) in enumerate(SLOTS):
                        s = 2 * (k % 3)
                        if k >= 3:
                            pe.wait_ge(*slot_read(a, k - 3))
                        if kind == "max" and n < NK:
                            pe.wait_ge(*upto("qs", a, n + 1))
                        if kind == "max":
                            scores_for_max(s, n)
                            if n + 2 < NK:
                                query_stack(n + 2)
                        elif kind == "shift":
                            maxima_T(s, n)
                        else:
                            scores_for_exp(s, n)
                            if n >= NPB - 1:
                                values(n - NPB + 1)
                    for v in range(2 * NK - NPB + 1, 2 * NK):
                        values(v)
                    if a:
                        pe.wait_ge(*upto("att_ready", a, 1))
                        for t in range(NT):
                            last = pe.transpose(bank(0)[:, t * P:(t + 1) * P], att[:, t, :], W["ident"][:])
                        last.then_inc(sem("attT_ps"), 1)
                        pe.wait_ge(*upto("attT", a, 1))
                        for t in range(NT):
                            last = pe.matmul(bank(1)[:, t * P:(t + 1) * P], attT[:, t * P:(t + 1) * P],
                                             W[L + "wo"][:], start=True, stop=True)
                        last.then_inc(sem("o_ps"), 1)

                keys_values(0)
                queries(0)
                for j in range(NK):
                    key_stack(0, j)
                attention(0)

                pe.wait_ge(sem("x_done"), 1)
                keys_values(1)
                norm_T(1)
                pe.wait_ge(sem("xT_ready"), n_T(1))

                def f0_out(e):
                    pe.wait_ge(sem("f0_h"), NC0 * (e + 1))
                    if e >= 2:
                        pe.wait_ge(sem("f0_out_read"), e - 1)
                    for t in range(NT):
                        for fc in range(NC0):
                            last = pe.matmul(bank(4 + e % 2)[:, t * P:(t + 1) * P],
                                             hT[:, e % 2, fc, t * P:(t + 1) * P], W["l0_wo"][:, e, fc, :],
                                             start=fc == 0, stop=fc == NC0 - 1)
                    last.then_inc(sem("f0_out"), 1)

                for e in range(E0 + 1):
                    for fc in range(NC0):
                        n = NC0 * e + fc
                        if n >= 4:
                            pe.wait_ge(sem("f0_act"), n - 3)
                        pe.matmul(bank(n % 4), W["l0_wi"][:, e, fc * P:(fc + 1) * P], xT[:], start=True, stop=True)\
                          .then_inc(sem("f0_in"), 1)
                    if e >= 1:
                        f0_out(e - 1)
                f0_out(E0)
                pe.wait_ge(*upto("kf", 1, 1))
                pe.wait_ge(*upto("vf", 1, 1))
                pe.wait_ge(sem("f0_gate"), 1)
                for t in range(NT):
                    last = pe.transpose(ps[0:8, 7, t * P:(t + 1) * P], gw[:, t, :], W["ident"][:])
                last.then_inc(sem("f0_gT_ps"), 1)
                pe.wait_ge(sem("f0_gT"), 1)
                for t in range(NT):
                    last = pe.matmul(bank(6)[:, t * P:(t + 1) * P], gT[:, t * P:(t + 1) * P], l0_exp_bo[:],
                                     start=True, stop=True)
                last.then_inc(sem("f0_b"), 1)

                def keys_and_queries(a):
                    pe.wait_ge(sem("x_done"), LN_OF_ATT[a])
                    for j in range(NK // 2):
                        key_stack(a, j)
                    queries(a)
                    for j in range(NK // 2, NK):
                        key_stack(a, j)

                keys_and_queries(1)
                attention(1)

                pe.wait_ge(sem("x_done"), 3)
                keys_values(2)
                pe.wait_ge(sem("f1_qx"), 1)
                xb = bank(0).bitcast(bf16)
                for t in range(NT):
                    last = pe.transpose(xb[:, t * P:(t + 1) * P], qx[:, t, :], ident_b[:])
                last.then_inc(sem("f1_qxT_ps"), 1)
                pe.wait_ge(sem("f1_qxT"), 1)
                for t in range(NT):
                    pe.matmul(bank(1 + t), qxT[:, t * P:(t + 1) * P], w1q[:], start=True, stop=True)\
                      .then_inc(sem("f1_h_ps"), 1)
                pe.wait_ge(sem("f1_qh"), 1)
                for t in range(NT):
                    hb = bank(1 + t).bitcast(bf16)
                    for fc in range(NC0):
                        last = pe.transpose(hb[:, fc * P:(fc + 1) * P], qh[:, t, fc * P:(fc + 1) * P], ident_b[:])
                    last.then_inc(sem("f1_qhT_ps"), 1)
                for t in range(NT):
                    pe.wait_ge(sem("f1_qhT"), t + 1)
                    for fc in range(NC0):
                        last = pe.matmul(bank(0)[:, t * P:(t + 1) * P], qhT[:, t, fc, :],
                                         w2q[:, fc * P:(fc + 1) * P], start=fc == 0, stop=fc == NC0 - 1)
                last.then_inc(sem("f1_o_ps"), 1)

                keys_and_queries(2)
                attention(2)

                norm_T(5)
                pe.wait_ge(sem("xT_ready"), n_T(5))
                pe.wait_ge(sem("x_done"), 5)
                for t in range(NT):
                    last = pe.matmul(bank(7)[:, t * 8:(t + 1) * 8], xT[:, t * P:(t + 1) * P], W["l2_wg"][:],
                                     start=True, stop=True)
                last.then_inc(sem("f2_lg"), 1)

                def f2_out(e):
                    pe.wait_ge(sem("f2_g"), NH2 * (e + 1))
                    if e >= 2:
                        pe.wait_ge(sem("f2_out_read"), e - 1)
                    for t in range(NT):
                        for hc in range(NH2):
                            last = pe.matmul(bank(4 + e % 2)[:, t * P:(t + 1) * P],
                                             hT[:, e % 2, hc, t * P:(t + 1) * P], W["l2_w2"][:, e, hc, :],
                                             start=hc == 0, stop=hc == NH2 - 1)
                    last.then_inc(sem("f2_out"), 1)

                for e in range(E2):
                    for hc in range(NH2):
                        n = NH2 * e + hc
                        if n >= 2:
                            pe.wait_ge(sem("f2_g"), n - 1)
                        s = 2 * (n % 2)
                        pe.matmul(bank(s), W["l2_w1"][:, e, hc * P:(hc + 1) * P], xT[:], start=True, stop=True)\
                          .then_inc(sem("f2_h1"), 1)
                        pe.matmul(bank(s + 1), W["l2_w3"][:, e, hc * P:(hc + 1) * P], xT[:], start=True, stop=True)\
                          .then_inc(sem("f2_h3"), 1)
                    if e >= 1:
                        f2_out(e - 1)
                f2_out(E2 - 1)
                pe.wait_ge(sem("f2_gate"), 1)
                for t in range(NT):
                    last = pe.transpose(ps[0:8, 7, t * P:(t + 1) * P], gw[:, t, :], W["ident"][:])
                last.then_inc(sem("f2_gT_ps"), 1)
                pe.wait_ge(sem("f2_gT"), 1)
                for t in range(NT):
                    last = pe.matmul(bank(6)[:, t * P:(t + 1) * P], gT[:, t * P:(t + 1) * P], W["l2_bias2"][:],
                                     start=True, stop=True)
                last.then_inc(sem("f2_b"), 1)

                pe.wait_ge(sem("x_done"), 6)
                pe.matmul(ps[0:DK3, 1, :], W["l3_wi"][:], cT[:], start=True, stop=True).then_inc(sem("l3_k_ps"), 1)
                for t in range(NT):
                    last = pe.matmul(bank(2)[:, t * DK3:(t + 1) * DK3], cT[:, t * P:(t + 1) * P], W["l3_wi"][:],
                                     start=True, stop=True)
                last.then_inc(sem("l3_v_ps"), 1)
                norm_T(6)
                pe.wait_ge(sem("xT_ready"), n_T(6))
                pe.matmul(ps[0:DK3, 3, :], W["l3_wi"][:], xT[:], start=True, stop=True).then_inc(sem("l3_q_ps"), 1)
                pe.wait_ge(sem("l3_k"), 1)
                pe.wait_ge(sem("l3_q"), 1)
                for t in range(NT):
                    b = t // 2
                    last = pe.matmul(bank(4 + b)[:, (t % 2) * S:(t % 2 + 1) * S], attT[0:DK3, t * P:(t + 1) * P],
                                     GT[0:DK3, b * S:(b + 1) * S], start=True, stop=True)
                last.then_inc(sem("l3_s"), 1)
                pe.wait_ge(sem("l3_p"), 1)
                for kt in range(2):
                    for t in range(NT):
                        last = pe.transpose(bank(6 + kt)[:, t * P:(t + 1) * P],
                                            pT[:, 0, t * S + kt * P:t * S + kt * P + P], W["ident"][:])
                    last.then_inc(sem("l3_pT_ps"), 1)
                pe.wait_ge(sem("l3_pT_act"), 1)
                pe.wait_ge(sem("l3_pT_dve"), 1)
                for b in range(NB):
                    for kt in range(2):
                        last = pe.matmul(ps[0:DK3, 1, b * S:(b + 1) * S], y[:, 2 * b + kt, 0:DK3],
                                         pT[:, 1, kt * T + b * S:kt * T + (b + 1) * S], start=kt == 0, stop=kt == 1)
                last.then_inc(sem("l3_head_ps"), 1)
                pe.wait_ge(sem("l3_head"), 1)
                for t in range(NT):
                    last = pe.matmul(bank(2)[:, t * P:(t + 1) * P], lg[0:DK3, t * P:(t + 1) * P], wo3[:],
                                     start=True, stop=True)
                last.then_inc(sem("l3_o_ps"), 1)

                norm_T(7)
                pe.wait_ge(sem("xT_ready"), n_T(7))
                pe.wait_ge(sem("x_done"), 7)
                pe.matmul(bank(1), W["l3_wm"][:], xT[:], start=True, stop=True).then_inc(sem("f3_h_ps"), 1)
                pe.wait_ge(sem("f3_h"), 1)
                for t in range(NT):
                    last = pe.matmul(bank(3)[:, t * P:(t + 1) * P], qf[:, t * P:(t + 1) * P], W["l3_emb"][:],
                                     start=True, stop=True)
                last.then_inc(sem("f3_lg"), 1)
                pe.wait_ge(sem("f3_hp"), 1)

                def head_stack(h):
                    if h >= 4:
                        pe.wait_ge(sem("f3_hs"), h - 3)
                    for n in range(3):
                        last = pe.matmul(ps[0:KS3, 4 + h % 4, :], W["sel_h"][:, n, h, :], qp[:, n, :],
                                         start=n == 0, stop=n == 2)
                    last.then_inc(sem("f3_hs_ps"), 1)

                for h in range(4):
                    head_stack(h)

                def f3_out(n):
                    w, ep = divmod(n, NEP // 2)
                    pe.wait_ge(sem("f3_mid"), n + 1)
                    if ep == 0 and w >= 2:
                        pe.wait_ge(sem("f3_prod"), w - 1)
                    pe.matmul(ps[32 * ep:32 * ep + 32, 4 + w % 2, :], W["l3_w2"][:, n % NEP, :],
                              hT[:, 0, n % 4, :], start=True, stop=True).then_inc(sem("f3_out"), 1)

                def f3_gates_T():
                    pe.wait_ge(sem("f3_gate"), 1)
                    for t in range(NT):
                        last = pe.transpose(bank(6)[:, t * P:(t + 1) * P],
                                            gates[:, 8 * t:8 * t + 8, :].rearrange("p h e -> p (h e)"),
                                            W["ident"][:])
                    last.then_inc(sem("f3_gT_ps"), 1)

                def f3_spread(w):
                    if w == 0:
                        pe.wait_ge(sem("f3_gT"), 2)
                        pe.wait_ge(sem("f3_gT_low"), 1)
                        pe.wait_ge(sem("spread"), 1)
                    if w >= 2:
                        pe.wait_ge(sem("f3_gr"), w - 1)
                    ones = spread[:, 8 * w:8 * w + 8, :].rearrange("p r d -> p (r d)")
                    pe.matmul(bank(6 + w % 2), ones, GTh, start=True, stop=False)
                    pe.matmul(bank(6 + w % 2), ones, GTl, start=False, stop=True).then_inc(sem("f3_gr_ps"), 1)
                    if w == 0:
                        pe.matmul(bank(3), W["l3_b2"][:], GT, start=True, stop=False)

                def f3_sum(h):
                    pe.wait_ge(sem("f3_head"), h + 1)
                    pe.matmul(bank(3), W["sum_o"][:, P - HD3 * (h + 1):2 * P - HD3 * (h + 1)], ex[:, 2 + h % 2, :],
                              start=False, stop=h == H3 - 1).then_inc(sem("f3_sum"), 1)

                def f3_step(m):
                    f3_out(m)
                    w, ep = divmod(m, NEP // 2)
                    if ep == NEP // 2 - 1:
                        f3_spread(w)
                    if ep == 1 and w >= 3 and w % 2 == 1:
                        f3_sum((w - 3) // 2)

                for n in range(H3 * NEP):
                    h, ep = divmod(n, NEP)
                    if ep == 0:
                        pe.wait_ge(sem("f3_hs"), h + 1)
                    if n >= 3:
                        pe.wait_ge(sem("f3_mid"), n - 2)
                    pe.matmul(bank(n % 3), w1s[:, ep * P:(ep + 1) * P], qS[0:KS3, h, :], start=True, stop=True)\
                      .then_inc(sem("f3_in"), 1)
                    if n < 4:
                        head_stack(4 + n)
                    if n == 3:
                        pe.wait_ge(sem("f3_hs"), H3)
                        f3_gates_T()
                    if n >= 3:
                        f3_step(n - 3)
                for n in range(H3 * NEP - 3, H3 * NEP):
                    f3_step(n)
                f3_sum(H3 - 1)
                pe.wait_ge(sem("f3_cT"), 1)
                for t in range(NT):
                    last = pe.matmul(bank(1)[:, t * P:(t + 1) * P], attT[:, t * P:(t + 1) * P], W["l3_fo"][:],
                                     start=True, stop=True)
                last.then_inc(sem("f3_o_ps"), 1)
                end_turn(pe, "pe")

        @block.scalar
        def _(act):
            act.wait_ge(sem("setup_loaded"), 16 * len(SETUP_WEIGHTS))
            act.activation(tg[:], W["g"][:], ACT.Tanh).then_inc(sem("tg_ready"), 1)
            act.activation(ident_b[:], W["ident"][:], ACT.Copy)
            end_turn(act, "act")

            with act.Fori(0, turns):
                act.wait_ge(sem("cT_ps"), 1)
                act.activation(cT[:], bank(3), ACT.Copy).then_inc(sem("cT_ready"), 1)

                def norm_T(n):
                    act.wait_ge(sem("xT_ps"), n_T(n))
                    act.activation(xT[:], bank(0), ACT.Copy).then_inc(sem("xT_ready"), 1)

                def keys(a):
                    act.wait_ge(*upto("k_ps", a, 1))
                    if a == 1:
                        ins = act.activation(kf[:], bank(6), ACT.Identity, bias=W["l1_bk"][:])
                    else:
                        ins = act.activation(kf[:], bank(6), ACT.Copy if a else ACT.Relu)
                    ins.then_inc(sem("kf"), 1)

                def key_stack(a, j):
                    act.wait_ge(*upto("ks_ps", a, j + 1))
                    act.activation(kS[:, j, :], bank(6 + j % 2), ACT.Copy)\
                       .then_inc(sem(("ks_even", "ks_odd")[j % 2]), 1)

                def queries(a):
                    norm_T(LN_OF_ATT[a])
                    act.wait_ge(*upto("q_ps", a, 1))
                    if a == 1:
                        ins = act.activation(qf[:], bank(1), ACT.Identity, bias=q_bias[:], scale=SC)
                    else:
                        ins = act.activation(qf[:], bank(1), ACT.Copy if a else ACT.Relu, scale=SC)
                    ins.then_inc(sem("qf"), 1)

                def attention(a):
                    for j in range(NK):
                        act.wait_ge(*upto("qs_ps", a, j + 1))
                        act.activation(qS[:, j, :], bank(6 + j % 2), ACT.Copy).then_inc(sem("qs"), 1)
                    for k, (kind, v) in enumerate(SLOTS):
                        s = 2 * (k % 3)
                        if kind == "max":
                            continue
                        if kind == "shift":
                            act.wait_ge(*upto("max_T", a, v + 1))
                            act.activation(nmT[0:2 * H, v * S:(v + 1) * S], ps[0:2 * H, s, :].bitcast(bf16)[:, 0:S],
                                           ACT.Copy).then_inc(sem("nmT"), 1)
                            continue
                        if a == 1:
                            act.wait_ge(sem("biased"), v + 1)
                        else:
                            act.wait_ge(*upto("s2", a, v + 1))
                        if v >= NPB:
                            act.wait_ge(*upto("p_low", a, v - NPB + 1))
                        scores = ps[:, s:s + 2, :].rearrange("p n k -> p (n k)")
                        if HIGH_BY_ACT(a, v):
                            if v >= NPB:
                                act.wait_ge(*upto("pv", a, v - NPB + 1))
                            act.activation(pH[:, v % NPB, :], scores, ACT.Exp)
                        act.activation(pT[:, v % NPB, :], scores, ACT.Exp).then_inc(sem("p_ready"), 1)
                    if a:
                        act.wait_ge(*upto("attT_ps", a, 1))
                        act.activation(attT[:], bank(0), ACT.Copy).then_inc(sem("attT"), 1)

                act.wait_ge(sem("x_free"), 1)
                act.activation(x[:], xn[:], ACT.Copy).then_inc(sem("x_copied"), 1)
                keys(0)
                queries(0)
                for j in range(0, NK, 2):
                    key_stack(0, j)
                attention(0)

                keys(1)
                norm_T(1)
                for n in range(NC0 * (E0 + 1)):
                    act.wait_ge(sem("f0_in"), n + 1)
                    if n >= 4:
                        act.wait_ge(sem("f0_h"), n - 3)
                    act.activation(ex[:, n % 4, :], bank(n % 4), ACT.Exp, bias=l0_exp_bias[:, n:n + 1])
                    act.activation(rl[:, n % 4, :], bank(n % 4), ACT.Relu, bias=W["l0_bi"][:, n:n + 1])\
                       .then_inc(sem("f0_act"), 1)
                act.wait_ge(sem("f0_gT_ps"), 1)
                act.activation(gT, ps[0:8, 7, :], ACT.Copy).then_inc(sem("f0_gT"), 1)

                def keys_and_queries(a):
                    for j in range(NK // 2):
                        key_stack(a, j)
                    queries(a)
                    for j in range(NK // 2, NK):
                        key_stack(a, j)

                keys_and_queries(1)
                attention(1)

                keys(2)
                act.wait_ge(sem("f1_qxT_ps"), 1)
                act.activation(qxT, bank(0).bitcast(bf16)[:, 0:T], ACT.Copy).then_inc(sem("f1_qxT"), 1)
                for t in range(NT):
                    act.wait_ge(sem("f1_y"), t + 1)
                    act.activation(hh[:, t, :], hT[:, 0, t, :], ACT.Gelu).then_inc(sem("f1_gelu"), 1)
                    act.wait_ge(sem("f1_gelu"), t + 1)
                    act.activation(hT[:, 1, t, :], hh[:, t, :], ACT.Square, accum_out=cols[:, 0, t:t + 1])\
                       .then_inc(sem("f1_sq"), 1)
                for t in range(NT):
                    act.wait_ge(sem("f1_qhT_ps"), t + 1)
                    act.activation(qhT[:, t].rearrange("p c k -> p (c k)"), bank(1 + t).bitcast(bf16)[:, 0:F0],
                                   ACT.Copy).then_inc(sem("f1_qhT"), 1)

                keys_and_queries(2)
                attention(2)

                norm_T(5)
                act.wait_ge(sem("f2_gap"), 1)
                act.activation(tw[:, :, 1], tws[:], ACT.Exp).then_inc(sem("f2_gap_exp"), 1)
                for n in range(NH2 * E2):
                    act.wait_ge(sem("f2_h1"), n + 1)
                    if n >= 2:
                        act.wait_ge(sem("f2_g"), n - 1)
                    act.activation(ex[:, n % 2, :], bank(2 * (n % 2)), ACT.Silu,
                                   bias=W["l2_bias1"][:, n:n + 1]).then_inc(sem("f2_silu"), 1)
                act.wait_ge(sem("f2_gT_ps"), 1)
                act.activation(gT, ps[0:8, 7, :], ACT.Copy).then_inc(sem("f2_gT"), 1)

                act.wait_ge(sem("l3_k_ps"), 1)
                act.activation(GT[0:DK3, :], ps[0:DK3, 1, :], ACT.Copy, scale=DK3 ** -0.5).then_inc(sem("l3_k"), 1)
                norm_T(6)
                act.wait_ge(sem("l3_q_ps"), 1)
                act.activation(attT[0:DK3, :], ps[0:DK3, 3, :], ACT.Copy).then_inc(sem("l3_q"), 1)
                act.wait_ge(sem("l3_max"), 1)
                for t in range(NT):
                    act.activation(ex[:, t // 2, (t % 2) * S:(t % 2 + 1) * S],
                                   bank(4 + t // 2)[:, (t % 2) * S:(t % 2 + 1) * S], ACT.Exp,
                                   bias=cols[:, 0, t:t + 1], accum_out=cols[:, 1, t:t + 1])\
                       .then_inc(sem("l3_exp"), 1)
                act.wait_ge(sem("l3_pT_ps"), 1)
                act.activation(pT[:, 1, 0:T], bank(6), ACT.Copy).then_inc(sem("l3_pT_act"), 1)

                norm_T(7)
                act.wait_ge(sem("f3_h_ps"), 1)
                act.activation(qf[:], bank(1), ACT.Identity, bias=W["l3_bm"][:]).then_inc(sem("f3_h"), 1)
                act.wait_ge(sem("f3_lgm"), 1)
                act.activation(gates[:].rearrange("p h e -> p (h e)"), rl[:, 0, :], ACT.Exp).then_inc(sem("f3_exp"), 1)
                act.activation(spare[:], tg[:, 0:1], ACT.Gelu)

                def head_stack(h):
                    act.wait_ge(sem("f3_hs_ps"), h + 1)
                    act.activation(qS[0:KS3, h, :], ps[0:KS3, 4 + h % 4, :], ACT.Copy).then_inc(sem("f3_hs"), 1)

                for h in range(4):
                    head_stack(h)

                def spread(w):
                    act.wait_ge(sem("f3_gr_ps"), w + 1)
                    if w >= 2:
                        act.wait_ge(sem("f3_prod"), w - 1)
                    act.activation(ex[:, w % 2, :], bank(6 + w % 2), ACT.Copy).then_inc(sem("f3_gr"), 1)

                for n in range(H3 * NEP):
                    act.wait_ge(sem("f3_in"), n + 1)
                    if n >= 4:
                        act.wait_ge(sem("f3_out"), n - 3)
                    act.activation(hT[:, 0, n % 4, :], bank(n % 3), ACT.Gelu,
                                   bias=W["l3_b1"][:, n % NEP:n % NEP + 1]).then_inc(sem("f3_mid"), 1)
                    if n < 4:
                        head_stack(4 + n)
                    if n == 3:
                        act.wait_ge(sem("f3_gT_ps"), 1)
                        act.activation(GTh, bank(6), ACT.Copy).then_inc(sem("f3_gT"), 1)
                        act.activation(GT, bank(6), ACT.Copy).then_inc(sem("f3_gT"), 1)
                    if n >= 6 and (n - 6) % 4 == 0:
                        spread((n - 6) // 4)
                spread(2 * H3 - 1)
                act.wait_ge(sem("f3_sum"), H3)
                act.activation(attT[:], bank(3), ACT.Copy).then_inc(sem("f3_cT"), 1)
                end_turn(act, "act")

        @block.vector
        def _(dve):
            step = Chain(dve, sem("dve_step"))
            dve.wait_ge(sem("setup_loaded"), 16 * len(SETUP_WEIGHTS))
            for n, name in enumerate(("l1_w1", "l1_w2")):
                step(dve.tensor_reduce(wsum[:, n:n + 1], W[name], AX.X, ALU.add, apply_absolute_value=True))
            dve.engine_nop().then_inc(sem("wsum_ready"), 1)
            dve.tensor_scalar(l0_exp_bias[:], W["l0_bi"][:], math.log(ALPHA), None, ALU.add)
            dve.tensor_scalar(q_bias[:], W["l1_bq"][:], SC, None, ALU.mult)
            w = W["l3_w1"]
            step(dve.tensor_copy(w1s[:], w))
            step(dve.scalar_tensor_tensor(w, w1s[:], W["less"][0:KS3, 0:1], w, ALU.mult, ALU.add))
            step(dve.tensor_copy(w1s[:], w))
            step(dve.scalar_tensor_tensor(w, w1s[:], W["less"][0:KS3, 1:2], w, ALU.mult, ALU.add))
            dve.tensor_copy(w1s[:], w)
            dve.tensor_reduce(wo3[:], W["l3_wo"].rearrange("p n d -> p d n"), AX.X, ALU.add)
            for m, name in enumerate(("l2_w1", "l2_w3")):
                dve.wait_ge(sem("lora"), m + 1)
                w = W[name][:].rearrange("p e h -> p (e h)")
                dve.tensor_tensor(w, w, ps[:, 4 * m:4 * m + 4, :].rearrange("p n k -> p (n k)"), ALU.add)\
                   .then_inc(sem("merged"), 1)
            dve.wait_ge(sem("lora"), 3)
            w = W["l2_w2"][:].rearrange("p e c d -> p (e c d)")
            dve.tensor_tensor(w, w, ps[:, 0:4, :].rearrange("p n k -> p (n k)"), ALU.add)
            dve.wait_ge(sem("colsum"), 1)
            dve.scalar_tensor_tensor(l0_gate_bo[:], bank(4, P), -LAMBDA * ALPHA, W["l0_gbo"], ALU.mult, ALU.add)
            dve.scalar_tensor_tensor(l0_exp_bo[:], ps[0:E0, 5, 0:P], -LAMBDA * ALPHA, W["l0_ebo"],
                                     ALU.mult, ALU.add)
            dve.wait_ge(sem("wabs"), 1)
            step(dve.tensor_scalar(wmean[:], bank(6, 2), 1.0 / (D * F0), 1e-5, ALU.mult, ALU.max))
            step(dve.reciprocal(wscale[:], wmean[:]))
            for n, (name, dst) in enumerate((("l1_w1", w1q), ("l1_w2", w2q))):
                step(dve.tensor_scalar(W[name], W[name], wscale[:, n:n + 1], -1.0, ALU.mult, ALU.max))
                step(dve.tensor_scalar(W[name], W[name], 1.0, MAGIC, ALU.min, ALU.add))
                step(dve.tensor_scalar(dst[:], W[name], -MAGIC, None, ALU.add))
            dve.wait_ge(sem("tg_ready"), 1)
            dve.tensor_scalar(tgl[:], tg[:, 4:5], LAMBDA, None, ALU.mult)
            end_turn(dve, "dve")

            with dve.Fori(0, turns):
                step = Chain(dve, sem("dve_step"))
                roots = [0]

                def root():
                    roots[0] += 1
                    dve.wait_ge(sem("rstd_ready"), roots[0])

                def layernorm(x=x):
                    for t in range(NT):
                        ins = dve.bn_stats(stats[:, t, :], x[:, t, :])
                    step(ins)
                    for t in range(NT):
                        ins = dve.bn_aggr(mv[:, t, :], stats[:, t, :])
                    step(ins)
                    dve.tensor_scalar(vare[:], mv[:, :, 1], EPS, None, ALU.add).then_inc(sem("var_ready"), 1)
                    root()
                    if x is xn:
                        dve.wait_ge(sem("x_copied"), 1)
                    for t in range(NT):
                        ins = dve.tensor_scalar(xn[:, t, :], x[:, t, :], mv[:, t, 0:1], rstd[:, t:t + 1],
                                                ALU.subtract, ALU.mult)
                    ins.then_inc(sem("xn_ready"), 1)

                def add_projected(banks_, bias, n, gate):
                    step(dve.tensor_tensor(y[:], banks_.rearrange("p (t d) -> p t d", t=NT),
                                           bias[:].unsqueeze(1).to_broadcast([P, NT, D]), ALU.add))
                    dve.scalar_tensor_tensor(x[:], y[:], tg[:, gate:gate + 1], x[:], ALU.mult, ALU.add)\
                       .then_inc(sem("x_done"), 1)
                    dve.wait_ge(sem("x_done"), n)

                def values(a):
                    dve.wait_ge(*upto("v_ps", a, 1))
                    src = bank(7).rearrange("p (t d) -> p t d", t=NT)
                    if a == 0:
                        ins = dve.tensor_scalar(vf[:], src, 0.0, None, ALU.max)
                    elif a == 1:
                        ins = dve.tensor_tensor(vf[:], src, W["l1_bv"][:].unsqueeze(1).to_broadcast([P, NT, D]),
                                                ALU.add)
                    else:
                        ins = dve.tensor_copy(vf[:], src)
                    ins.then_inc(sem("vf"), 1)

                def key_stack(a, j):
                    dve.wait_ge(*upto("ks_ps", a, j + 1))
                    dve.tensor_copy(kS[:, j, :], bank(6 + j % 2)).then_inc(sem("ks_odd"), 1)

                rest = acc[:].rearrange("p t d -> p (t d)")

                def split(src, part):
                    step(dve.tensor_copy(part[:, 0, :], src))
                    step(dve.tensor_tensor(rest, src, part[:, 0, :], ALU.subtract))
                    step(dve.tensor_copy(part[:, 1, :], rest))
                    return dve.tensor_tensor(part[:, 2, :], rest, part[:, 1, :], ALU.subtract)

                def attention(a):
                    L = f"l{a}_"
                    if a:
                        dve.wait_ge(*upto("qf", a, 1))
                        split(qf[:], qp).then_inc(sem("qp"), 1)

                    def maxima(s, n):
                        b, j = divmod(n, NK)
                        dve.wait_ge(*upto("s1", a, n + 1))
                        dve.tensor_reduce(nm[:, 2 * b:2 * b + 2, HP * j:HP * j + HP].rearrange("p t g -> p g t"),
                                          ps[:, s:s + 2, :].rearrange("p g (t k) -> p g t k", t=2),
                                          AX.X, ALU.max, negate=True).then_inc(sem("max_ready"), 1)
                        if j == NK - 1:
                            dve.wait_ge(*upto("max_ready", a, n + 1))
                            row, parts = nm[:, 2 * b:2 * b + 2, :], nmp[:, 2 * b:2 * b + 2]
                            step(dve.tensor_scalar(parts[:, :, 0, :], row, CAP, None, ALU.min))
                            dve.scalar_tensor_tensor(parts[:, :, 1, :], row, CAP, parts[:, :, 0, :], ALU.min,
                                                     ALU.subtract).then_inc(sem("max_parts"), 1)

                    def row_sum(b):
                        dve.wait_ge(*upto("pv", a, NK * (b + 1)))
                        for qt in range(2):
                            ins = dve.tensor_reduce(osum[:, 2 * b + qt], ps[:, 6 + qt, 0:H * VW].rearrange(
                                "p (h n d) -> p h d n", h=H, n=3), AX.X, ALU.add)
                        ins.then_inc(sem("o_read"), 1)

                    def bias(s, v):
                        b = v // NK
                        dve.wait_ge(*upto("s2", 1, v + 1))
                        dve.tensor_tensor(bank(s + 1).rearrange("p (t k) -> p t k", t=2),
                                          bank(s + 1).rearrange("p (t k) -> p t k", t=2),
                                          bfull[:, 2 * b:2 * b + 2, :], ALU.add).then_inc(sem("biased"), 1)

                    def low(v):
                        dve.wait_ge(*upto("p_ready", a, v + 1))
                        if v >= NPB:
                            dve.wait_ge(*upto("pv", a, v - NPB + 1))
                        if not HIGH_BY_ACT(a, v):
                            step(dve.tensor_copy(pH[:, v % NPB, :], pT[:, v % NPB, :]))
                        dve.tensor_tensor(pL[:, v % NPB, :], pT[:, v % NPB, :], pH[:, v % NPB, :], ALU.subtract)\
                           .then_inc(sem("p_low"), 1)
                        if v == NK + NPB - 3:
                            row_sum(0)

                    if a == 1:
                        dve.wait_ge(sem("l1_bias_ready"), 1)
                    for k, (kind, n) in enumerate(SLOTS):
                        if kind == "max":
                            maxima(2 * (k % 3), n)
                        if kind == "exp" and a == 1:
                            bias(2 * (k % 3), n)
                        if k >= DVE_LAG and SLOTS[k - DVE_LAG][0] == "exp":
                            low(SLOTS[k - DVE_LAG][1])
                    for k in range(len(SLOTS) - DVE_LAG, len(SLOTS)):
                        low(SLOTS[k][1])
                    row_sum(1)
                    dve.wait_ge(*upto("o_read", a, NB))
                    step(dve.reciprocal(rc[:], osum[:, :, :, DH]))
                    ins = dve.tensor_tensor(att[:].rearrange("p t (h d) -> p (t h) d", h=H),
                                            osum[:, :, :, 0:DH].rearrange("p t h d -> p (t h) d"),
                                            rc[:].rearrange("p t h -> p (t h)").unsqueeze(2)
                                            .to_broadcast([P, NT * H, DH]), ALU.mult)
                    if a == 0:
                        step(ins)
                        dve.scalar_tensor_tensor(x[:], att[:], tg[:, 0:1], x[:], ALU.mult, ALU.add)\
                           .then_inc(sem("x_done"), 1)
                        dve.wait_ge(sem("x_done"), 1)
                    else:
                        ins.then_inc(sem("att_ready"), 1)
                        dve.wait_ge(*upto("o_ps", a, 1))
                        add_projected(bank(1), W[L + "bo"], 2 * a + 1, a)

                def top2(src, n):
                    for r in range(n):
                        ins = dve.max(mx8[:, r, :], src[:, r, :])
                    step(ins)
                    for r in range(n):
                        ins = dve.max_index(ix8[:, r, :], mx8[:, r, :], src[:, r, :])
                    step(ins)
                    step(dve.tensor_copy(ixf[:, 0:n, :], ix8[:, 0:n, 0:2]))

                def expert_weights(done):
                    for k in range(2):
                        dve.tensor_tensor(oh[:, k], W["iota"][:, 0:8].unsqueeze(1).to_broadcast([P, NT, 8]),
                                          ixf[:, 0:NT, k].unsqueeze(2).to_broadcast([P, NT, 8]), ALU.is_equal)\
                           .then_inc(sem("dve_step"), 1)
                    step.n += 2
                    dve.wait_ge(step.sem, step.n)
                    for k in range(2):
                        ins = dve.tensor_tensor(oh[:, k], oh[:, k], tw[:, :, k].unsqueeze(2).to_broadcast([P, NT, 8]),
                                                ALU.mult)
                    step(ins)
                    dve.tensor_tensor(gw[:], oh[:, 0], oh[:, 1], ALU.add).then_inc(sem(done), 1)

                def expert_sum(read, n):
                    for t in range(NT):
                        src = bank(4 + (n[0]) % 2)[:, t * P:(t + 1) * P]
                        if n[1] == 0:
                            ins = dve.tensor_scalar(acc[:, t, :], src, gw[:, t, n[1]:n[1] + 1], None, ALU.mult)
                        else:
                            ins = dve.scalar_tensor_tensor(acc[:, t, :], src, gw[:, t, n[1]:n[1] + 1],
                                                           acc[:, t, :], ALU.mult, ALU.add)
                    ins.then_inc(sem(read), 1)

                def quantise(src, dst, F, n):
                    dve.tensor_scalar(vare[:], cols[:, 0, :], 1.0 / F, EPS, ALU.mult, ALU.add)\
                       .then_inc(sem("var_ready"), 1)
                    root()
                    step(dve.tensor_tensor(cols[:, 2, :], cols[:, 1, :], rstd[:], ALU.mult))
                    step(dve.tensor_scalar(cols[:, 3, :], cols[:, 2, :], 1e-5, None, ALU.max))
                    step(dve.reciprocal(cols[:, 4, :], cols[:, 3, :]))
                    step(dve.scalar_tensor_tensor(cols[:, 5, :], cols[:, 4, :], 127.0, rstd[:], ALU.mult, ALU.mult))
                    step(dve.tensor_scalar(cols[:, 6, :], cols[:, 3, :], wmean[:, n:n + 1], 1.0 / 127.0,
                                           ALU.mult, ALU.mult))
                    for t in range(NT):
                        ins = dve.tensor_scalar(src[:, t, :], src[:, t, :], cols[:, 5, t:t + 1], -128.0,
                                                ALU.mult, ALU.max)
                    step(ins)
                    step(dve.tensor_scalar(src, src, 127.0, MAGIC, ALU.min, ALU.add))
                    return dve.tensor_scalar(dst, src, -MAGIC, None, ALU.add)

                layernorm(xn)
                dve.wait_ge(*upto("kf", 0, 1))
                split(kf[:], kp0).then_inc(sem("kp"), 1)
                values(0)
                key_stack(0, 1)
                dve.wait_ge(*upto("qf", 0, 1))
                step(dve.tensor_copy(qp[:, 0, :], qf[:]))
                key_stack(0, 3)
                step(dve.tensor_tensor(rest, qf[:], qp[:, 0, :], ALU.subtract))
                key_stack(0, 5)
                step(dve.tensor_copy(qp[:, 1, :], rest))
                dve.tensor_tensor(qp[:, 2, :], rest, qp[:, 1, :], ALU.subtract).then_inc(sem("qp"), 1)
                key_stack(0, 7)
                attention(0)

                layernorm()
                values(1)
                for e in range(E0 + 2):
                    if e <= E0:
                        for fc in range(NC0):
                            n = NC0 * e + fc
                            dve.wait_ge(sem("f0_act"), n + 1)
                            if e >= 2 and fc == 0:
                                dve.wait_ge(sem("f0_out"), e - 1)
                            dve.scalar_tensor_tensor(hT[:, e % 2, fc, :], ex[:, n % 4, :], ALPHA, rl[:, n % 4, :],
                                                     ALU.min, ALU.add).then_inc(sem("f0_h"), 1)
                    if e == 1:
                        dve.wait_ge(sem("f0_out"), 1)
                        lgv = lg.rearrange("p (t d) -> p t d", t=NT)
                        dve.scalar_tensor_tensor(lgv, bank(4).rearrange("p (t d) -> p t d", t=NT), LAMBDA,
                                                 l0_gate_bo[:].unsqueeze(1).to_broadcast([P, NT, D]),
                                                 ALU.mult, ALU.add).then_inc(sem("f0_out_read"), 1)
                        dve.wait_ge(sem("f0_out_read"), 1)
                        top2(lgv, NT)
                        step(dve.tensor_tensor(tws[:], mx8[:, 0:NT, 0], mx8[:, 0:NT, 1], ALU.add))
                        step(dve.reciprocal(tws[:], tws[:]))
                        step(dve.tensor_tensor(tw[:], mx8[:, 0:NT, 0:2], tws[:].unsqueeze(2).to_broadcast([P, NT, 2]),
                                               ALU.mult))
                        expert_weights("f0_gate")
                        dve.wait_ge(sem("f0_gate"), 1)
                    if e >= 2:
                        dve.wait_ge(sem("f0_out"), e)
                        if e >= 3:
                            dve.wait_ge(sem("f0_out_read"), e - 1)
                        expert_sum("f0_out_read", (e - 1, e - 2))
                dve.wait_ge(sem("f0_out_read"), E0 + 1)
                step(dve.scalar_tensor_tensor(x[:], acc[:], tgl[:], x[:], ALU.mult, ALU.add))
                dve.wait_ge(sem("f0_b"), 1)
                dve.scalar_tensor_tensor(x[:], bank(6).rearrange("p (t d) -> p t d", t=NT), tg[:, 4:5], x[:],
                                         ALU.mult, ALU.add).then_inc(sem("x_done"), 1)
                dve.wait_ge(sem("x_done"), 2)

                layernorm()
                attention(1)

                layernorm()
                dve.wait_ge(sem("xn_ready"), 4)
                step(dve.tensor_tensor(y[:], xn[:], xn[:], ALU.mult))
                dve.tensor_reduce(cols[:, 1, :], xn[:], AX.X, ALU.max, apply_absolute_value=True)
                step(dve.tensor_reduce(cols[:, 0, :], y[:], AX.X, ALU.add))
                quantise(xn[:], qx, D, 0).then_inc(sem("f1_qx"), 1)
                values(2)
                for t in range(NT):
                    dve.wait_ge(sem("f1_h_ps"), t + 1)
                    dve.scalar_tensor_tensor(hT[:, 0, t, :], bank(1 + t), cols[:, 6, t:t + 1], W["l1_b1"][:],
                                             ALU.mult, ALU.add).then_inc(sem("f1_y"), 1)
                dve.wait_ge(sem("f1_gelu"), NT)
                dve.wait_ge(sem("f1_sq"), NT)
                step(dve.tensor_reduce(cols[:, 1, :], hh[:], AX.X, ALU.max, apply_absolute_value=True))
                quantise(hh[:], qh, F0, 1).then_inc(sem("f1_qh"), 1)
                dve.wait_ge(sem("f1_o_ps"), 1)
                for t in range(NT):
                    ins = dve.scalar_tensor_tensor(y[:, t, :], bank(0)[:, t * P:(t + 1) * P], cols[:, 6, t:t + 1],
                                                   W["l1_b2"][:], ALU.mult, ALU.add)
                step(ins)
                dve.scalar_tensor_tensor(x[:], y[:], tg[:, 5:6], x[:], ALU.mult, ALU.add)\
                   .then_inc(sem("x_done"), 1)
                dve.wait_ge(sem("x_done"), 4)

                layernorm()
                attention(2)

                layernorm()
                dve.wait_ge(sem("f2_lg"), 1)
                lgv = lg[:, 0:NT * 8].rearrange("p (t e) -> p t e", t=NT)
                step(dve.tensor_copy(lg[:, 0:NT * 8], bank(7, NT * 8)))
                top2(lgv, NT)
                dve.tensor_tensor(tws[:], mx8[:, 0:NT, 1], mx8[:, 0:NT, 0], ALU.subtract)\
                   .then_inc(sem("f2_gap"), 1)
                dve.wait_ge(sem("f2_gap_exp"), 1)
                step(dve.tensor_scalar(tws[:], tw[:, :, 1], 1.0, None, ALU.add))
                step(dve.reciprocal(tw[:, :, 0], tws[:]))
                step(dve.tensor_tensor(tw[:, :, 1], tw[:, :, 1], tw[:, :, 0], ALU.mult))
                expert_weights("f2_gate")
                dve.wait_ge(sem("f2_gate"), 1)
                for e in range(E2 + 1):
                    if e < E2:
                        for hc in range(NH2):
                            n = NH2 * e + hc
                            dve.wait_ge(sem("f2_silu"), n + 1)
                            dve.wait_ge(sem("f2_h3"), n + 1)
                            if e >= 2 and hc == 0:
                                dve.wait_ge(sem("f2_out"), e - 1)
                            dve.scalar_tensor_tensor(hT[:, e % 2, hc, :], bank(2 * (n % 2) + 1),
                                                     W["l2_bias3"][:, n:n + 1], ex[:, n % 2, :],
                                                     ALU.add, ALU.mult).then_inc(sem("f2_g"), 1)
                    if e >= 1:
                        dve.wait_ge(sem("f2_out"), e)
                        if e >= 2:
                            dve.wait_ge(sem("f2_out_read"), e - 1)
                        expert_sum("f2_out_read", (e - 1, e - 1))
                dve.wait_ge(sem("f2_out_read"), E2)
                step(dve.scalar_tensor_tensor(x[:], acc[:], tg[:, 6:7], x[:], ALU.mult, ALU.add))
                dve.wait_ge(sem("f2_b"), 1)
                dve.scalar_tensor_tensor(x[:], bank(6).rearrange("p (t d) -> p t d", t=NT), tg[:, 6:7], x[:],
                                         ALU.mult, ALU.add).then_inc(sem("x_done"), 1)
                dve.wait_ge(sem("x_done"), 6)

                layernorm()
                dve.wait_ge(sem("l3_v_ps"), 1)
                dve.tensor_copy(y[:, :, 0:DK3], bank(2, NT * DK3).rearrange("p (t d) -> p t d", t=NT))
                dve.wait_ge(sem("l3_s"), 1)
                dve.tensor_reduce(cols[:, 0, :].rearrange("p (b t) -> p b t", b=2),
                                  ps[:, 4:6, :].rearrange("p b (t k) -> p b t k", t=2),
                                  AX.X, ALU.max, negate=True).then_inc(sem("l3_max"), 1)
                dve.wait_ge(sem("l3_exp"), NT)
                step(dve.reciprocal(cols[:, 2, :], cols[:, 1, :]))
                for t in range(NT):
                    ins = dve.tensor_scalar(pT[:, 0, t * S:(t + 1) * S], ex[:, t // 2, (t % 2) * S:(t % 2 + 1) * S],
                                            cols[:, 2, t:t + 1], None, ALU.mult)
                ins.then_inc(sem("l3_p"), 1)
                dve.wait_ge(sem("l3_pT_ps"), 2)
                dve.tensor_copy(pT[:, 1, T:2 * T], bank(7)).then_inc(sem("l3_pT_dve"), 1)
                dve.wait_ge(sem("l3_head_ps"), 1)
                dve.tensor_tensor(lg[0:DK3, :], ps[0:DK3, 1, :], attT[0:DK3, :], ALU.add).then_inc(sem("l3_head"), 1)
                dve.wait_ge(sem("l3_o_ps"), 1)
                add_projected(bank(2), W["l3_bo"], 7, 3)

                layernorm()
                dve.wait_ge(sem("f3_lg"), 1)
                step(dve.tensor_copy(lg, bank(3)))
                lgv = lg.rearrange("p (r e) -> p r e", e=E3)
                step(dve.tensor_reduce(gsum[:], lgv, AX.X, ALU.max))
                dve.tensor_tensor(rl[:, 0, :].rearrange("p (r e) -> p r e", e=E3), lgv,
                                  gsum[:].unsqueeze(2).to_broadcast([P, 32, E3]), ALU.subtract)\
                   .then_inc(sem("f3_lgm"), 1)
                top2(lgv, 32)
                for k in range(2):
                    ins = dve.tensor_tensor(oh16[:, k], W["iota"][:].unsqueeze(1).to_broadcast([P, 32, E3]),
                                            ixf[:, :, k:k + 1].to_broadcast([P, 32, E3]), ALU.is_equal)
                step(ins)
                step(dve.tensor_tensor(oh16[:, 0], oh16[:, 0], oh16[:, 1], ALU.add))
                dve.wait_ge(sem("f3_exp"), 1)
                step(dve.tensor_reduce(gsum[:], gates[:], AX.X, ALU.add))
                step(dve.reciprocal(gsum[:], gsum[:]))
                step(dve.tensor_tensor(gates[:], gates[:], oh16[:, 0], ALU.mult))
                dve.tensor_tensor(gates[:], gates[:], gsum[:].unsqueeze(2).to_broadcast([P, 32, E3]), ALU.mult)\
                   .then_inc(sem("f3_gate"), 1)
                dve.wait_ge(sem("f3_gT"), 2)
                dve.tensor_tensor(GTl, GT, GTh, ALU.subtract).then_inc(sem("f3_gT_low"), 1)
                unit = rl[:, 0, :]
                for w in range(2 * H3):
                    h = w // 2
                    dve.wait_ge(sem("f3_out"), NEP // 2 * (w + 1))
                    dve.wait_ge(sem("f3_gr"), w + 1)
                    if w % 2 == 0:
                        if h >= 2:
                            dve.wait_ge(sem("f3_sum"), h - 1)
                        dve.tensor_tensor(ex[:, 2 + h % 2, :], bank(4), ex[:, 0, :], ALU.mult)\
                           .then_inc(sem("f3_prod"), 1)
                    else:
                        dve.tensor_tensor(unit, bank(5), ex[:, 1, :], ALU.mult).then_inc(sem("f3_prod"), 1)
                        dve.wait_ge(sem("f3_prod"), w + 1)
                        dve.tensor_tensor(ex[:, 2 + h % 2, :], ex[:, 2 + h % 2, :], unit, ALU.add)\
                           .then_inc(sem("f3_head"), 1)
                        if w + 1 < 2 * H3:
                            dve.wait_ge(sem("f3_head"), h + 1)
                dve.wait_ge(sem("f3_o_ps"), 1)
                add_projected(bank(1), W["l3_fbo"], 8, 7)
                end_turn(dve, "dve")

        @block.sync
        def _(sp):
            for name in SETUP_WEIGHTS:
                sp.dma_start(W[name] if name in SETUP_ONLY else W[name][:], A[name]).then_inc(sem("setup_loaded"), 16)
            rest = [name for name in WEIGHTS if name not in SETUP_WEIGHTS]
            for name in rest:
                source = A[name].bitcast(bf16) if WEIGHTS[name][1] == "b" else A[name]
                sp.dma_start(W[name][:], source).then_inc(sem("weights_loaded"), 16)
            x_loaded, ctx_loaded = sem("x_loaded"), sem("ctx_loaded")
            numbers = sorted(s.num for n, s in sems.items() if n not in kept)
            assert numbers[-1] - numbers[0] + 1 == len(numbers)

            def clear():
                sp.wait_ge(turn_end, 4)
                sp.sem_clear(turn_end)
                sp.sem_clear(range(numbers[0], numbers[-1] + 1))
                for e in GO:
                    sp.sem_inc(GO[e], 1)

            xv = A["x"].rearrange("(n p) d -> p n d", p=P)
            cv = A["ctx"].rearrange("(n p) d -> p n d", p=P)
            ov = out.rearrange("(n p) d -> p n d", p=P)
            mq = A["mask1_q"].rearrange("(n p) k -> p n k", p=P)
            mk = A["mask1_k"].rearrange("(n p) k -> p n k", p=P)
            sp.dma_start(ctxs[:], cv[:, 0:NT, :]).then_inc(ctx_loaded, 16)
            sp.dma_start(xn[:], xv[:, 0:NT, :]).then_inc(x_loaded, 16)
            sp.wait_ge(sem("setup_loaded"), 16 * len(SETUP_WEIGHTS))
            sp.wait_ge(sem("weights_loaded"), 16 * len(rest))
            sp.wait_ge(x_loaded, 16)
            sp.wait_ge(ctx_loaded, 16)
            sp.sem_inc(stored, 16)
            clear()
            with sp.Fori(0, turns) as i:
                sp.wait_ge(stored, 16)
                sp.sem_clear(stored)
                sp.sem_inc(sem("x_free"), 1)
                sp.dma_start(m1[:], mq[:, bass.ds(i * NT, NT), :]).then_inc(sem("masks_loaded"), 16)
                sp.wait_ge(sem("mask_read"), 1)
                sp.wait_ge(sem("masks_loaded"), 16)
                sp.dma_start(m1[:], mk[:, bass.ds(i * NT, NT), :]).then_inc(sem("masks_loaded"), 16)
                sp.wait_ge(*upto("attT_ps", 2, 1))
                sp.dma_start(ctxs[:], cv[:, bass.ds((i + 1) * NT, NT), :]).then_inc(ctx_loaded, 16)
                sp.wait_ge(sem("xT_ps"), n_T(7))
                sp.dma_start(xn[:], xv[:, bass.ds((i + 1) * NT, NT), :]).then_inc(x_loaded, 16)
                sp.wait_ge(sem("x_done"), 8)
                sp.dma_start(ov[:, bass.ds(i * NT, NT), :], x[:]).then_inc(stored, 16)
                sp.wait_ge(ctx_loaded, 16)
                sp.wait_ge(x_loaded, 16)
                clear()
            sp.wait_ge(stored, 16)


SLOTS = [("max", n) for n in range(NK + 2)] + [("shift", 0)]
for _n in range(NK + 2, 2 * NK):
    SLOTS += [("max", _n), ("exp", _n - NK - 2)]
SLOTS += [("exp", NK - 2), ("shift", 1)] + [("exp", _n) for _n in range(NK - 1, 2 * NK)]
DVE_LAG = 2


def HIGH_BY_ACT(a, v):
    return v < NK or (v % 8 != 3 if a == 1 else v % 3 != 2)


PER_ATTENTION = {
    "k_ps": 1, "kf": 1, "kp": 1, "ks_ps": NK, "ks_even": NK // 2, "ks_odd": NK // 2,
    "v_ps": 1, "vf": 1, "v_ready": 1,
    "q_ps": 1, "qf": 1, "qp": 1, "qs_ps": NK, "qs": NK,
    "s1": 2 * NK, "max_ready": 2 * NK, "max_parts": NB, "max_T": NB, "nmT": NB,
    "s2": 2 * NK, "p_ready": 2 * NK, "p_low": 2 * NK, "pv": 2 * NK, "o_read": NB,
    "att_ready": 1, "attT_ps": 1, "attT": 1, "o_ps": 1,
}
PROJECTED = ("att_ready", "attT_ps", "attT", "o_ps")
LN_OF_ATT = (0, 2, 4)


def n_T(n):
    return n + 1 - (n > 3)


BF16_ONE = 0x3F80

WEIGHTS = {
    "ident": ([P, P], "f"), "ones": ([P, P], "f"), "pick": ([P, E0, E0], "f"), "iota": ([P, E3], "f"),
    "less": ([P, 2], "f"), "sum_o": ([P, 2 * P - HD3], "f"), "g": ([P, 8], "f"),
    "sel_x": ([P, 3, NK, P], "b"), "sel_y": ([P, 3, NK, P], "b"), "sel_h": ([P, 3, H3, KS3], "b"),
    "sel_m": ([P, H], "b"),
    "l0_wq": ([P, P], "f"), "l0_wk": ([P, P], "f"), "l0_wv": ([P, P], "f"),
    "l1_wq": ([P, P], "f"), "l1_wk": ([P, P], "f"), "l1_wv": ([P, P], "f"), "l1_wo": ([P, P], "f"),
    "l1_bq": ([P, 1], "f"), "l1_bk": ([P, 1], "f"), "l1_bv": ([P, P], "f"), "l1_bo": ([P, P], "f"),
    "l2_wq": ([P, P], "f"), "l2_wk": ([P, P], "f"), "l2_wv": ([P, P], "f"), "l2_wo": ([P, P], "f"),
    "l2_bo": ([P, P], "f"),
    "adj_q": ([P, 2, S], "f"), "adj_k": ([P, 2, S], "f"), "mask0_q": ([P, 2, S], "i"), "mask0_k": ([P, 2, S], "i"),
    "l0_wi": ([P, E0 + 1, F0], "f"), "l0_bi": ([P, (E0 + 1) * NC0], "f"), "l0_wo": ([P, E0 + 1, NC0, P], "f"),
    "l0_gbo": ([P, P], "f"), "l0_ebo": ([E0, P], "f"),
    "l1_w1": ([P, F0], "f"), "l1_b1": ([P, F0], "f"), "l1_w2": ([P, F0], "f"), "l1_b2": ([P, P], "f"),
    "l2_wg": ([P, E2], "f"), "l2_w1": ([P, E2, H2], "f"), "l2_w3": ([P, E2, H2], "f"),
    "l2_w2": ([P, E2, NH2, P], "f"), "l2_a1": ([R2, E2, P], "f"), "l2_a3": ([R2, E2, P], "f"),
    "l2_a2": ([R2, E2, H2], "f"), "l2_b1": ([R2, E2, H2], "f"), "l2_b3": ([R2, E2, H2], "f"),
    "l2_b2": ([R2, E2, P], "f"), "l2_bias1": ([P, E2 * NH2], "f"), "l2_bias3": ([P, E2 * NH2], "f"),
    "l2_bias2": ([E2, P], "f"),
    "l3_wi": ([P, DK3], "f"), "l3_wo": ([DK3, 16, P], "f"), "l3_bo": ([P, P], "f"),
    "l3_wm": ([P, P], "f"), "l3_bm": ([P, 1], "f"), "l3_emb": ([P, P], "f"), "l3_w1": ([KS3, E3 * I3], "f"),
    "l3_b1": ([P, NEP], "f"), "l3_w2": ([P, NEP, 32], "f"), "l3_b2": ([P, P], "f"), "l3_fo": ([P, P], "f"),
    "l3_fbo": ([P, P], "f"),
}
SETUP_ONLY = {
    "l1_w1": ("m1", 0), "l1_w2": ("m1", F0), "l2_a1": ("hT", 0), "l2_b1": ("hT", E2 * P),
    "l2_a3": ("hT", E2 * (P + H2)), "l2_b3": ("qP", 0),
    "l3_w1": ("vfree", 0), "l2_a2": ("kP", 0), "l2_b2": ("rl", 0), "l3_wo": ("ex", 0),
    "mask0_q": ("rl", E2 * P), "mask0_k": ("rl", E2 * P + 2 * S),
    "ones": ("y", 0), "l0_gbo": ("y", P), "l0_ebo": ("y", 2 * P), "pick": ("y", 3 * P),
}
SETUP_WEIGHTS = ("ident", "g", "less", "l1_bq", "l0_bi", *SETUP_ONLY, "l2_w1", "l2_w3", "l2_w2", "l0_wo")


def layout(I):
    import numpy as np
    f = np.float32

    def rows(v):
        return np.repeat(v.reshape(1, -1), P, 0)

    def tiles(m):
        return m.reshape(2, P, -1).transpose(1, 0, 2)

    o = {"ident": np.eye(P, dtype=f), "ones": np.ones((P, P), f),
         "pick": np.repeat(np.eye(E0, dtype=f)[None], P, 0), "iota": rows(np.arange(E3, dtype=f))}
    less = np.zeros((P, 2), f)
    for c, part in enumerate(Y_PARTS):
        less[16 * c:16 * c + 16, 0] = -1.0 * (part >= 1)
        less[16 * c:16 * c + 16, 1] = -1.0 * (part >= 2)
    o["less"] = less
    o["sum_o"] = np.zeros((P, 2 * P - HD3), f)
    o["sum_o"][:, P - HD3:P] = np.tile(np.eye(HD3, dtype=f), (P // HD3, 1))

    def select(parts, n, width, places, rows_):
        r = np.zeros((P, 3, n, rows_), np.uint16)
        for j in range(n):
            for g, place in enumerate(places):
                for c, part in enumerate(parts):
                    for d in range(width):
                        r[(j * len(places) + g) * width + d, part, j, place + c * width + d] = BF16_ONE
        return r

    o["sel_x"] = select(X_PARTS, NK, DH, (0, 64), P)
    o["sel_y"] = select(Y_PARTS, NK, DH, (0, 64), P)
    o["sel_h"] = select(X_PARTS, H3, HD3, (0,), KS3)
    o["sel_m"] = np.zeros((P, H), np.uint16)
    o["sel_m"][0:2 * H] = np.tile(np.eye(H, dtype=np.uint16) * np.uint16(BF16_ONE), (2, 1))
    o["g"] = rows(np.concatenate([I["g_xattn"], I["g_ffn"]]))
    for a, (q, k, v) in enumerate((("Wq", "Wk", "Wv"), ("Wq", "Wk", "Wv"), ("wq", "wk", "wv"))):
        for name, w in (("q", q), ("k", k), ("v", v)):
            o[f"l{a}_w{name}"] = I[f"L{a}_xattn_{w}"].T
    o["l1_wo"], o["l2_wo"] = I["L1_xattn_Wo"].T, I["L2_xattn_wo"].T
    o["l1_bq"], o["l1_bk"] = I["L1_xattn_bq"].reshape(P, 1), I["L1_xattn_bk"].reshape(P, 1)
    o["l1_bv"], o["l1_bo"], o["l2_bo"] = rows(I["L1_xattn_bv"]), rows(I["L1_xattn_bo"]), rows(I["L2_xattn_bo"])
    o["adj_q"], o["adj_k"] = tiles(I["L1_xattn_adj"]), tiles(I["L1_xattn_adj"].T)
    m0 = I["mask_1x1xSxS2_ik0"][0, 0]
    o["mask0_q"], o["mask0_k"] = tiles(m0), tiles(m0.T)
    m1 = I["mask_Bx1xSxS2_ik1"][:, 0]
    o["mask1_q"] = m1.reshape(BATCH * S, S)
    o["mask1_k"] = m1.transpose(0, 2, 1).reshape(BATCH * S, S)
    wi = np.concatenate([I["L0_ffn_gate_wi"][None], I["L0_ffn_exp_wi"]])
    bi = np.concatenate([I["L0_ffn_gate_bi"][None], I["L0_ffn_exp_bi"]])
    wo = np.concatenate([I["L0_ffn_gate_wo"][None], I["L0_ffn_exp_wo"]])
    o["l0_wi"] = wi.transpose(1, 0, 2)
    o["l0_bi"] = bi.reshape(-1, P).T
    o["l0_wo"] = wo.reshape(E0 + 1, NC0, P, P).transpose(2, 0, 1, 3)
    o["l0_gbo"], o["l0_ebo"] = rows(I["L0_ffn_gate_bo"]), I["L0_ffn_exp_bo"]
    o["l1_w1"], o["l1_b1"] = I["L1_ffn_w1"].T, rows(I["L1_ffn_b1"])
    o["l1_w2"] = I["L1_ffn_w2"].T.reshape(NC0, P, P).transpose(1, 0, 2).reshape(P, F0)
    o["l1_b2"] = rows(I["L1_ffn_b2"])
    o["l2_wg"] = I["L2_ffn_Wg"].T
    for n in "13":
        o["l2_w" + n] = I["L2_ffn_W" + n].transpose(2, 0, 1)
        o["l2_a" + n] = I["L2_ffn_A" + n].transpose(1, 0, 2)
        o["l2_b" + n] = I["L2_ffn_B" + n].transpose(2, 0, 1)
        o[f"l2_bias{n}"] = I["L2_ffn_b" + n].reshape(-1, P).T
    o["l2_w2"] = I["L2_ffn_W2"].transpose(2, 0, 1).reshape(NH2, P, E2, P).transpose(1, 2, 0, 3)
    o["l2_a2"] = I["L2_ffn_A2"].transpose(1, 0, 2)
    o["l2_b2"] = I["L2_ffn_B2"].transpose(2, 0, 1)
    o["l2_bias2"] = I["L2_ffn_b2"]
    o["l3_wi"] = I["L3_xattn_wi"]
    o["l3_wo"] = I["L3_xattn_Wo"].reshape(16, DK3, P).transpose(1, 0, 2)
    o["l3_bo"] = rows(I["L3_xattn_bo"])
    o["l3_wm"], o["l3_bm"] = I["L3_ffn_Wm"], I["L3_ffn_bm"].reshape(P, 1)
    emb = np.zeros((H3, HD3, H3, E3), f)
    for h in range(H3):
        emb[h, :, h] = I["L3_ffn_expert_emb"]
    o["l3_emb"] = emb.reshape(P, H3 * E3)
    o["l3_w1"] = np.zeros((KS3, E3 * I3), f)
    o["l3_w1"][0:NSEG * HD3] = np.tile(I["L3_ffn_W1"].transpose(1, 0, 2).reshape(HD3, E3 * I3), (NSEG, 1))
    o["l3_b1"] = I["L3_ffn_b1"].reshape(NEP, P).T
    w2 = np.zeros((2, I3, NEP, 2, HD3), f)
    for k in range(2):
        w2[k, :, :, k] = I["L3_ffn_W2"][k::2].transpose(1, 0, 2)
    o["l3_w2"] = w2.reshape(P, NEP, 32)
    b2 = np.zeros((H3, E3, H3, HD3), f)
    for h in range(H3):
        b2[h, :, h] = I["L3_ffn_b2"]
    o["l3_b2"] = b2.reshape(P, P)
    o["l3_fo"], o["l3_fbo"] = I["L3_ffn_Wo"], rows(I["L3_ffn_bo"])
    for name, v in (("x", I["x"]), ("ctx", I["ctx_1024"])):
        o[name] = np.concatenate([v, v[0:NB]]).reshape((BATCH + NB) * S, D)
    return o


def kernel(**inputs):
    import numpy as np
    import concourse.bacc as bacc
    from concourse.bass_utils import run_bass_kernel_spmd as run

    nc = bacc.Bacc("TRN2", target_bir_lowering=False, num_devices=1)
    arrays = {k: np.ascontiguousarray(v) for k, v in layout({k: np.asarray(v) for k, v in inputs.items()}).items()}
    A = {k: nc.dram_tensor("in_" + k, v.shape, mybir.dt.from_np(v.dtype), kind="ExternalInput").ap()
         for k, v in arrays.items()}
    out = nc.dram_tensor("out_x", (BATCH * S, D), mybir.dt.float32, kind="ExternalOutput").ap()
    flamingo(nc, A, out)
    r = run(nc, [{"in_" + k: v for k, v in arrays.items()}], core_ids=[0])
    return r.results[0]["out_x"].reshape(BATCH, S, D)
```
